# Optimizing a Trainium2 kernel written in Bass

```python
import numpy as np
import jax
import jax.numpy as jnp

def _softmax(x, axis=-1):
    return jax.nn.softmax(x, axis=axis)

def _gelu(x):
    return jax.nn.gelu(x, approximate=True)

def _silu(x):
    return jax.nn.silu(x)

def _sigmoid(x):
    return jax.nn.sigmoid(x)

def _layernorm(x, axis=-1, eps=1e-05):
    m = jnp.mean(x, axis=axis, keepdims=True)
    v = jnp.var(x, axis=axis, keepdims=True)
    return (x - m) / jnp.sqrt(v + eps)

def _scatter_add(tgt, idx, src, axis=0):
    return tgt.at[idx].add(src)

def _segment_sum(src, seg, n):
    return jax.ops.segment_sum(src, seg, n)
kernel_name = 'mk_gnn_preln_d2_gnn_r32_1933d9'

def setup_inputs(seed: int=0):
    np.random.seed(seed)
    _w = jnp.asarray

    def _rec_inputs():
        import jax
        import jax.numpy as jnp
        _gk = jax.random.key(seed)
        x = -0.000202 + 1 * jax.random.normal(jax.random.fold_in(_gk, 1), (50000, 128), jnp.float32)
        src = jax.random.randint(jax.random.fold_in(_gk, 2), (50000,), 0, 50000, jnp.int32)
        dst = jnp.minimum((50000 * jax.random.uniform(jax.random.fold_in(_gk, 3), (50000,)) ** 2.0).astype(jnp.int32), 49999)
        _o = jnp.argsort(dst, stable=True)
        src = src[_o]
        dst = dst[_o]
        edge_attr_128 = -4.21973e-05 + 0.999841 * jax.random.normal(jax.random.fold_in(_gk, 12), (50000, 128), jnp.float32)
        return (x, src, dst, edge_attr_128)
    x, src, dst, edge_attr_128 = _rec_inputs()

    def _L0_gnn_setup():
        import jax, jax.numpy as jnp
        import numpy as np
        H = 8
        DH = 16
        D = 128
        EPS_BN = 1e-05

        def _batchnorm(h, gamma, beta):
            mu = h.mean(axis=0)
            var = h.var(axis=0)
            return (h - mu) / jnp.sqrt(var + EPS_BN) * gamma + beta

        def _forward(x, edge_attr, edge_index, Wq, Wk, We, Wv, bn1_g, bn1_b, W1, b1, W2, b2, bn2_g, bn2_b):
            N = x.shape[0]
            src, dst = (edge_index[0], edge_index[1])
            Q_h = (x @ Wq).reshape(N, H, DH)
            K_h = (x @ Wk).reshape(N, H, DH)
            V_h = (x @ Wv).reshape(N, H, DH)
            E_e = (edge_attr @ We).reshape(-1, H, DH)
            score = K_h[src] * Q_h[dst] / np.sqrt(DH) * E_e
            score = jnp.exp(jnp.clip(score.sum(-1, keepdims=True), -5.0, 5.0))
            msg = V_h[src] * score
            wV = jax.ops.segment_sum(msg, dst, num_segments=N)
            Z = jax.ops.segment_sum(score, dst, num_segments=N)
            h_attn = (wV / (Z + 1e-06)).reshape(N, D)
            h = x + h_attn
            h = _batchnorm(h, bn1_g, bn1_b)
            h2 = jax.nn.relu(h @ W1 + b1)
            h2 = h2 @ W2 + b2
            h = h + h2
            h = _batchnorm(h, bn2_g, bn2_b)
            return h
        key = jax.random.key(seed)
        ks = jax.random.split(key, 16)
        N, E = (50000, 18750)
        s = 1.0 / np.sqrt(D)
        inp = {'x': jax.random.normal(ks[0], (N, D), jnp.float32), 'edge_attr': jax.random.normal(ks[1], (E, D), jnp.float32), 'edge_index': jax.random.randint(ks[2], (2, E), 0, N, jnp.int64), 'Wq': jax.random.normal(ks[3], (D, D), jnp.float32) * s, 'Wk': jax.random.normal(ks[4], (D, D), jnp.float32) * s, 'We': jax.random.normal(ks[5], (D, D), jnp.float32) * s, 'Wv': jax.random.normal(ks[6], (D, D), jnp.float32) * s, 'bn1_g': jnp.ones((D,), jnp.float32), 'bn1_b': jnp.zeros((D,), jnp.float32), 'W1': jax.random.normal(ks[7], (D, 2 * D), jnp.float32) * s, 'b1': jnp.zeros((2 * D,), jnp.float32), 'W2': jax.random.normal(ks[8], (2 * D, D), jnp.float32) * (1.0 / np.sqrt(2 * D)), 'b2': jnp.zeros((D,), jnp.float32), 'bn2_g': jnp.ones((D,), jnp.float32), 'bn2_b': jnp.zeros((D,), jnp.float32)}
        return inp
    _L0_gnn_all = _L0_gnn_setup()
    _L0_gnn_in = {k: v for k, v in _L0_gnn_all.items() if k in ('Wq', 'Wk', 'We', 'Wv', 'bn1_g', 'bn1_b', 'W1', 'b1', 'W2', 'b2', 'bn2_g', 'bn2_b')}
    del _L0_gnn_all

    def _L1_gnn_setup():
        import jax, jax.numpy as jnp
        import numpy as np
        N_NODES = 3125
        N_EDGES = 50000
        D_IN = 128
        D_OUT = 128
        key = jax.random.key(seed)
        k1, k2, k3, k4, k5 = jax.random.split(key, 5)
        feature = jax.random.normal(k1, (N_NODES, D_IN), dtype=jnp.float32)
        src = jax.random.randint(k2, (N_EDGES,), 0, N_NODES, dtype=jnp.int32)
        dst = jax.random.randint(k3, (N_EDGES,), 0, N_NODES, dtype=jnp.int32)
        bound = float(np.sqrt(6.0 / (D_IN + D_OUT)))
        W_self = jax.random.uniform(k4, (D_IN, D_OUT), jnp.float32, -bound, bound)
        W_inter = jax.random.uniform(k5, (D_IN, D_OUT), jnp.float32, -bound, bound)
        return {'feature': feature, 'src': src, 'dst': dst, 'W_self': W_self, 'W_inter': W_inter}
    _L1_gnn_all = _L1_gnn_setup()
    _L1_gnn_in = {k: v for k, v in _L1_gnn_all.items() if k in ('W_self', 'W_inter')}
    del _L1_gnn_all
    return {'x': x, 'src': src, 'dst': dst, 'edge_attr_128': edge_attr_128, 'L0_gnn_Wq': _L0_gnn_in['Wq'], 'L0_gnn_Wk': _L0_gnn_in['Wk'], 'L0_gnn_We': _L0_gnn_in['We'], 'L0_gnn_Wv': _L0_gnn_in['Wv'], 'L0_gnn_bn1_g': _L0_gnn_in['bn1_g'], 'L0_gnn_bn1_b': _L0_gnn_in['bn1_b'], 'L0_gnn_W1': _L0_gnn_in['W1'], 'L0_gnn_b1': _L0_gnn_in['b1'], 'L0_gnn_W2': _L0_gnn_in['W2'], 'L0_gnn_b2': _L0_gnn_in['b2'], 'L0_gnn_bn2_g': _L0_gnn_in['bn2_g'], 'L0_gnn_bn2_b': _L0_gnn_in['bn2_b'], 'L1_gnn_W_self': _L1_gnn_in['W_self'], 'L1_gnn_W_inter': _L1_gnn_in['W_inter']}

def reference(x, src, dst, edge_attr_128, L0_gnn_Wq, L0_gnn_Wk, L0_gnn_We, L0_gnn_Wv, L0_gnn_bn1_g, L0_gnn_bn1_b, L0_gnn_W1, L0_gnn_b1, L0_gnn_W2, L0_gnn_b2, L0_gnn_bn2_g, L0_gnn_bn2_b, L1_gnn_W_self, L1_gnn_W_inter):
    import jax
    import jax.numpy as jnp

    def _L0_gnn_ref(x, edge_attr, edge_index, Wq, Wk, We, Wv, bn1_g, bn1_b, W1, b1, W2, b2, bn2_g, bn2_b):
        import jax, jax.numpy as jnp
        import numpy as np
        H = 8
        DH = 16
        D = 128
        EPS_BN = 1e-05

        def _batchnorm(h, gamma, beta):
            mu = h.mean(axis=0)
            var = h.var(axis=0)
            return (h - mu) / jnp.sqrt(var + EPS_BN) * gamma + beta

        def _forward(x, edge_attr, edge_index, Wq, Wk, We, Wv, bn1_g, bn1_b, W1, b1, W2, b2, bn2_g, bn2_b):
            N = x.shape[0]
            src, dst = (edge_index[0], edge_index[1])
            Q_h = (x @ Wq).reshape(N, H, DH)
            K_h = (x @ Wk).reshape(N, H, DH)
            V_h = (x @ Wv).reshape(N, H, DH)
            E_e = (edge_attr @ We).reshape(-1, H, DH)
            score = K_h[src] * Q_h[dst] / np.sqrt(DH) * E_e
            score = jnp.exp(jnp.clip(score.sum(-1, keepdims=True), -5.0, 5.0))
            msg = V_h[src] * score
            wV = jax.ops.segment_sum(msg, dst, num_segments=N)
            Z = jax.ops.segment_sum(score, dst, num_segments=N)
            h_attn = (wV / (Z + 1e-06)).reshape(N, D)
            h = x + h_attn
            h = _batchnorm(h, bn1_g, bn1_b)
            h2 = jax.nn.relu(h @ W1 + b1)
            h2 = h2 @ W2 + b2
            h = h + h2
            h = _batchnorm(h, bn2_g, bn2_b)
            return h
        return _forward(x, edge_attr, edge_index, Wq, Wk, We, Wv, bn1_g, bn1_b, W1, b1, W2, b2, bn2_g, bn2_b)

    def _L1_gnn_ref(feature, src, dst, W_self, W_inter):
        import jax, jax.numpy as jnp
        import numpy as np
        N_NODES = 3125
        N_EDGES = 50000
        D_IN = 128
        D_OUT = 128
        n = feature.shape[0]
        ones = jnp.ones_like(src, dtype=jnp.float32)
        out_deg = jnp.clip(jax.ops.segment_sum(ones, src, num_segments=n), 1.0)
        in_deg = jnp.clip(jax.ops.segment_sum(ones, dst, num_segments=n), 1.0)
        h = feature * (out_deg ** (-0.5))[:, None]
        h_self = jax.ops.segment_sum(h[src], dst, num_segments=n)
        m_inter = h[src] * feature[dst]
        h_inter = jax.ops.segment_sum(m_inter, dst, num_segments=n)
        rst = h_self @ W_self + h_inter @ W_inter
        rst = rst * (in_deg ** (-0.5))[:, None]
        rst = rst + feature @ W_self
        return rst
    edge_index = jnp.stack([src, dst])
    h = jnp.maximum(_layernorm(x, axis=-1), 0.0)
    x = x + _L0_gnn_ref(h, edge_attr_128, edge_index, L0_gnn_Wq, L0_gnn_Wk, L0_gnn_We, L0_gnn_Wv, L0_gnn_bn1_g, L0_gnn_bn1_b, L0_gnn_W1, L0_gnn_b1, L0_gnn_W2, L0_gnn_b2, L0_gnn_bn2_g, L0_gnn_bn2_b)
    h = jnp.maximum(_layernorm(x, axis=-1), 0.0)
    x = x + _L1_gnn_ref(h, src, dst, L1_gnn_W_self, L1_gnn_W_inter)
    return x

_drawn_inputs = setup_inputs


def setup_inputs(seed=0):
    import zlib

    import numpy as np

    out = dict(_drawn_inputs(seed))
    spreads = {'L0_gnn_bn1_g': (1.0, 0.2),
     'L0_gnn_bn1_b': (0.0, 0.384),
     'L0_gnn_b1': (0.0, 0.348),
     'L0_gnn_b2': (0.0, 0.8),
     'L0_gnn_bn2_g': (1.0, 0.2),
     'L0_gnn_bn2_b': (0.0, 0.1)}
    factors = {}
    for name, (base, spread) in spreads.items():
        noise = np.random.default_rng([zlib.crc32(name.encode()), seed]).standard_normal(out[name].shape)
        drawn = base * np.exp(spread * noise) if base else spread * noise
        out[name] = jnp.asarray(drawn.astype(out[name].dtype))
    for name, factor in factors.items():
        out[name] = (out[name] * factor).astype(out[name].dtype)
    return out
```

```python
import concourse.bass as bass
from concourse import mybir
from contextlib import ExitStack

FP32 = mybir.dt.float32
BF16 = mybir.dt.bfloat16
I32 = mybir.dt.int32
ALU = mybir.AluOpType
ACT = mybir.ActivationFunctionType
AX = mybir.AxisListType

P = 128
N = 50000
D = 128
H, DH = 8, 16
EPS = 1e-5

ET = N // P
ER = N - ET * P
EU = ET // 2
NG = 97
NT = 4 * NG
NR, NRC = 112, 3
assert P * NT + NR * NRC == N and EU * 2 == ET
NC = NT + NRC

ROW = 144
WCOL, CCOL = D, D + H
USED = D + H + 1
TROWS = N + P


class Step:

    def __init__(self, eng, index, turn, slot, tail, sizes):
        self.eng, self.index, self.turn, self.slot, self.tail = eng, index, turn, slot, tail
        self.rows, self.tiles = sizes[1] if tail else sizes[0]
        self.first = isinstance(index, int) and index == 0
        self.fresh = isinstance(index, int) and index < 2
        self.done = self.value(index + 1)

    def value(self, x):
        return x if isinstance(x, int) else self.eng.snap(x)


def walk(eng, units, stages, sizes):
    most = max(lag for lag, _ in stages)
    first = most + 2
    first += (units - first) % 2

    def full(u):
        for lag, fn in stages:
            if 0 <= u - lag <= units:
                fn(Step(eng, u - lag, (u - lag) // 2, (u - lag) % 2, u - lag == units, sizes))

    for u in range(first):
        full(u)
    with eng.Fori(0, (units - first) // 2) as i:
        for half in range(2):
            for lag, fn in stages:
                at = first + half - lag
                fn(Step(eng, i * 2 + at, i + at // 2, at % 2, False, sizes))
    for u in range(units, units + most + 1):
        full(u)


EDGE_SIZES = ((P, 2), (ER, 1))
NODE_SIZES = ((P, 4), (NR, NRC))


def edge_rows(t, s):
    if s.tail:
        return t[P * ET:N, :].rearrange("(p t) d -> p t d", t=1)
    return t[0:P * ET, :].rearrange("(p t) d -> p t d", p=P)[:, bass.ds(s.index * 2, 2), :]


def node_rows(t, s):
    if s.tail:
        return t[P * NT:N, :].rearrange("(p t) d -> p t d", p=NR)
    return t[0:P * NT, :].rearrange("(p t) d -> p t d", p=P)[:, bass.ds(s.index * 4, 4), :]


def cols(t, s, width):
    if s.tail:
        return t[0:s.rows, width * s.index:width * s.index + s.tiles]
    return t[:, bass.ds(s.index * width, width)]


def spread(ap, n):
    a, b = ap.shape
    return ap.unsqueeze(2).broadcast_to([a, b, n])


def build(nc, x, src, dst, edge_attr, Wq, Wk, We, Wv, bn1_g, bn1_b, W1, b1, W2, b2, bn2_g, bn2_b,
          W_self, W_inter, out):
    ctx = ExitStack()
    with ctx:
        def sb(name, shape, dt=FP32):
            return ctx.enter_context(nc.sbuf_tensor(name, shape, dt))

        def dram(name, shape):
            return nc.dram_tensor(name, shape, FP32, kind="Internal").ap()

        k = {}
        k["bank"] = [ctx.enter_context(nc.psum_tensor(f"bank{i}", [P, 512], FP32)) for i in range(8)]
        k["table"] = dram("table", (TROWS, ROW))
        k["sums"] = [dram(f"sums{i}", (TROWS, D)) for i in range(2)]
        k["h1T"] = dram("h1T", (NG + 1, P, 512))
        k["zT"] = dram("zT", (NG + 1, P, 512))
        k["x2"] = dram("x2", (N, D))
        k["g"] = dram("g", (N, D))
        k["degree"] = dram("degree", (ET + 1, P))

        k["ident"] = sb("ident", [P, P])
        k["Wkv"] = sb("Wkv", [P, 2 * D])
        k["Wq"] = sb("Wq", [P, D])
        k["We"] = sb("We", [P, D])
        k["W1"] = sb("W1", [P, 2 * D])
        k["W2"] = sb("W2", [P, 2, D])
        k["Ws"] = sb("Ws", [P, D])
        k["Wi"] = sb("Wi", [P, D])
        k["b1"] = sb("b1", [P, 2])
        for name in ("b2", "g1", "be1", "g2", "be2", "eps"):
            k[name] = sb(name, [P, 1])
        k["dst_f"] = sb("dst_f", [P, ET + 1])
        k["ends"] = sb("ends", [P, ET + 1, 2], I32)
        k["target"] = sb("target", [P, ET + 1], I32)
        k["in_deg"] = sb("in_deg", [P, NC])
        k["out_deg"] = sb("out_deg", [P, NC])
        k["scale2"] = sb("scale2", [P, NC])
        k["shift2"] = sb("shift2", [P, NC])
        k["bn1"] = sb("bn1", [P, NG + 1, 6])
        k["bn2"] = sb("bn2", [P, NG + 1, 6])

        edge_stages(nc, k, x, src, dst, edge_attr, Wq, Wk, We, Wv, bn1_g, bn1_b, W1, b1, W2, b2, bn2_g,
                    bn2_b, W_self, W_inter)
        residual_stage(nc, k, x)
        mlp_stage(nc, k)
        normed_stage(nc, k, x)
        convolution_stage(nc, k)
        output_stage(nc, k, out)


def edge_stages(nc, k, x, src, dst, edge_attr, Wq, Wk, We, Wv, bn1_g, bn1_b, W1, b1, W2, b2, bn2_g,
                bn2_b, W_self, W_inter):
    ctx = ExitStack()
    with ctx:
        def sb(name, shape, dt=FP32):
            return ctx.enter_context(nc.sbuf_tensor(name, shape, dt))

        def sem(name):
            return ctx.enter_context(nc.semaphore(name))

        table, ident, dst_f, ends, target = k["table"], k["ident"], k["dst_f"], k["ends"], k["target"]
        src_i = sb("src_i", [P, ET + 1], I32)
        dst_i = sb("dst_i", [P, ET + 1], I32)
        bits = sb("bits", [P, ET + 1], I32)
        src_lo = sb("src_lo", [P, ET + 1])
        src_hi = sb("src_hi", [P, ET + 1])
        spare = sb("spare", [P, ET + 1])
        spare_row = sb("spare_row", [P, 1])
        count_i = sb("count_i", [P, ET + 1], I32)
        count_f = sb("count_f", [P, ET + 1])
        prow_i = sb("prow_i", [P, 1], I32)
        before = sb("before", [P, P])
        ones = sb("ones", [P, P])
        zero_cols = 2169
        zeros = sb("zeros", [P, zero_cols])

        index = sb("index", [P, 2, 2, 2], I32)
        rows_in = sb("rows_in", [P, 2, 2, 2, D])
        attr = sb("attr", [P, 2, 2, D])
        stat = sb("stat", [P, 2, 4, 6])
        mv = sb("mv", [P, 2, 4, 2])
        negmean = sb("negmean", [P, 2, 4])
        lnvar = sb("lnvar", [P, 2, 4])
        rstd = sb("rstd", [P, 2, 4])
        rr = sb("rr", [P, 2, 2])
        dst_now = sb("dst_now", [P, 2, 2])
        h = sb("h", [P, 2, 4, D])
        hT = sb("hT", [P, 2, 4, P])
        attrT = sb("attrT", [P, 2, 2, P])
        q = sb("q", [P, 2, 2, D])
        kq = sb("kq", [P, 2, D])
        kqe = sb("kqe", [P, 2, D])
        raw = sb("raw", [P, 2, H])
        scaled = sb("scaled", [P, 2, H])
        clipped = sb("clipped", [P, 2, H])
        wr = sb("wr", [P, 2, H])
        message = sb("message", [P, 2, 2, ROW])
        same = sb("same", [P, 2, 2, P])
        earlier = sb("earlier", [P, 2, P])
        rank = sb("rank", [P, 2])
        move = sb("move", [P, 2])
        hot_lo = sb("hot_lo", [P, 2, 2, P], BF16)
        hot_hi = sb("hot_hi", [P, 2, 2, ET + 1], BF16)
        group = sb("group", [P, 2, 2, ROW])
        add_at = sb("add_at", [P, 2, 2], I32)
        hist = sb("hist", [P, ET + 1])
        histT = sb("histT", [P, 4, P])

        loaded, cleared, const_ready = sem("loaded"), sem("cleared"), sem("const_ready")
        prep, zeros_ready = sem("prep"), sem("zeros_ready")
        index_ready = sem("index_ready")
        landed = [sem(f"landed{i}") for i in range(2)]
        attr_landed = [sem(f"attr_landed{i}") for i in range(2)]
        stats_ready, mv_ready, negmean_ready = sem("stats_ready"), sem("mv_ready"), sem("negmean_ready")
        ln_ready, rstd_ready, h_ready = sem("ln_ready"), sem("rstd_ready"), sem("h_ready")
        turned, attr_turned, dst_turned = sem("turned"), sem("attr_turned"), sem("dst_turned")
        hT_ready, attrT_ready = sem("hT_ready"), sem("attrT_ready")
        same_ready, earlier_ready, rank_ready = sem("same_ready"), sem("earlier_ready"), sem("rank_ready")
        move_ready, target_ready = sem("move_ready"), sem("target_ready")
        hot_ready, counted = sem("hot_ready"), sem("counted")
        products_ready, q_ready = sem("products_ready"), sem("q_ready")
        kq_ready, kqe_ready, raw_ready = sem("kq_ready"), sem("kqe_ready"), sem("raw_ready")
        rr_ready, scaled_ready, clipped_ready = sem("rr_ready"), sem("scaled_ready"), sem("clipped_ready")
        weight_ready, wr_ready, message_ready = sem("weight_ready"), sem("wr_ready"), sem("message_ready")
        grouped, group_ready = sem("grouped"), sem("group_ready")
        rows_added, held = sem("rows_added"), sem("held")
        sums_cleared = sem("sums_cleared")
        hist_ready, hist_turned, histT_ready, degree_stored = (
            sem("hist_ready"), sem("hist_turned"), sem("histT_ready"), sem("degree_stored"))

        bank = k["bank"]
        bank_rows, bank_attr, bank_kv, bank_qe, bank_group, bank_hist, bank_dst = bank[0:7]
        rowsT = bank_rows[:, :].rearrange("p (a e) -> p a e", a=4)
        attr_ps = bank_attr[:, 0:2 * P].rearrange("p (a e) -> p a e", a=2)
        dst_ps = bank_dst[:, 0:2 * P].rearrange("p (a e) -> p a e", a=2)
        kv = bank_kv[:, :].rearrange("p (t a f) -> p t a f", t=2, a=2)
        qe = bank_qe[:, :].rearrange("p (t a f) -> p t a f", t=2, a=2)
        grp = bank_group[:, 0:2 * ROW].rearrange("p (t f) -> p t f", t=2)
        hist_ps = bank_hist[:, 0:ET + 1]
        histT_ps = bank_rows[:, :].rearrange("p (a e) -> p a e", a=4)

        weight_loads = [
            (k["Wkv"][:, 0:D], Wk), (k["Wkv"][:, D:2 * D], Wv), (k["Wq"][:, :], Wq), (k["We"][:, :], We),
            (k["W1"][:, :], W1), (k["W2"][:, :, :], W2.rearrange("(c p) n -> p c n", p=P)),
            (k["Ws"][:, :], W_self), (k["Wi"][:, :], W_inter),
        ] + [(k["b1"][:, c:c + 1], b1[c * D:(c + 1) * D].rearrange("(p o) -> p o", o=1)) for c in range(2)
        ] + [(k[name][:, :], v.rearrange("(p o) -> p o", o=1)) for name, v in
             (("b2", b2), ("g1", bn1_g), ("be1", bn1_b), ("g2", bn2_g), ("be2", bn2_b))]
        index_loads = [
            (t[:, 0:ET], v[0:P * ET].rearrange("(p t) -> p t", p=P)) for t, v in ((src_i, src), (dst_i, dst))
        ] + [(t[0:ER, ET:ET + 1], v[P * ET:N].rearrange("(p t) -> p t", t=1))
             for t, v in ((src_i, src), (dst_i, dst))]

        with nc.Block() as block:
            @block.sync
            def _(sp):
                for to, of in index_loads + weight_loads:
                    sp.dma_start(to, of).then_inc(loaded, 16)
                sp.wait_ge(zeros_ready, 1)
                flat = table.rearrange("r f -> (r f)").rearrange("(p c n) -> p c n", p=P, n=zero_cols)
                sp.dma_start(flat, zeros[:, :].unsqueeze(1).broadcast_to([P, TROWS * ROW // P // zero_cols,
                                                                          zero_cols])).then_inc(cleared, 16)
                sp.wait_ge(cleared, 16)

            @block.gpsimd
            def _(pool):
                nc.gpsimd.iota(count_i[:, :], pattern=[[1, ET + 1]], base=0, channel_multiplier=0)\
                    .then_inc(const_ready, 1)
                nc.gpsimd.iota(prow_i[:, :], pattern=[[1, 1]], base=N, channel_multiplier=1)\
                    .then_inc(const_ready, 1)
                pool.wait_ge(prep, 1)
                nc.gpsimd.affine_select(out=ident[:, :], in_=ones[:, :], compare_op=ALU.is_equal, fill=0.0,
                                        base=0, pattern=[[-1, P]], channel_multiplier=1)\
                    .then_inc(const_ready, 1)
                nc.gpsimd.affine_select(out=before[:, :], in_=ones[:, :], compare_op=ALU.is_gt, fill=0.0,
                                        base=0, pattern=[[-1, P]], channel_multiplier=1)\
                    .then_inc(const_ready, 1)

            @block.vector
            def _(dve):
                dve.memset(zeros[:, :], 0.0).then_inc(zeros_ready, 1)
                dve.memset(ones[:, :], 1.0).then_inc(prep, 1)
                dve.memset(message[:, :, :, USED:ROW], 0.0).then_inc(prep, 1)
                dve.memset(message[:, :, :, CCOL:CCOL + 1], 1.0).then_inc(prep, 1)
                dve.memset(k["eps"][:, :], EPS).then_inc(prep, 1)
                dve.wait_ge(const_ready, 2)
                dve.tensor_copy(count_f[:, :], count_i[:, :])
                dve.tensor_copy(spare_row[:, :], prow_i[:, :]).then_inc(prep, 1)
                dve.wait_ge(loaded, 16 * len(index_loads + weight_loads))
                for rows, c0, c1 in ((P, 0, ET), (ER, ET, ET + 1)):
                    a = slice(0, rows), slice(c0, c1)
                    dve.tensor_copy(ends[a[0], a[1], 0], src_i[a])
                    dve.tensor_copy(ends[a[0], a[1], 1], dst_i[a])
                    dve.tensor_copy(dst_f[a], dst_i[a])
                    dve.tensor_scalar(bits[a], src_i[a], P - 1, None, ALU.bitwise_and).then_inc(prep, 1)
                dve.wait_ge(prep, 7)
                for rows, c0, c1 in ((P, 0, ET), (ER, ET, ET + 1)):
                    a = slice(0, rows), slice(c0, c1)
                    dve.tensor_copy(src_lo[a], bits[a])
                    dve.tensor_scalar(spare[a], dst_f[a], -1.0, spare_row[0:rows, :], ALU.mult, ALU.add)\
                        .then_inc(prep, 1)
                dve.wait_ge(prep, 9)
                for rows, c0, c1 in ((P, 0, ET), (ER, ET, ET + 1)):
                    a = slice(0, rows), slice(c0, c1)
                    dve.tensor_scalar(bits[a], src_i[a], 7, None, ALU.logical_shift_right).then_inc(prep, 1)
                dve.wait_ge(prep, 11)
                for rows, c0, c1 in ((P, 0, ET), (ER, ET, ET + 1)):
                    a = slice(0, rows), slice(c0, c1)
                    dve.tensor_copy(src_hi[a], bits[a])

        with nc.Block() as block:
            @block.sync
            def _(sp):
                def load_attr(s):
                    free = s.value(s.index - 1)
                    if not s.fresh:
                        sp.wait_ge(attr_turned, free)
                    sp.dma_start(attr[0:s.rows, s.slot, 0:s.tiles, :], edge_rows(edge_attr, s))\
                        .then_inc(attr_landed[s.slot], 16)

                def clear_sums(s):
                    rows, parts = (TROWS - 2 * P * EU, (TROWS - 2 * P * EU) // 2) if s.tail else (2 * P, P)
                    r0 = s.value(s.index * (2 * P))
                    for t in k["sums"]:
                        part = t[r0:r0 + rows, :] if s.tail else t[bass.ds(r0, rows), :]
                        sp.dma_start(part.rearrange("(p r) d -> p (r d)", r=2), zeros[0:parts, 0:2 * D])\
                            .then_inc(sums_cleared, 16)

                walk(sp, EU, [(0, load_attr), (0, clear_sums)], EDGE_SIZES)
                sp.wait_ge(sums_cleared, 32 * (EU + 1))

            @block.gpsimd
            def _(pool):
                def hold(*waits):
                    for sem_, value in waits:
                        pool.wait_ge(sem_, value)
                    pool.sem_inc(held, 1)

                def gather(s, j):
                    for end in range(2):
                        pool.indirect_dma_start(
                            rows_in[0:s.rows, s.slot, j, end, :], None, x,
                            bass.IndirectOffsetOnAxis(index[0:s.rows, s.slot, j, end:end + 1], 0))\
                            .then_inc(landed[s.slot], 16)

                def add(s, j):
                    pool.indirect_dma_start(
                        table, bass.IndirectOffsetOnAxis(add_at[0:s.rows, s.slot, j:j + 1], 0),
                        group[0:s.rows, s.slot, j, :], None, compute_op=ALU.add).then_inc(rows_added, 16)

                def gather_first(s):
                    free = s.value(s.index - 1)
                    waits = [(index_ready, s.done)]
                    if not s.fresh:
                        waits.append((h_ready, free))
                    hold(*waits)
                    gather(s, 0)

                def gather_second(s):
                    if s.tiles > 1:
                        gather(s, 1)

                def add_first(s):
                    last = s.value(s.index * 32)
                    waits = [(group_ready, s.done)]
                    if not s.first:
                        waits.append((rows_added, last))
                    hold(*waits)
                    add(s, 0)

                def add_second(s):
                    last = s.value(s.index * 32 + 16)
                    if s.tiles > 1:
                        hold((rows_added, last))
                        add(s, 1)

                walk(pool, EU, [(3, add_first), (0, gather_first), (3, add_second), (0, gather_second)],
                     EDGE_SIZES)
                pool.wait_ge(rows_added, 32 * EU + 16)

            @block.vector
            def _(dve):
                def hold(*waits):
                    for sem_, value in waits:
                        dve.wait_ge(sem_, value)
                    dve.sem_inc(held, 1)

                def make_index(s):
                    landed_value = s.value(s.turn * 64)
                    if not s.fresh:
                        hold((landed[s.slot], landed_value))
                    t0 = s.index * 2
                    part = (ends[0:s.rows, t0:t0 + s.tiles, :] if s.tail
                            else ends[:, bass.ds(t0, 2), :])
                    dve.tensor_copy(index[0:s.rows, s.slot, 0:s.tiles, :], part).then_inc(index_ready, 1)

                def stats(s):
                    full = s.value(s.turn * 64 + (32 if s.tail else 64))
                    n, r = 2 * s.tiles, s.rows
                    dve.wait_ge(landed[s.slot], full)
                    for a in range(n):
                        last = dve.bn_stats(stat[0:r, s.slot, a, :], rows_in[0:r, s.slot, a // 2, a % 2, :])
                    last.then_inc(stats_ready, 1)
                    hold((stats_ready, s.done))
                    for a in range(n):
                        last = dve.bn_aggr(mv[0:r, s.slot, a, :], stat[0:r, s.slot, a, :])
                    last.then_inc(mv_ready, 1)
                    dve.tensor_copy(dst_now[0:r, s.slot, 0:s.tiles], cols(dst_f, s, 2))
                    dve.wait_ge(mv_ready, s.done)
                    dve.tensor_scalar(negmean[0:r, s.slot, 0:n], mv[0:r, s.slot, 0:n, 0], -1.0, None,
                                      ALU.mult).then_inc(negmean_ready, 1)

                def score(s):
                    r, n = s.rows, s.tiles
                    dve.wait_ge(q_ready, s.done)
                    dve.tensor_tensor(kq[0:r, 0:n, :], kv[0:r, 0:n, 0, :], q[0:r, s.slot, 0:n, :], ALU.mult)\
                        .then_inc(kq_ready, 1)
                    dve.wait_ge(rstd_ready, s.done)
                    rs = rstd[0:r, s.slot, 0:2 * n].rearrange("p (t a) -> p t a", a=2)
                    dve.tensor_tensor(rr[0:r, s.slot, 0:n], rs[:, :, 0], rs[:, :, 1], ALU.mult)\
                        .then_inc(rr_ready, 1)
                    dve.wait_ge(kq_ready, s.done)
                    dve.tensor_tensor(kqe[0:r, 0:n, :], kq[0:r, 0:n, :], qe[0:r, 0:n, 1, :], ALU.mult)\
                        .then_inc(kqe_ready, 1)
                    dve.wait_ge(kqe_ready, s.done)
                    dve.tensor_reduce(raw[0:r, 0:n, :],
                                      kqe[0:r, 0:n, :].rearrange("p t (h d) -> p t h d", h=H), AX.X,
                                      ALU.add).then_inc(raw_ready, 1)
                    dve.wait_ge(rr_ready, s.done)
                    dve.wait_ge(raw_ready, s.done)
                    dve.tensor_tensor(scaled[0:r, 0:n, :], raw[0:r, 0:n, :], spread(rr[0:r, s.slot, 0:n], H),
                                      ALU.mult).then_inc(scaled_ready, 1)
                    dve.wait_ge(scaled_ready, s.done)
                    dve.tensor_scalar(clipped[0:r, 0:n, :], scaled[0:r, 0:n, :], 5.0, -5.0, ALU.min, ALU.max)\
                        .then_inc(clipped_ready, 1)

                def compare(s):
                    r, n = s.rows, s.tiles
                    turn_free = s.value(s.index - 1)
                    if not s.fresh:
                        dve.wait_ge(grouped, turn_free)
                    dve.wait_ge(dst_turned, s.done)
                    dve.tensor_tensor(same[0:r, s.slot, 0:n, 0:r], dst_ps[0:r, 0:n, 0:r],
                                      spread(cols(dst_f, s, 2), r), ALU.is_equal).then_inc(same_ready, 1)
                    dve.wait_ge(same_ready, s.done)
                    dve.tensor_tensor(earlier[0:r, 0:n, 0:r], same[0:r, s.slot, 0:n, 0:r],
                                      before[0:r, 0:r].unsqueeze(1).broadcast_to([r, n, r]), ALU.mult)\
                        .then_inc(earlier_ready, 1)
                    dve.wait_ge(earlier_ready, s.done)
                    dve.tensor_reduce(rank[0:r, 0:n], earlier[0:r, 0:n, 0:r], AX.X, ALU.add)\
                        .then_inc(rank_ready, 1)
                    dve.wait_ge(rank_ready, s.done)
                    dve.scalar_tensor_tensor(move[0:r, 0:n], rank[0:r, 0:n], 0.0, cols(spare, s, 2),
                                             ALU.is_gt, ALU.mult).then_inc(move_ready, 1)
                    dve.wait_ge(move_ready, s.done)
                    dve.tensor_tensor(cols(target, s, 2), move[0:r, 0:n], cols(dst_f, s, 2), ALU.add)\
                        .then_inc(target_ready, 1)

                def one_hots(s):
                    r = s.rows
                    free = s.value(s.index - 1)
                    if not s.fresh:
                        hold((counted, free))
                    for j in range(s.tiles):
                        t = s.index * 2 + j
                        lo = src_lo[0:r, t:t + 1] if s.tail else src_lo[0:r, bass.ds(t, 1)]
                        hi = src_hi[0:r, t:t + 1] if s.tail else src_hi[0:r, bass.ds(t, 1)]
                        dve.tensor_scalar(hot_lo[0:r, s.slot, j, :], count_f[0:r, 0:P], lo, None,
                                          ALU.is_equal)
                        last = dve.tensor_scalar(hot_hi[0:r, s.slot, j, :], count_f[0:r, :], hi, None,
                                                 ALU.is_equal)
                    last.then_inc(hot_ready, 1)

                def messages(s):
                    r, n = s.rows, s.tiles
                    slot_added = s.value(s.index * 32 - 32)
                    t0 = s.index * 2
                    dve.wait_ge(weight_ready, s.done)
                    if not s.fresh:
                        dve.wait_ge(rows_added, slot_added)
                    rs = rstd[0:r, s.slot, 0:2 * n].rearrange("p (t a) -> p t a", a=2)
                    dve.tensor_tensor(wr[0:r, 0:n, :], message[0:r, s.slot, 0:n, WCOL:WCOL + H],
                                      spread(rs[:, :, 0], H), ALU.mult).then_inc(wr_ready, 1)
                    hold((target_ready, s.done))
                    part = (target[0:r, t0:t0 + n] if s.tail else target[:, bass.ds(t0, 2)])
                    dve.tensor_copy(add_at[0:r, s.slot, 0:n], part)
                    dve.wait_ge(wr_ready, s.done)
                    for j in range(n):
                        last = dve.tensor_tensor(
                            message[0:r, s.slot, j, 0:D].rearrange("p (h d) -> p h d", h=H),
                            kv[0:r, j, 1, :].rearrange("p (h d) -> p h d", h=H),
                            spread(wr[0:r, j, :], DH), ALU.mult)
                    last.then_inc(message_ready, 1)

                walk(dve, EU, [(2, stats), (0, make_index), (3, score), (2, compare), (2, one_hots),
                               (3, messages)], EDGE_SIZES)
                dve.wait_ge(counted, EU + 1)
                dve.tensor_copy(hist[:, :], hist_ps).then_inc(hist_ready, 1)
                dve.wait_ge(hist_turned, 1)
                for c in range(4):
                    w = min(P, ET + 1 - c * P)
                    last = dve.tensor_copy(histT[0:w, c, :], histT_ps[0:w, c, :])
                last.then_inc(histT_ready, 1)

            @block.scalar
            def _(act):
                act.preload_act_table_set("natural_log_exp_and_others")

                def queries(s):
                    r, n = s.rows, s.tiles
                    act.wait_ge(products_ready, s.done)
                    act.activation(q[0:r, s.slot, 0:n, :], qe[0:r, 0:n, 0, :], ACT.Copy,
                                   scale=float(DH) ** -0.5).then_inc(q_ready, 1)

                def norm(s):
                    r, n = s.rows, 2 * s.tiles
                    act.wait_ge(negmean_ready, s.done)
                    for a in range(n):
                        last = act.activation(h[0:r, s.slot, a, :], rows_in[0:r, s.slot, a // 2, a % 2, :],
                                              ACT.Relu, bias=negmean[0:r, s.slot, a:a + 1])
                    last.then_inc(h_ready, 1)
                    act.activation(lnvar[0:r, s.slot, 0:n], mv[0:r, s.slot, 0:n, 1], ACT.Ln,
                                   bias=k["eps"][0:r, :]).then_inc(ln_ready, 1)
                    act.wait_ge(ln_ready, s.done)
                    act.activation(rstd[0:r, s.slot, 0:n], lnvar[0:r, s.slot, 0:n], ACT.Exp, scale=-0.5)\
                        .then_inc(rstd_ready, 1)

                def weights(s):
                    r, n = s.rows, s.tiles
                    act.wait_ge(clipped_ready, s.done)
                    act.activation(message[0:r, s.slot, 0:n, WCOL:WCOL + H], clipped[0:r, 0:n, :], ACT.Exp)\
                        .then_inc(weight_ready, 1)

                def evacuate(s):
                    r, n = s.rows, s.tiles
                    act.wait_ge(turned, s.done)
                    act.activation(hT[:, s.slot, 0:2 * n, 0:r], rowsT[:, 0:2 * n, 0:r], ACT.Copy)\
                        .then_inc(hT_ready, 1)
                    act.wait_ge(attr_turned, s.done)
                    act.activation(attrT[:, s.slot, 0:n, 0:r], attr_ps[:, 0:n, 0:r], ACT.Copy)\
                        .then_inc(attrT_ready, 1)

                def group_sums(s):
                    r, n = s.rows, s.tiles
                    act.wait_ge(grouped, s.done)
                    act.activation(group[0:r, s.slot, 0:n, :], grp[0:r, 0:n, :], ACT.Copy)\
                        .then_inc(group_ready, 1)

                walk(act, EU, [(1, queries), (0, norm), (1, weights), (0, evacuate), (1, group_sums)],
                     EDGE_SIZES)
                act.wait_ge(histT_ready, 1)
                for c in range(4):
                    w = min(P, ET + 1 - c * P)
                    act.dma_start(k["degree"][c * P:c * P + w, :], histT[0:w, c, :])\
                        .then_inc(degree_stored, 16)
                act.wait_ge(degree_stored, 64)

            @block.tensor
            def _(pe):
                def turn(s):
                    r, n = s.rows, s.tiles
                    full = s.value(s.turn * 16 + 16)
                    prev = s.value(s.index * 1)
                    pe.wait_ge(h_ready, s.done)
                    if not s.first:
                        pe.wait_ge(hT_ready, prev)
                    for a in range(2 * n):
                        last = pe.transpose(rowsT[:, a, 0:r], h[0:r, s.slot, a, :], ident[0:r, 0:r])
                    last.then_inc(turned, 1)
                    pe.wait_ge(attr_landed[s.slot], full)
                    if not s.first:
                        pe.wait_ge(attrT_ready, prev)
                    for j in range(n):
                        last = pe.transpose(attr_ps[:, j, 0:r], attr[0:r, s.slot, j, :], ident[0:r, 0:r])
                    last.then_inc(attr_turned, 1)
                    if not s.first:
                        pe.wait_ge(same_ready, prev)
                    for j in range(n):
                        last = pe.transpose(dst_ps[:, j, 0:r],
                                            dst_now[0:r, s.slot, j:j + 1].broadcast_to([r, P]),
                                            ident[0:r, 0:r])
                    last.then_inc(dst_turned, 1)

                def count(s):
                    r = s.rows
                    pe.wait_ge(hot_ready, s.done)
                    for j in range(s.tiles):
                        last = pe.matmul(hist_ps, hot_lo[0:r, s.slot, j, :], hot_hi[0:r, s.slot, j, :],
                                         start=s.first and j == 0, stop=s.tail)
                    last.then_inc(counted, 1)

                def product(s):
                    r = s.rows
                    prev = s.value(s.index * 1)
                    pe.wait_ge(hT_ready, s.done)
                    pe.wait_ge(attrT_ready, s.done)
                    if not s.first:
                        pe.wait_ge(message_ready, prev)
                    for j in range(s.tiles):
                        pe.matmul(kv[0:r, j, :, :].rearrange("p a f -> p (a f)"), hT[:, s.slot, 2 * j, 0:r],
                                  k["Wkv"][:, :], start=True, stop=True)
                        pe.matmul(qe[0:r, j, 0, :], hT[:, s.slot, 2 * j + 1, 0:r], k["Wq"][:, :],
                                  start=True, stop=True)
                        last = pe.matmul(qe[0:r, j, 1, :], attrT[:, s.slot, j, 0:r], k["We"][:, :],
                                         start=True, stop=True)
                    last.then_inc(products_ready, 1)

                def group_up(s):
                    r = s.rows
                    prev = s.value(s.index * 1)
                    pe.wait_ge(message_ready, s.done)
                    if not s.first:
                        pe.wait_ge(group_ready, prev)
                    for j in range(s.tiles):
                        last = pe.matmul(grp[0:r, j, :], same[0:r, s.slot, j, 0:r],
                                         message[0:r, s.slot, j, :], start=True, stop=True)
                    last.then_inc(grouped, 1)

                walk(pe, EU, [(0, turn), (0, count), (1, group_up), (0, product)], EDGE_SIZES)
                pe.wait_ge(hist_ready, 1)
                for c in range(4):
                    w = min(P, ET + 1 - c * P)
                    last = pe.transpose(histT_ps[0:w, c, :], hist[:, c * P:c * P + w], ident[:, :])
                last.then_inc(hist_turned, 1)


def norm_constants(k, act, dve, stats, gamma, beta, tiles, sems):
    mean_var, logvar, std_inv, scale, shift = tiles
    aggregated, logged, inverted, scaled, shift_ready = sems

    def on_act():
        act.wait_ge(aggregated, 1)
        act.activation(logvar[:, :], mean_var[:, 1:2], ACT.Ln, bias=k["eps"][:, :]).then_inc(logged, 1)
        act.wait_ge(logged, 1)
        act.activation(std_inv[:, :], logvar[:, :], ACT.Exp, scale=-0.5).then_inc(inverted, 1)

    def on_dve():
        dve.bn_aggr(mean_var[:, :], stats[:, :, :].rearrange("p a b -> p (a b)")).then_inc(aggregated, 1)
        dve.wait_ge(inverted, 1)
        dve.tensor_tensor(scale[:, :], std_inv[:, :], gamma[:, :], ALU.mult).then_inc(scaled, 1)
        dve.wait_ge(scaled, 1)
        dve.tensor_tensor(logvar[:, :], mean_var[:, 0:1], scale[:, :], ALU.mult).then_inc(scaled, 1)
        dve.wait_ge(scaled, 2)
        dve.tensor_tensor(shift[:, :], beta[:, :], logvar[:, :], ALU.subtract).then_inc(shift_ready, 1)

    return on_act, on_dve


def residual_stage(nc, k, x):
    ctx = ExitStack()
    with ctx:
        def sb(name, shape, dt=FP32):
            return ctx.enter_context(nc.sbuf_tensor("b_" + name, shape, dt))

        def sem(name):
            return ctx.enter_context(nc.semaphore("b_" + name))

        xg = sb("xg", [P, 2, 4, D])
        acc = sb("acc", [P, 2, 4, ROW])
        stat = sb("stat", [P, 2, 4, 6])
        mv = sb("mv", [P, 2, 4, 2])
        lnvar = sb("lnvar", [P, 2, 4])
        rstd = sb("rstd", [P, 2, 4])
        shift = sb("shift", [P, 2, 4])
        h = sb("h", [P, 2, 4, D])
        weight = sb("weight", [P, 2, 4, H])
        weight_inv = sb("weight_inv", [P, 2, 4, H])
        attn = sb("attn", [P, 2, 4, D])
        h1 = sb("h1", [P, 2, 4, D])
        h1T = sb("h1T", [P, 2, 512])

        x_landed = [sem(f"x_landed{i}") for i in range(2)]
        acc_landed = [sem(f"acc_landed{i}") for i in range(2)]
        h1T_stored = [sem(f"h1T_stored{i}") for i in range(2)]
        stats_ready, mv_ready, ln_ready, rstd_ready = (
            sem("stats_ready"), sem("mv_ready"), sem("ln_ready"), sem("rstd_ready"))
        shift_ready, h_ready = sem("shift_ready"), sem("h_ready")
        weight_ready, inv_ready, attn_ready = sem("weight_ready"), sem("inv_ready"), sem("attn_ready")
        h1_ready, turned, h1T_ready, h1T_measured = (
            sem("h1_ready"), sem("turned"), sem("h1T_ready"), sem("h1T_measured"))
        held = sem("held")
        banks = k["bank"][0:2]

        with nc.Block() as block:
            @block.sync
            def _(sp):
                def load(s):
                    free = s.value(s.index - 1)
                    if not s.fresh:
                        sp.wait_ge(h_ready, free)
                    sp.dma_start(xg[0:s.rows, s.slot, 0:s.tiles, :], node_rows(x, s))\
                        .then_inc(x_landed[s.slot], 16)
                    if not s.fresh:
                        sp.wait_ge(attn_ready, free)
                    sp.dma_start(acc[0:s.rows, s.slot, 0:s.tiles, :], node_rows(k["table"], s))\
                        .then_inc(acc_landed[s.slot], 16)

                def store(s):
                    w = s.rows * s.tiles
                    sp.wait_ge(h1T_ready, s.done)
                    to = k["h1T"][s.index, :, 0:w] if s.tail else k["h1T"][bass.ds(s.index, 1), :, :]\
                        .rearrange("a p n -> p (a n)")
                    sp.dma_start(to, h1T[:, s.slot, 0:w]).then_inc(h1T_stored[s.slot], 16)

                walk(sp, NG, [(0, load), (2, store)], NODE_SIZES)
                sp.wait_ge(h1T_stored[0], 16 * ((NG + 2) // 2))
                sp.wait_ge(h1T_stored[1], 16 * ((NG + 1) // 2))

            @block.gpsimd
            def _(pool):
                def residual(s):
                    r, n = s.rows, s.tiles
                    pool.wait_ge(h_ready, s.done)
                    pool.wait_ge(attn_ready, s.done)
                    if not s.fresh:
                        pool.wait_ge(turned, s.value(s.index - 1))
                    pool.tensor_tensor(h1[0:r, s.slot, 0:n, :], h[0:r, s.slot, 0:n, :],
                                       attn[0:r, s.slot, 0:n, :], ALU.add).then_inc(h1_ready, 1)

                walk(pool, NG, [(0, residual)], NODE_SIZES)

            @block.vector
            def _(dve):
                def hold(*waits):
                    for sem_, value in waits:
                        dve.wait_ge(sem_, value)
                    dve.sem_inc(held, 1)

                def stats(s):
                    r, n = s.rows, s.tiles
                    landed = s.value(s.turn * 16 + 16)
                    free = s.value(s.index - 1)
                    dve.wait_ge(x_landed[s.slot], landed)
                    for j in range(n):
                        last = dve.bn_stats(stat[0:r, s.slot, j, :], xg[0:r, s.slot, j, :])
                    last.then_inc(stats_ready, 1)
                    dve.wait_ge(acc_landed[s.slot], landed)
                    dve.tensor_scalar(weight[0:r, s.slot, 0:n, :], acc[0:r, s.slot, 0:n, WCOL:WCOL + H],
                                      1e-6, None, ALU.add).then_inc(weight_ready, 1)
                    hold((stats_ready, s.done))
                    for j in range(n):
                        last = dve.bn_aggr(mv[0:r, s.slot, j, :], stat[0:r, s.slot, j, :])
                    last.then_inc(mv_ready, 1)
                    dve.wait_ge(weight_ready, s.done)
                    dve.reciprocal(weight_inv[0:r, s.slot, 0:n, :], weight[0:r, s.slot, 0:n, :])\
                        .then_inc(inv_ready, 1)
                    dve.tensor_copy(cols(k["in_deg"], s, 4), acc[0:r, s.slot, 0:n, CCOL])
                    dve.wait_ge(inv_ready, s.done)
                    if not s.fresh:
                        dve.wait_ge(h1_ready, free)
                    dve.tensor_tensor(
                        attn[0:r, s.slot, 0:n, :].rearrange("p t (h d) -> p t h d", h=H),
                        acc[0:r, s.slot, 0:n, 0:D].rearrange("p t (h d) -> p t h d", h=H),
                        weight_inv[0:r, s.slot, 0:n, :].unsqueeze(3).broadcast_to([r, n, H, DH]), ALU.mult)\
                        .then_inc(attn_ready, 1)
                    dve.wait_ge(rstd_ready, s.done)
                    dve.scalar_tensor_tensor(shift[0:r, s.slot, 0:n], mv[0:r, s.slot, 0:n, 0], -1.0,
                                             rstd[0:r, s.slot, 0:n], ALU.mult, ALU.mult)\
                        .then_inc(shift_ready, 1)

                def measure(s):
                    w = s.rows * s.tiles
                    dve.wait_ge(h1T_ready, s.done)
                    if s.tail:
                        dve.bn_stats(k["bn1"][:, s.index, :], h1T[:, s.slot, 0:w]).then_inc(h1T_measured, 1)
                    else:
                        dve.sem_inc(held, 1)
                        dve.bn_stats(k["bn1"][:, bass.ds(s.index, 1), :].rearrange("p a b -> p (a b)"),
                                     h1T[:, s.slot, 0:w]).then_inc(h1T_measured, 1)

                walk(dve, NG, [(0, stats), (1, measure)], NODE_SIZES)

            @block.scalar
            def _(act):
                def norm_scale(s):
                    r, n = s.rows, s.tiles
                    act.wait_ge(mv_ready, s.done)
                    act.activation(lnvar[0:r, s.slot, 0:n], mv[0:r, s.slot, 0:n, 1], ACT.Ln,
                                   bias=k["eps"][0:r, :]).then_inc(ln_ready, 1)
                    act.wait_ge(ln_ready, s.done)
                    act.activation(rstd[0:r, s.slot, 0:n], lnvar[0:r, s.slot, 0:n], ACT.Exp, scale=-0.5)\
                        .then_inc(rstd_ready, 1)

                def norm(s):
                    r, n = s.rows, s.tiles
                    act.wait_ge(shift_ready, s.done)
                    if not s.fresh:
                        act.wait_ge(h1_ready, s.value(s.index - 1))
                    for j in range(n):
                        last = act.activation(h[0:r, s.slot, j, :], xg[0:r, s.slot, j, :], ACT.Relu,
                                              bias=shift[0:r, s.slot, j:j + 1],
                                              scale=rstd[0:r, s.slot, j:j + 1])
                    last.then_inc(h_ready, 1)

                def evacuate(s):
                    w = s.rows * s.tiles
                    stored = s.value(s.turn * 16)
                    free = s.value(s.index - 1)
                    act.wait_ge(turned, s.done)
                    if not s.fresh:
                        act.wait_ge(h1T_stored[s.slot], stored)
                        act.wait_ge(h1T_measured, free)
                    act.activation(h1T[:, s.slot, 0:w], banks[s.slot][:, 0:w], ACT.Copy)\
                        .then_inc(h1T_ready, 1)

                walk(act, NG, [(0, norm_scale), (1, evacuate), (0, norm)], NODE_SIZES)

            @block.tensor
            def _(pe):
                def turn(s):
                    r = s.rows
                    pe.wait_ge(h1_ready, s.done)
                    if not s.fresh:
                        pe.wait_ge(h1T_ready, s.value(s.index - 1))
                    for j in range(s.tiles):
                        last = pe.transpose(banks[s.slot][:, j * r:(j + 1) * r], h1[0:r, s.slot, j, :],
                                            k["ident"][0:r, 0:r])
                    last.then_inc(turned, 1)

                walk(pe, NG, [(0, turn)], NODE_SIZES)


def bn_tiles(sb, sem):
    return ([sb("mean_var", [P, 2])] + [sb(n, [P, 1]) for n in ("bn_log", "std_inv", "bn_scale", "bn_shift")],
            [sem(n) for n in ("aggregated", "logged", "inverted", "bn_scaled", "bn_ready")])


def mlp_stage(nc, k):
    ctx = ExitStack()
    with ctx:
        def sb(name, shape, dt=FP32):
            return ctx.enter_context(nc.sbuf_tensor("c_" + name, shape, dt))

        def sem(name):
            return ctx.enter_context(nc.semaphore("c_" + name))

        tiles, sems = bn_tiles(sb, sem)
        h1T = sb("h1T", [P, 2, 512])
        y = sb("y", [P, 2, 512])
        hidden = sb("hidden", [P, 2, 2, 512])
        z = sb("z", [P, 2, 512])
        landed = [sem(f"landed{i}") for i in range(2)]
        stored = [sem(f"stored{i}") for i in range(2)]
        y_ready, up_ready, hid0_ready, hid1_ready = (
            sem("y_ready"), sem("up_ready"), sem("hid0_ready"), sem("hid1_ready"))
        down_ready, z_ready, z_measured, held = (
            sem("down_ready"), sem("z_ready"), sem("z_measured"), sem("held"))
        up = [k["bank"][0:2], k["bank"][2:4]]
        down = k["bank"][4:6]

        with nc.Block() as block:
            @block.sync
            def _(sp):
                def load(s):
                    w = s.rows * s.tiles
                    if not s.fresh:
                        sp.wait_ge(y_ready, s.value(s.index - 1))
                    of = k["h1T"][s.index, :, 0:w] if s.tail else k["h1T"][bass.ds(s.index, 1), :, :]\
                        .rearrange("a p n -> p (a n)")
                    sp.dma_start(h1T[:, s.slot, 0:w], of).then_inc(landed[s.slot], 16)

                def store(s):
                    w = s.rows * s.tiles
                    sp.wait_ge(z_ready, s.done)
                    to = k["zT"][s.index, :, 0:w] if s.tail else k["zT"][bass.ds(s.index, 1), :, :]\
                        .rearrange("a p n -> p (a n)")
                    sp.dma_start(to, z[:, s.slot, 0:w]).then_inc(stored[s.slot], 16)

                walk(sp, NG, [(0, load), (3, store)], NODE_SIZES)
                sp.wait_ge(stored[0], 16 * ((NG + 2) // 2))
                sp.wait_ge(stored[1], 16 * ((NG + 1) // 2))

            @block.scalar
            def _(act):
                norm_constants(k, act, None, k["bn1"], k["g1"], k["be1"], tiles, sems)[0]()
                act.wait_ge(sems[4], 1)

                def normed(s):
                    w = s.rows * s.tiles
                    act.wait_ge(landed[s.slot], s.value(s.turn * 16 + 16))
                    if not s.fresh:
                        act.wait_ge(z_ready, s.value(s.index - 1))
                    act.activation(y[:, s.slot, 0:w], h1T[:, s.slot, 0:w], ACT.Identity,
                                   bias=tiles[4][:, :], scale=tiles[3][:, :]).then_inc(y_ready, 1)

                def hidden_first(s):
                    w = s.rows * s.tiles
                    act.wait_ge(up_ready, s.done)
                    if not s.fresh:
                        act.wait_ge(down_ready, s.value(s.index - 1))
                    act.activation(hidden[:, s.slot, 0, 0:w], up[s.slot][0][:, 0:w], ACT.Relu,
                                   bias=k["b1"][:, 0:1]).then_inc(hid0_ready, 1)

                walk(act, NG, [(0, normed), (1, hidden_first)], NODE_SIZES)

            @block.vector
            def _(dve):
                norm_constants(k, None, dve, k["bn1"], k["g1"], k["be1"], tiles, sems)[1]()

                def hidden_second(s):
                    w = s.rows * s.tiles
                    dve.wait_ge(up_ready, s.done)
                    if not s.fresh:
                        dve.wait_ge(down_ready, s.value(s.index - 1))
                    dve.tensor_scalar(hidden[:, s.slot, 1, 0:w], up[s.slot][1][:, 0:w], k["b1"][:, 1:2],
                                      0.0, ALU.add, ALU.max).then_inc(hid1_ready, 1)

                def output(s):
                    w = s.rows * s.tiles
                    kept = s.value(s.turn * 16)
                    dve.wait_ge(down_ready, s.done)
                    if not s.fresh:
                        dve.wait_ge(stored[s.slot], kept)
                    dve.scalar_tensor_tensor(z[:, s.slot, 0:w], down[s.slot][:, 0:w], k["b2"][:, :],
                                             y[:, s.slot, 0:w], ALU.add, ALU.add).then_inc(z_ready, 1)
                    dve.wait_ge(z_ready, s.done)
                    if not s.tail:
                        dve.sem_inc(held, 1)
                    to = (k["bn2"][:, s.index, :] if s.tail else
                          k["bn2"][:, bass.ds(s.index, 1), :].rearrange("p a b -> p (a b)"))
                    dve.bn_stats(to, z[:, s.slot, 0:w]).then_inc(z_measured, 1)

                walk(dve, NG, [(1, hidden_second), (2, output)], NODE_SIZES)

            @block.tensor
            def _(pe):
                def expand(s):
                    w = s.rows * s.tiles
                    free = s.value(s.index - 1)
                    pe.wait_ge(y_ready, s.done)
                    if not s.fresh:
                        pe.wait_ge(hid0_ready, free)
                        pe.wait_ge(hid1_ready, free)
                    for c in range(2):
                        last = pe.matmul(up[s.slot][c][:, 0:w], k["W1"][:, c * D:(c + 1) * D],
                                         y[:, s.slot, 0:w], start=True, stop=True)
                    last.then_inc(up_ready, 1)

                def contract(s):
                    w = s.rows * s.tiles
                    pe.wait_ge(hid0_ready, s.done)
                    pe.wait_ge(hid1_ready, s.done)
                    if not s.fresh:
                        pe.wait_ge(z_ready, s.value(s.index - 1))
                    for c in range(2):
                        last = pe.matmul(down[s.slot][:, 0:w], k["W2"][:, c, :], hidden[:, s.slot, c, 0:w],
                                         start=c == 0, stop=c == 1)
                    last.then_inc(down_ready, 1)

                walk(pe, NG, [(0, expand), (1, contract)], NODE_SIZES)


def normed_stage(nc, k, x):
    ctx = ExitStack()
    with ctx:
        def sb(name, shape, dt=FP32):
            return ctx.enter_context(nc.sbuf_tensor("d_" + name, shape, dt))

        def sem(name):
            return ctx.enter_context(nc.semaphore("d_" + name))

        tiles, sems = bn_tiles(sb, sem)
        xg = sb("xg", [P, 2, 4, D])
        zT = sb("zT", [P, 2, 512])
        zn = sb("zn", [P, 2, 512])
        x2 = sb("x2", [P, 2, 4, D])
        g = sb("g", [P, 2, 4, D])
        stat = sb("stat", [P, 2, 4, 6])
        mv = sb("mv", [P, 2, 4, 2])
        lnvar = sb("lnvar", [P, 2, 4])
        rstd = sb("rstd", [P, 2, 4])
        gscale = sb("gscale", [P, 2, 4])
        gshift = sb("gshift", [P, 2, 4])
        x_landed = [sem(f"x_landed{i}") for i in range(2)]
        z_landed = [sem(f"z_landed{i}") for i in range(2)]
        x2_stored = [sem(f"x2_stored{i}") for i in range(2)]
        g_stored = [sem(f"g_stored{i}") for i in range(2)]
        deg_landed, deg_clipped, deg_logged, deg_ready = (
            sem("deg_landed"), sem("deg_clipped"), sem("deg_logged"), sem("deg_ready"))
        zn_ready, turned, x2_ready, stats_ready, mv_ready = (
            sem("zn_ready"), sem("turned"), sem("x2_ready"), sem("stats_ready"), sem("mv_ready"))
        ln_ready, rstd_ready, shift_ready, gshift_ready, g_ready, held = (
            sem("ln_ready"), sem("rstd_ready"), sem("shift_ready"), sem("gshift_ready"), sem("g_ready"),
            sem("held"))
        banks = k["bank"][0:2]
        out_deg, in_deg = k["out_deg"], k["in_deg"]
        deg_parts = [(t, slice(0, r), slice(c0, c1)) for t in (out_deg, in_deg)
                     for r, c0, c1 in ((P, 0, NT), (NR, NT, NC))]

        with nc.Block() as block:
            @block.sync
            def _(sp):
                flat = k["degree"].rearrange("a p -> (a p)")
                sp.dma_start(out_deg[:, 0:NT], flat[0:P * NT].rearrange("(p t) -> p t", p=P))\
                    .then_inc(deg_landed, 16)
                sp.dma_start(out_deg[0:NR, NT:NC], flat[P * NT:N].rearrange("(p t) -> p t", p=NR))\
                    .then_inc(deg_landed, 16)

                def load(s):
                    w = s.rows * s.tiles
                    free = s.value(s.index - 1)
                    if not s.fresh:
                        sp.wait_ge(zn_ready, free)
                    of = k["zT"][s.index, :, 0:w] if s.tail else k["zT"][bass.ds(s.index, 1), :, :]\
                        .rearrange("a p n -> p (a n)")
                    sp.dma_start(zT[:, s.slot, 0:w], of).then_inc(z_landed[s.slot], 16)
                    if not s.fresh:
                        sp.wait_ge(x2_ready, free)
                    sp.dma_start(xg[0:s.rows, s.slot, 0:s.tiles, :], node_rows(x, s))\
                        .then_inc(x_landed[s.slot], 16)

                def store(s):
                    sp.wait_ge(x2_ready, s.done)
                    sp.dma_start(node_rows(k["x2"], s), x2[0:s.rows, s.slot, 0:s.tiles, :])\
                        .then_inc(x2_stored[s.slot], 16)
                    sp.wait_ge(g_ready, s.done)
                    sp.dma_start(node_rows(k["g"], s), g[0:s.rows, s.slot, 0:s.tiles, :])\
                        .then_inc(g_stored[s.slot], 16)

                walk(sp, NG, [(0, load), (2, store)], NODE_SIZES)
                for t in (x2_stored, g_stored):
                    sp.wait_ge(t[0], 16 * ((NG + 2) // 2))
                    sp.wait_ge(t[1], 16 * ((NG + 1) // 2))

            @block.scalar
            def _(act):
                norm_constants(k, act, None, k["bn2"], k["g2"], k["be2"], tiles, sems)[0]()
                act.wait_ge(deg_clipped, 4)
                for t, rs, cs in deg_parts:
                    act.activation(t[rs, cs], t[rs, cs], ACT.Ln).then_inc(deg_logged, 1)
                act.wait_ge(deg_logged, 4)
                for t, rs, cs in deg_parts:
                    act.activation(t[rs, cs], t[rs, cs], ACT.Exp, scale=-0.5).then_inc(deg_ready, 1)
                act.wait_ge(sems[4], 1)

                def normed(s):
                    w = s.rows * s.tiles
                    landed = s.value(s.turn * 16 + 16)
                    act.wait_ge(z_landed[s.slot], landed)
                    if not s.fresh:
                        act.wait_ge(turned, s.value(s.index - 1))
                    act.activation(zn[:, s.slot, 0:w], zT[:, s.slot, 0:w], ACT.Identity,
                                   bias=tiles[4][:, :], scale=tiles[3][:, :]).then_inc(zn_ready, 1)

                def norm_scale(s):
                    r, n = s.rows, s.tiles
                    act.wait_ge(mv_ready, s.done)
                    act.activation(lnvar[0:r, s.slot, 0:n], mv[0:r, s.slot, 0:n, 1], ACT.Ln,
                                   bias=k["eps"][0:r, :]).then_inc(ln_ready, 1)
                    act.wait_ge(ln_ready, s.done)
                    act.activation(rstd[0:r, s.slot, 0:n], lnvar[0:r, s.slot, 0:n], ACT.Exp, scale=-0.5)\
                        .then_inc(rstd_ready, 1)

                def scaled_rows(s):
                    r, n = s.rows, s.tiles
                    act.wait_ge(gshift_ready, s.done)
                    if not s.fresh:
                        act.wait_ge(g_stored[s.slot], s.value(s.turn * 16))
                    for j in range(n):
                        last = act.activation(g[0:r, s.slot, j, :], x2[0:r, s.slot, j, :], ACT.Relu,
                                              bias=gshift[0:r, s.slot, j:j + 1],
                                              scale=gscale[0:r, s.slot, j:j + 1])
                    last.then_inc(g_ready, 1)

                walk(act, NG, [(0, normed), (1, norm_scale), (1, scaled_rows)], NODE_SIZES)

            @block.vector
            def _(dve):
                norm_constants(k, None, dve, k["bn2"], k["g2"], k["be2"], tiles, sems)[1]()
                dve.wait_ge(deg_landed, 32)
                for t, rs, cs in deg_parts:
                    dve.tensor_scalar(t[rs, cs], t[rs, cs], 1.0, None, ALU.max).then_inc(deg_clipped, 1)
                dve.wait_ge(deg_ready, 4)

                def residual(s):
                    r, n = s.rows, s.tiles
                    landed, kept = s.value(s.turn * 16 + 16), s.value(s.turn * 16)
                    free = s.value(s.index - 1)
                    dve.wait_ge(x_landed[s.slot], landed)
                    dve.wait_ge(turned, s.done)
                    if not s.fresh:
                        dve.wait_ge(x2_stored[s.slot], kept)
                        dve.wait_ge(g_ready, free)
                    dve.tensor_tensor(x2[0:r, s.slot, 0:n, :],
                                      banks[s.slot][0:r, 0:n * D].rearrange("p (t f) -> p t f", t=n),
                                      xg[0:r, s.slot, 0:n, :], ALU.add).then_inc(x2_ready, 1)
                    dve.wait_ge(x2_ready, s.done)
                    for j in range(n):
                        last = dve.bn_stats(stat[0:r, s.slot, j, :], x2[0:r, s.slot, j, :])
                    last.then_inc(stats_ready, 1)
                    dve.wait_ge(stats_ready, s.done)
                    dve.sem_inc(held, 1)
                    for j in range(n):
                        last = dve.bn_aggr(mv[0:r, s.slot, j, :], stat[0:r, s.slot, j, :])
                    last.then_inc(mv_ready, 1)

                def constants(s):
                    r, n = s.rows, s.tiles
                    dve.wait_ge(rstd_ready, s.done)
                    dve.scalar_tensor_tensor(cols(k["shift2"], s, 4), mv[0:r, s.slot, 0:n, 0], -1.0,
                                             rstd[0:r, s.slot, 0:n], ALU.mult, ALU.mult)\
                        .then_inc(shift_ready, 1)
                    dve.tensor_tensor(gscale[0:r, s.slot, 0:n], rstd[0:r, s.slot, 0:n], cols(out_deg, s, 4),
                                      ALU.mult)
                    dve.tensor_copy(cols(k["scale2"], s, 4), rstd[0:r, s.slot, 0:n])
                    dve.wait_ge(shift_ready, s.done)
                    dve.tensor_tensor(gshift[0:r, s.slot, 0:n], cols(k["shift2"], s, 4), cols(out_deg, s, 4),
                                      ALU.mult).then_inc(gshift_ready, 1)

                walk(dve, NG, [(0, residual), (1, constants)], NODE_SIZES)

            @block.tensor
            def _(pe):
                def turn(s):
                    r = s.rows
                    pe.wait_ge(zn_ready, s.done)
                    if not s.fresh:
                        pe.wait_ge(x2_ready, s.value(s.index - 1))
                    for j in range(s.tiles):
                        last = pe.transpose(banks[s.slot][0:r, j * D:(j + 1) * D],
                                            zn[:, s.slot, j * r:(j + 1) * r], k["ident"][:, :])
                    last.then_inc(turned, 1)

                walk(pe, NG, [(0, turn)], NODE_SIZES)


def convolution_stage(nc, k):
    ctx = ExitStack()
    with ctx:
        def sb(name, shape, dt=FP32):
            return ctx.enter_context(nc.sbuf_tensor("e_" + name, shape, dt))

        def sem(name):
            return ctx.enter_context(nc.semaphore("e_" + name))

        index = sb("index", [P, 2, 2], I32)
        add_at = sb("add_at", [P, 2, 2], I32)
        dst_now = sb("dst_now", [P, 2, 2])
        g = sb("g", [P, 2, 2, D])
        same = sb("same", [P, 2, 2, P])
        group = sb("group", [P, 2, 2, D])
        landed = [sem(f"landed{i}") for i in range(2)]
        rows_added = [sem(f"rows_added{i}") for i in range(2)]
        index_ready, target_ready, dst_turned, same_ready, grouped, group_ready, held = (
            sem("index_ready"), sem("target_ready"), sem("dst_turned"), sem("same_ready"), sem("grouped"),
            sem("group_ready"), sem("held"))
        bank_dst, bank_grp = k["bank"][0:2], k["bank"][2:4]
        dst_f, ends, target, ident = k["dst_f"], k["ends"], k["target"], k["ident"]

        with nc.Block() as block:
            @block.gpsimd
            def _(pool):
                def hold(*waits):
                    for sem_, value in waits:
                        pool.wait_ge(sem_, value)
                    pool.sem_inc(held, 1)

                def gather(s):
                    free = s.value(s.index - 1)
                    waits = [(index_ready, s.done)]
                    if not s.fresh:
                        waits.append((grouped, free))
                    hold(*waits)
                    for j in range(s.tiles):
                        pool.indirect_dma_start(
                            g[0:s.rows, s.slot, j, :], None, k["g"],
                            bass.IndirectOffsetOnAxis(index[0:s.rows, s.slot, j:j + 1], 0))\
                            .then_inc(landed[s.slot], 16)

                def add(s):
                    last = s.value(s.index * 16)
                    for j in range(s.tiles):
                        waits = [(group_ready, s.done), (target_ready, s.done)]
                        if not s.first:
                            waits.append((rows_added[j], last))
                        hold(*waits)
                        pool.indirect_dma_start(
                            k["sums"][j], bass.IndirectOffsetOnAxis(add_at[0:s.rows, s.slot, j:j + 1], 0),
                            group[0:s.rows, s.slot, j, :], None, compute_op=ALU.add)\
                            .then_inc(rows_added[j], 16)

                walk(pool, EU, [(0, gather), (2, add)], EDGE_SIZES)
                pool.wait_ge(rows_added[0], 16 * (EU + 1))
                pool.wait_ge(rows_added[1], 16 * EU)

            @block.vector
            def _(dve):
                def make_index(s):
                    read, free = s.value(s.turn * 32), s.value(s.index - 1)
                    if not s.fresh:
                        dve.wait_ge(dst_turned, free)
                        dve.wait_ge(landed[s.slot], read)
                        dve.sem_inc(held, 1)
                    dve.tensor_copy(dst_now[0:s.rows, s.slot, 0:s.tiles], cols(dst_f, s, 2))
                    t0, n = s.index * 2, s.tiles
                    part = ends[0:s.rows, t0:t0 + n, 0] if s.tail else ends[:, bass.ds(t0, 2), 0]
                    dve.tensor_copy(index[0:s.rows, s.slot, 0:n], part).then_inc(index_ready, 1)

                def compare(s):
                    r, n = s.rows, s.tiles
                    free = s.value(s.index - 1)
                    dve.wait_ge(dst_turned, s.done)
                    if not s.fresh:
                        dve.wait_ge(grouped, free)
                    dve.tensor_tensor(same[0:r, s.slot, 0:n, 0:r],
                                      bank_dst[s.slot][0:r, 0:n * P].rearrange("p (t e) -> p t e", t=n)[:, :, 0:r],
                                      spread(cols(dst_f, s, 2), r), ALU.is_equal).then_inc(same_ready, 1)

                def targets(s):
                    n = s.tiles
                    added = s.value(s.index * 16 - 16)
                    if not s.fresh:
                        dve.wait_ge(rows_added[0], added)
                        dve.wait_ge(rows_added[1], added)
                        dve.sem_inc(held, 1)
                    t0 = s.index * 2
                    part = target[0:s.rows, t0:t0 + n] if s.tail else target[:, bass.ds(t0, 2)]
                    dve.tensor_copy(add_at[0:s.rows, s.slot, 0:n], part).then_inc(target_ready, 1)

                walk(dve, EU, [(0, make_index), (2, compare), (3, targets)], EDGE_SIZES)

            @block.scalar
            def _(act):
                def evacuate(s):
                    r, n = s.rows, s.tiles
                    added = s.value(s.index * 16 - 16)
                    act.wait_ge(grouped, s.done)
                    if not s.fresh:
                        act.wait_ge(rows_added[0], added)
                        act.wait_ge(rows_added[1], added)
                    act.activation(group[0:r, s.slot, 0:n, :],
                                   bank_grp[s.slot][0:r, 0:n * D].rearrange("p (t f) -> p t f", t=n),
                                   ACT.Copy).then_inc(group_ready, 1)

                walk(act, EU, [(0, evacuate)], EDGE_SIZES)

            @block.tensor
            def _(pe):
                def turn(s):
                    r = s.rows
                    free = s.value(s.index - 1)
                    pe.wait_ge(index_ready, s.done)
                    if not s.fresh:
                        pe.wait_ge(same_ready, free)
                    for j in range(s.tiles):
                        last = pe.transpose(bank_dst[s.slot][0:P, j * P:j * P + r],
                                            dst_now[0:r, s.slot, j:j + 1].broadcast_to([r, P]),
                                            ident[0:r, 0:r])
                    last.then_inc(dst_turned, 1)

                def group_up(s):
                    r = s.rows
                    full = s.value(s.turn * 32 + (16 if s.tail else 32))
                    free = s.value(s.index - 1)
                    pe.wait_ge(landed[s.slot], full)
                    pe.wait_ge(same_ready, s.done)
                    if not s.fresh:
                        pe.wait_ge(group_ready, free)
                    for j in range(s.tiles):
                        last = pe.matmul(bank_grp[s.slot][0:r, j * D:(j + 1) * D],
                                         same[0:r, s.slot, j, 0:r], g[0:r, s.slot, j, :],
                                         start=True, stop=True)
                    last.then_inc(grouped, 1)

                walk(pe, EU, [(0, turn), (1, group_up)], EDGE_SIZES)


def output_stage(nc, k, out):
    ctx = ExitStack()
    with ctx:
        def sb(name, shape, dt=FP32):
            return ctx.enter_context(nc.sbuf_tensor("f_" + name, shape, dt))

        def sem(name):
            return ctx.enter_context(nc.semaphore("f_" + name))

        x2 = sb("x2", [P, 2, 4, D])
        sums = [sb(f"sums{i}", [P, 2, 4, D]) for i in range(2)]
        h = sb("h", [P, 2, 4, D])
        total = sb("total", [P, 2, 4, D])
        hs = sb("hs", [P, 2, 4, D])
        both = sb("both", [P, 2, 2, 4, D])
        bothT = sb("bothT", [P, 2, 2, 512])
        res = sb("res", [P, 2, 4, D])
        x_landed = [sem(f"x_landed{i}") for i in range(2)]
        sums_landed = [sem(f"sums_landed{i}") for i in range(2)]
        stored = [sem(f"stored{i}") for i in range(2)]
        h_ready, total_ready, hs_ready, plus_ready, times_ready = (
            sem("h_ready"), sem("total_ready"), sem("hs_ready"), sem("plus_ready"), sem("times_ready"))
        plus_turned, times_turned, plusT_ready, timesT_ready, product_ready, res_ready, held = (
            sem("plus_turned"), sem("times_turned"), sem("plusT_ready"), sem("timesT_ready"),
            sem("product_ready"), sem("res_ready"), sem("held"))
        bank_plus, bank_times, bank_out = k["bank"][0:2], k["bank"][2:4], k["bank"][4:6]

        with nc.Block() as block:
            @block.sync
            def _(sp):
                def load(s):
                    free = s.value(s.index - 1)
                    if not s.fresh:
                        sp.wait_ge(total_ready, free)
                    for i in range(2):
                        sp.dma_start(sums[i][0:s.rows, s.slot, 0:s.tiles, :], node_rows(k["sums"][i], s))\
                            .then_inc(sums_landed[s.slot], 16)
                    if not s.fresh:
                        sp.wait_ge(res_ready, free)
                    sp.dma_start(x2[0:s.rows, s.slot, 0:s.tiles, :], node_rows(k["x2"], s))\
                        .then_inc(x_landed[s.slot], 16)

                def store(s):
                    sp.wait_ge(res_ready, s.done)
                    sp.dma_start(node_rows(out, s), res[0:s.rows, s.slot, 0:s.tiles, :])\
                        .then_inc(stored[s.slot], 16)

                walk(sp, NG, [(0, load), (2, store)], NODE_SIZES)
                sp.wait_ge(stored[0], 16 * ((NG + 2) // 2))
                sp.wait_ge(stored[1], 16 * ((NG + 1) // 2))

            @block.gpsimd
            def _(pool):
                def add_tables(s):
                    r, n = s.rows, s.tiles
                    full = s.value(s.turn * 32 + 32)
                    free = s.value(s.index - 1)
                    pool.wait_ge(sums_landed[s.slot], full)
                    if not s.fresh:
                        pool.wait_ge(hs_ready, free)
                    pool.tensor_tensor(total[0:r, s.slot, 0:n, :], sums[0][0:r, s.slot, 0:n, :],
                                       sums[1][0:r, s.slot, 0:n, :], ALU.add).then_inc(total_ready, 1)

                def plus(s):
                    r, n = s.rows, s.tiles
                    free = s.value(s.index - 1)
                    pool.wait_ge(hs_ready, s.done)
                    pool.wait_ge(h_ready, s.done)
                    if not s.fresh:
                        pool.wait_ge(plus_turned, free)
                    pool.tensor_tensor(both[0:r, s.slot, 0, 0:n, :], hs[0:r, s.slot, 0:n, :],
                                       h[0:r, s.slot, 0:n, :], ALU.add).then_inc(plus_ready, 1)

                walk(pool, NG, [(0, add_tables), (1, plus)], NODE_SIZES)

            @block.scalar
            def _(act):
                def norm(s):
                    r, n = s.rows, s.tiles
                    landed = s.value(s.turn * 16 + 16)
                    free = s.value(s.index - 1)
                    act.wait_ge(x_landed[s.slot], landed)
                    if not s.fresh:
                        act.wait_ge(plus_ready, free)
                        act.wait_ge(times_ready, free)
                    act.sem_inc(held, 1)
                    for j in range(n):
                        t = s.index * 4 + j
                        sc, sh = (v[0:r, t:t + 1] if s.tail else v[0:r, bass.ds(t, 1)]
                                  for v in (k["scale2"], k["shift2"]))
                        last = act.activation(h[0:r, s.slot, j, :], x2[0:r, s.slot, j, :], ACT.Relu,
                                              bias=sh, scale=sc)
                    last.then_inc(h_ready, 1)

                def evacuate(s):
                    w = s.rows * s.tiles
                    free = s.value(s.index - 1)
                    for c, (bank, turned, ready) in enumerate(((bank_plus, plus_turned, plusT_ready),
                                                               (bank_times, times_turned, timesT_ready))):
                        act.wait_ge(turned, s.done)
                        if not s.fresh and c == 0:
                            act.wait_ge(product_ready, free)
                        act.activation(bothT[:, s.slot, c, 0:w], bank[s.slot][:, 0:w], ACT.Copy)\
                            .then_inc(ready, 1)

                walk(act, NG, [(0, norm), (1, evacuate)], NODE_SIZES)

            @block.vector
            def _(dve):
                def scale_sums(s):
                    r, n = s.rows, s.tiles
                    free = s.value(s.index - 1)
                    dve.wait_ge(total_ready, s.done)
                    if not s.fresh:
                        dve.wait_ge(plus_ready, free)
                    dve.tensor_tensor(hs[0:r, s.slot, 0:n, :], total[0:r, s.slot, 0:n, :],
                                      spread(cols(k["in_deg"], s, 4), D), ALU.mult).then_inc(hs_ready, 1)
                    dve.wait_ge(h_ready, s.done)
                    dve.wait_ge(hs_ready, s.done)
                    if not s.fresh:
                        dve.wait_ge(times_turned, free)
                    dve.tensor_tensor(both[0:r, s.slot, 1, 0:n, :], hs[0:r, s.slot, 0:n, :],
                                      h[0:r, s.slot, 0:n, :], ALU.mult).then_inc(times_ready, 1)

                def result(s):
                    r, n = s.rows, s.tiles
                    kept = s.value(s.turn * 16)
                    dve.wait_ge(product_ready, s.done)
                    if not s.fresh:
                        dve.wait_ge(stored[s.slot], kept)
                    dve.tensor_tensor(res[0:r, s.slot, 0:n, :],
                                      bank_out[s.slot][0:r, 0:n * D].rearrange("p (t f) -> p t f", t=n),
                                      x2[0:r, s.slot, 0:n, :], ALU.add).then_inc(res_ready, 1)

                walk(dve, NG, [(2, result), (0, scale_sums)], NODE_SIZES)

            @block.tensor
            def _(pe):
                def turn(s):
                    r = s.rows
                    free = s.value(s.index - 1)
                    for c, (bank, ready, turned, read) in enumerate((
                            (bank_times, times_ready, times_turned, timesT_ready),
                            (bank_plus, plus_ready, plus_turned, plusT_ready))):
                        pe.wait_ge(ready, s.done)
                        if not s.fresh:
                            pe.wait_ge(read, free)
                        for j in range(s.tiles):
                            last = pe.transpose(bank[s.slot][:, j * r:(j + 1) * r],
                                                both[0:r, s.slot, 1 - c, j, :], k["ident"][0:r, 0:r])
                        last.then_inc(turned, 1)

                def product(s):
                    r = s.rows
                    free = s.value(s.index - 1)
                    pe.wait_ge(plusT_ready, s.done)
                    pe.wait_ge(timesT_ready, s.done)
                    if not s.fresh:
                        pe.wait_ge(res_ready, free)
                    for j in range(s.tiles):
                        o = bank_out[s.slot][0:r, j * D:(j + 1) * D]
                        pe.matmul(o, bothT[:, s.slot, 0, j * r:(j + 1) * r], k["Ws"][:, :], start=True,
                                  stop=False)
                        last = pe.matmul(o, bothT[:, s.slot, 1, j * r:(j + 1) * r], k["Wi"][:, :],
                                         start=False, stop=True)
                    last.then_inc(product_ready, 1)

                walk(pe, NG, [(0, turn), (1, product)], NODE_SIZES)


_INS = ["x", "src", "dst", "edge_attr_128", "L0_gnn_Wq", "L0_gnn_Wk", "L0_gnn_We", "L0_gnn_Wv",
        "L0_gnn_bn1_g", "L0_gnn_bn1_b", "L0_gnn_W1", "L0_gnn_b1", "L0_gnn_W2", "L0_gnn_b2",
        "L0_gnn_bn2_g", "L0_gnn_bn2_b", "L1_gnn_W_self", "L1_gnn_W_inter"]


def kernel(**inputs):
    import numpy as _np
    import concourse.bacc as _bacc
    from concourse import mybir as _mybir
    from concourse.bass_utils import run_bass_kernel_spmd as _run

    nc = _bacc.Bacc("TRN2", target_bir_lowering=False, num_devices=1)
    arrays, args = {}, []
    for name in _INS:
        a = _np.ascontiguousarray(inputs[name])
        arrays[f"in_{name}_dram"] = a
        args.append(nc.dram_tensor(f"in_{name}_dram", a.shape, _mybir.dt.from_np(a.dtype), kind="ExternalInput").ap())
    args.append(nc.dram_tensor("out_0_dram", (N, D), FP32, kind="ExternalOutput").ap())
    build(nc, *args)
    r = _run(nc, [arrays], core_ids=[0])
    return r.results[0]["out_0_dram"]
```

```python
import concourse.bass as bass
from concourse import mybir
from contextlib import ExitStack

FP32 = mybir.dt.float32
FP16 = mybir.dt.float16
I32 = mybir.dt.int32
ALU = mybir.AluOpType
ACT = mybir.ActivationFunctionType
AX = mybir.AxisListType

P = 128
N = 50000
D = 128
H, DH = 8, 16
EPS = 1e-5

ET = N // P
ER = N - ET * P
EU = ET // 2
NG = 97
NT = 4 * NG
NR, NRC = 112, 3
assert P * NT + NR * NRC == N and EU * 2 == ET
NC = NT + NRC
RING = 4
OUT_RING = 6

HI = ET + 2

ROW = 144
WCOL, CCOL = D, D + H
USED = D + H + 1
TROWS = N + P


class Step:

    def __init__(self, eng, index, turn, slot, bank, tail, sizes):
        self.eng, self.index, self.turn, self.slot, self.tail = eng, index, turn, slot, tail
        self.rows, self.tiles = sizes[1] if tail else sizes[0]
        self.width = self.rows * self.tiles
        self.bank = bank
        self.first = isinstance(index, int) and index == 0
        self.done = self.value(index + 1)

    def value(self, x):
        return x if isinstance(x, int) else self.eng.snap(x)

    def had(self, n):
        return not isinstance(self.index, int) or self.index >= n

    def ago(self, n):
        return self.value(self.index + (1 - n)) if self.had(n) else None

    def landed(self, n=1):
        return self.value(self.turn * (16 * n) + 16 * n)

    def landed_before(self, n=1):
        return self.value(self.turn * (16 * n))


def walk(eng, units, ring, stages, sizes):
    most = max(lag for lag, _ in stages)
    first = most + ring
    first += (units - first) % (ring if ring % 2 == 0 else 2 * ring)

    def full(u):
        for lag, fn in stages:
            at = u - lag
            if 0 <= at <= units:
                fn(Step(eng, at, at // ring, at % ring, at % 2, at == units, sizes))

    for u in range(first):
        full(u)
    lap = ring if ring % 2 == 0 else 2 * ring
    with eng.Fori(0, (units - first) // lap) as i:
        for part in range(lap):
            for lag, fn in stages:
                at = first + part - lag
                fn(Step(eng, i * lap + at, i * (lap // ring) + at // ring, at % ring, at % 2, False, sizes))
    for u in range(units, units + most + 1):
        full(u)


EDGE_SIZES = ((P, 2), (ER, 1))
NODE_SIZES = ((P, 4), (NR, NRC))


def edge_rows(t, s):
    if s.tail:
        return t[P * ET:N, :].rearrange("(p t) d -> p t d", t=1)
    return t[0:P * ET, :].rearrange("(p t) d -> p t d", p=P)[:, bass.ds(s.index * 2, 2), :]


def node_rows(t, s):
    if s.tail:
        return t[P * NT:N, :].rearrange("(p t) d -> p t d", p=NR)
    return t[0:P * NT, :].rearrange("(p t) d -> p t d", p=P)[:, bass.ds(s.index * 4, 4), :]


def cols(t, s, width):
    if s.tail:
        return t[0:s.rows, width * s.index:width * s.index + s.tiles]
    return t[:, bass.ds(s.index * width, width)]


def group_rows(t, s):
    return t[s.index, :, 0:s.width] if s.tail else t[bass.ds(s.index, 1), :, :].rearrange("a p n -> p (a n)")


def stat_cols(t, s):
    return t[:, s.index, :] if s.tail else t[:, bass.ds(s.index, 1), :].rearrange("p a b -> p (a b)")


def wait_stored(eng, sems):
    for i, s in enumerate(sems):
        eng.wait_ge(s, 16 * len(range(i, NG + 1, len(sems))))


def stage_semaphore(nc, ctx, name):
    sem = nc.alloc_semaphore(name)
    ctx.sems.append(sem)
    return sem


class Stage(ExitStack):

    def __init__(self, nc):
        super().__init__()
        self.nc, self.sems = nc, []

    def __exit__(self, *e):
        self.nc.clear_and_free_semaphores(self.sems)
        self.nc.all_engine_barrier()
        return super().__exit__(*e)


def spread(ap, n):
    a, b = ap.shape
    return ap.unsqueeze(2).broadcast_to([a, b, n])


def build(nc, x, src, dst, edge_attr, Wq, Wk, We, Wv, bn1_g, bn1_b, W1, b1, W2, b2, bn2_g, bn2_b,
          W_self, W_inter, out):
    ctx = ExitStack()
    with ctx:
        def sb(name, shape, dt=FP32):
            return ctx.enter_context(nc.sbuf_tensor(name, shape, dt))

        def dram(name, shape):
            return nc.dram_tensor(name, shape, FP32, kind="Internal").ap()

        k = {}
        k["bank"] = [ctx.enter_context(nc.psum_tensor(f"bank{i}", [P, 512], FP32)) for i in range(8)]
        k["table"] = dram("table", (TROWS, ROW))
        k["sums"] = [dram(f"sums{i}", (TROWS, D)) for i in range(2)]
        k["h1T"] = dram("h1T", (NG + 1, P, 512))
        k["zT"] = dram("zT", (NG + 1, P, 512))
        k["x2"] = dram("x2", (N, D))
        k["g"] = dram("g", (N, D))
        k["degree"] = dram("degree", (ET + 1, P))

        k["ident"] = sb("ident", [P, P])
        k["Wkv"] = sb("Wkv", [P, 2 * D])
        k["Wq"] = sb("Wq", [P, D])
        k["We"] = sb("We", [P, D])
        k["W1"] = sb("W1", [P, 2 * D])
        k["W2"] = sb("W2", [P, 2, D])
        k["Ws"] = sb("Ws", [P, D])
        k["Wi"] = sb("Wi", [P, D])
        k["b1"] = sb("b1", [P, 2])
        for name in ("b2", "g1", "be1", "g2", "be2", "eps"):
            k[name] = sb(name, [P, 1])
        k["dst_f"] = sb("dst_f", [P, ET + 1])
        k["ends"] = sb("ends", [P, ET + 1, 2], I32)
        k["target"] = sb("target", [P, ET + 1], I32)
        k["in_deg"] = sb("in_deg", [P, NC])
        k["out_deg"] = sb("out_deg", [P, NC])
        k["scale2"] = sb("scale2", [P, NC])
        k["shift2"] = sb("shift2", [P, NC])
        k["bn1"] = sb("bn1", [P, NG + 1, 6])
        k["bn2"] = sb("bn2", [P, NG + 1, 6])

        edge_stages(nc, k, x, src, dst, edge_attr, Wq, Wk, We, Wv, bn1_g, bn1_b, W1, b1, W2, b2, bn2_g,
                    bn2_b, W_self, W_inter)
        residual_stage(nc, k, x)
        mlp_stage(nc, k)
        normed_stage(nc, k, x)
        convolution_stage(nc, k)
        output_stage(nc, k, out)


def edge_stages(nc, k, x, src, dst, edge_attr, Wq, Wk, We, Wv, bn1_g, bn1_b, W1, b1, W2, b2, bn2_g,
                bn2_b, W_self, W_inter):
    ctx = Stage(nc)
    with ctx:
        def sb(name, shape, dt=FP32):
            return ctx.enter_context(nc.sbuf_tensor(name, shape, dt))

        def sem(name):
            return stage_semaphore(nc, ctx, name)

        table, ident, dst_f, ends, target = k["table"], k["ident"], k["dst_f"], k["ends"], k["target"]
        src_i = sb("src_i", [P, ET + 1], I32)
        dst_i = sb("dst_i", [P, ET + 1], I32)
        bits = sb("bits", [P, ET + 1], I32)
        src_lo = sb("src_lo", [P, ET + 1])
        src_hi = sb("src_hi", [P, ET + 1])
        spare = sb("spare", [P, ET + 1])
        spare_row = sb("spare_row", [P, 1])
        count_i = sb("count_i", [P, HI], I32)
        count_h = sb("count_h", [P, HI], FP16)
        prow_i = sb("prow_i", [P, 1], I32)
        before = sb("before", [P, P])
        ones = sb("ones", [P, P])
        zero_cols = 2169
        zeros = sb("zeros", [P, zero_cols])

        index = sb("index", [P, 2, 2, 2], I32)
        rows_in = sb("rows_in", [P, 2, 2, 2, D])
        attr = sb("attr", [P, 2, 2, D])
        stat = sb("stat", [P, 2, 4, 6])
        mv = sb("mv", [P, 2, 4, 2])
        negmean = sb("negmean", [P, 2, 4])
        lnvar = sb("lnvar", [P, 2, 4])
        rstd = sb("rstd", [P, 2, 4])
        rr = sb("rr", [P, 2, 2])
        dst_now = sb("dst_now", [P, 2, 2])
        h = sb("h", [P, 2, 4, D])
        hT = sb("hT", [P, 2, 4, P])
        attrT = sb("attrT", [P, 2, 2, P])
        q = sb("q", [P, 2, 2, D])
        kq = sb("kq", [P, 2, D])
        kqe = sb("kqe", [P, 2, D])
        raw = sb("raw", [P, 2, H])
        scaled = sb("scaled", [P, 2, H])
        clipped = sb("clipped", [P, 2, H])
        wr = sb("wr", [P, 2, H])
        message = sb("message", [P, 2, 2, ROW])
        same = sb("same", [P, 2, 2, P])
        earlier = sb("earlier", [P, 2, P])
        rank = sb("rank", [P, 2])
        move = sb("move", [P, 2])
        hot_lo = sb("hot_lo", [P, 2, 2, P], FP16)
        lo_now = sb("lo_now", [P, 2, 2])
        hot_hi = sb("hot_hi", [P, 2, 2, HI], FP16)
        group = sb("group", [P, 2, 2, ROW])
        add_at = sb("add_at", [P, 2, 2], I32)
        hist = sb("hist", [P, HI])
        histT = sb("histT", [P, 4, P])

        loaded, cleared, const_ready = sem("loaded"), sem("cleared"), sem("const_ready")
        prep, zeros_ready = sem("prep"), sem("zeros_ready")
        index_ready = sem("index_ready")
        landed = [sem(f"landed{i}") for i in range(2)]
        attr_landed = [sem(f"attr_landed{i}") for i in range(2)]
        stats_ready, mv_ready, negmean_ready = sem("stats_ready"), sem("mv_ready"), sem("negmean_ready")
        ln_ready, rstd_ready, h_ready = sem("ln_ready"), sem("rstd_ready"), sem("h_ready")
        turned, attr_turned, dst_turned = sem("turned"), sem("attr_turned"), sem("dst_turned")
        hT_ready, attrT_ready = sem("hT_ready"), sem("attrT_ready")
        same_ready, rank_ready = sem("same_ready"), sem("rank_ready")
        move_ready, target_ready = sem("move_ready"), sem("target_ready")
        hot_ready, lo_now_ready, low_ready, counted = (
            sem("hot_ready"), sem("lo_now_ready"), sem("low_ready"), sem("counted"))
        products_ready, q_ready = sem("products_ready"), sem("q_ready")
        kq_ready, kqe_ready, raw_ready = sem("kq_ready"), sem("kqe_ready"), sem("raw_ready")
        rr_ready, scaled_ready, clipped_ready = sem("rr_ready"), sem("scaled_ready"), sem("clipped_ready")
        weight_ready, wr_ready, message_ready = sem("weight_ready"), sem("wr_ready"), sem("message_ready")
        grouped, group_ready = sem("grouped"), sem("group_ready")
        rows_added, held = sem("rows_added"), sem("held")
        sums_cleared = sem("sums_cleared")
        hist_ready, hist_turned, histT_ready, degree_stored = (
            sem("hist_ready"), sem("hist_turned"), sem("histT_ready"), sem("degree_stored"))

        bank = k["bank"]
        bank_rows, bank_attr, bank_dst, bank_group = bank[0:4]
        rowsT = bank_rows[:, :].rearrange("p (a e) -> p a e", a=4)
        attr_ps = bank_attr[:, 0:2 * P].rearrange("p (a e) -> p a e", a=2)
        dst_ps = bank_dst[:, 0:2 * P].rearrange("p (a e) -> p a e", a=2)
        kv = [b[:, :].rearrange("p (t a f) -> p t a f", t=2, a=2) for b in bank[4:6]]
        qe = [b[:, :].rearrange("p (t a f) -> p t a f", t=2, a=2) for b in bank[6:8]]
        grp = bank_group[:, 0:2 * ROW].rearrange("p (t f) -> p t f", t=2)
        hist_ps = bank[1][:, 0:HI]
        histT_ps = bank_rows[:, :].rearrange("p (a e) -> p a e", a=4)

        weight_loads = [
            (k["Wkv"][:, 0:D], Wk), (k["Wkv"][:, D:2 * D], Wv), (k["Wq"][:, :], Wq), (k["We"][:, :], We),
            (k["W1"][:, :], W1), (k["W2"][:, :, :], W2.rearrange("(c p) n -> p c n", p=P)),
            (k["Ws"][:, :], W_self), (k["Wi"][:, :], W_inter),
        ] + [(k["b1"][:, c:c + 1], b1[c * D:(c + 1) * D].rearrange("(p o) -> p o", o=1)) for c in range(2)
        ] + [(k[name][:, :], v.rearrange("(p o) -> p o", o=1)) for name, v in
             (("b2", b2), ("g1", bn1_g), ("be1", bn1_b), ("g2", bn2_g), ("be2", bn2_b))]
        index_loads = [
            (t[:, 0:ET], v[0:P * ET].rearrange("(p t) -> p t", p=P)) for t, v in ((src_i, src), (dst_i, dst))
        ] + [(t[0:ER, ET:ET + 1], v[P * ET:N].rearrange("(p t) -> p t", t=1))
             for t, v in ((src_i, src), (dst_i, dst))]

        with nc.Block() as block:
            @block.sync
            def _(sp):
                for to, of in index_loads + weight_loads:
                    sp.dma_start(to, of).then_inc(loaded, 16)
                sp.wait_ge(zeros_ready, 1)
                flat = table.rearrange("r f -> (r f)").rearrange("(p c n) -> p c n", p=P, n=zero_cols)
                sp.dma_start(flat, zeros[:, :].unsqueeze(1).broadcast_to([P, TROWS * ROW // P // zero_cols,
                                                                          zero_cols])).then_inc(cleared, 16)
                sp.wait_ge(cleared, 16)

            @block.gpsimd
            def _(pool):
                nc.gpsimd.iota(count_i[:, :], pattern=[[1, HI]], base=0, channel_multiplier=0)\
                    .then_inc(const_ready, 1)
                nc.gpsimd.iota(prow_i[:, :], pattern=[[1, 1]], base=N, channel_multiplier=1)\
                    .then_inc(const_ready, 1)
                pool.wait_ge(prep, 1)
                nc.gpsimd.affine_select(out=ident[:, :], in_=ones[:, :], compare_op=ALU.is_equal, fill=0.0,
                                        base=0, pattern=[[-1, P]], channel_multiplier=1)\
                    .then_inc(const_ready, 1)
                nc.gpsimd.affine_select(out=before[:, :], in_=ones[:, :], compare_op=ALU.is_gt, fill=0.0,
                                        base=0, pattern=[[-1, P]], channel_multiplier=1)\
                    .then_inc(const_ready, 1)
                pool.wait_ge(prep, 13)

                def low_one_hots(s):
                    r, n = s.rows, s.tiles
                    free = s.ago(2)
                    if s.had(2):
                        pool.wait_ge(counted, free)
                    pool.sem_inc(held, 1)
                    pool.tensor_copy(lo_now[0:r, s.slot, 0:n], cols(src_lo, s, 2)).then_inc(lo_now_ready, 1)
                    pool.wait_ge(lo_now_ready, s.done)
                    pool.sem_inc(held, 1)
                    pool.tensor_scalar(hot_lo[0:r, s.slot, 0, :], count_h[0:r, 0:P],
                                       lo_now[0:r, s.slot, 0:1], None, ALU.is_equal).then_inc(low_ready, 1)

                walk(pool, EU, 2, [(0, low_one_hots)], EDGE_SIZES)

            @block.vector
            def _(dve):
                dve.memset(zeros[:, :], 0.0).then_inc(zeros_ready, 1)
                dve.memset(ones[:, :], 1.0).then_inc(prep, 1)
                dve.memset(message[:, :, :, USED:ROW], 0.0).then_inc(prep, 1)
                dve.memset(message[:, :, :, CCOL:CCOL + 1], 1.0).then_inc(prep, 1)
                dve.memset(k["eps"][:, :], EPS).then_inc(prep, 1)
                dve.wait_ge(const_ready, 2)
                dve.tensor_copy(count_h[:, :], count_i[:, :])
                dve.tensor_copy(spare_row[:, :], prow_i[:, :]).then_inc(prep, 1)
                dve.wait_ge(loaded, 16 * len(index_loads + weight_loads))
                for rows, c0, c1 in ((P, 0, ET), (ER, ET, ET + 1)):
                    a = slice(0, rows), slice(c0, c1)
                    dve.tensor_copy(ends[a[0], a[1], 0], src_i[a])
                    dve.tensor_copy(ends[a[0], a[1], 1], dst_i[a])
                    dve.tensor_copy(dst_f[a], dst_i[a])
                    dve.tensor_scalar(bits[a], src_i[a], P - 1, None, ALU.bitwise_and).then_inc(prep, 1)
                dve.wait_ge(prep, 7)
                for rows, c0, c1 in ((P, 0, ET), (ER, ET, ET + 1)):
                    a = slice(0, rows), slice(c0, c1)
                    dve.tensor_copy(src_lo[a], bits[a])
                    dve.tensor_scalar(spare[a], dst_f[a], -1.0, spare_row[0:rows, :], ALU.mult, ALU.add)\
                        .then_inc(prep, 1)
                dve.wait_ge(prep, 9)
                for rows, c0, c1 in ((P, 0, ET), (ER, ET, ET + 1)):
                    a = slice(0, rows), slice(c0, c1)
                    dve.tensor_scalar(bits[a], src_i[a], 7, None, ALU.logical_shift_right).then_inc(prep, 1)
                dve.wait_ge(prep, 11)
                for rows, c0, c1 in ((P, 0, ET), (ER, ET, ET + 1)):
                    a = slice(0, rows), slice(c0, c1)
                    dve.tensor_copy(src_hi[a], bits[a]).then_inc(prep, 1)
                dve.wait_ge(prep, 13)

                def one_hots(s):
                    r = s.rows
                    free = s.ago(2)
                    if s.had(2):
                        dve.wait_ge(counted, free)
                        dve.sem_inc(held, 1)
                    for j in range(s.tiles):
                        t = s.index * 2 + j
                        lo = src_lo[0:r, t:t + 1] if s.tail else src_lo[0:r, bass.ds(t, 1)]
                        hi = src_hi[0:r, t:t + 1] if s.tail else src_hi[0:r, bass.ds(t, 1)]
                        if j > 0:
                            dve.tensor_scalar(hot_lo[0:r, s.slot, j, :], count_h[0:r, 0:P], lo, None,
                                              ALU.is_equal)
                        last = dve.tensor_scalar(hot_hi[0:r, s.slot, j, :], count_h[0:r, :], hi, None,
                                                 ALU.is_equal)
                    last.then_inc(hot_ready, 1)

                walk(dve, EU, 2, [(0, one_hots)], EDGE_SIZES)
                dve.wait_ge(counted, EU + 1)
                dve.tensor_copy(hist[:, :], hist_ps).then_inc(hist_ready, 1)
                dve.wait_ge(hist_turned, 1)
                for c in range(4):
                    w = min(P, ET + 1 - c * P)
                    last = dve.tensor_copy(histT[0:w, c, :], histT_ps[0:w, c, :])
                last.then_inc(histT_ready, 1)

            @block.scalar
            def _(act):
                act.wait_ge(histT_ready, 1)
                for c in range(4):
                    w = min(P, ET + 1 - c * P)
                    act.dma_start(k["degree"][c * P:c * P + w, :], histT[0:w, c, :])\
                        .then_inc(degree_stored, 16)
                act.wait_ge(degree_stored, 64)

            @block.tensor
            def _(pe):
                pe.wait_ge(const_ready, 4)

                def count(s):
                    r = s.rows
                    pe.wait_ge(hot_ready, s.done)
                    pe.wait_ge(low_ready, s.done)
                    for j in range(s.tiles):
                        last = pe.matmul(hist_ps, hot_lo[0:r, s.slot, j, :], hot_hi[0:r, s.slot, j, :],
                                         start=s.first and j == 0, stop=s.tail)
                    last.then_inc(counted, 1)

                walk(pe, EU, 2, [(0, count)], EDGE_SIZES)
                pe.wait_ge(hist_ready, 1)
                for c in range(4):
                    w = min(P, ET + 1 - c * P)
                    last = pe.transpose(histT_ps[0:w, c, :], hist[:, c * P:c * P + w], ident[:, :])
                last.then_inc(hist_turned, 1)


        with nc.Block() as block:
            @block.sync
            def _(sp):
                def load_attr(s):
                    free = s.ago(2)
                    if s.had(2):
                        sp.wait_ge(attr_turned, free)
                    sp.dma_start(attr[0:s.rows, s.slot, 0:s.tiles, :], edge_rows(edge_attr, s))\
                        .then_inc(attr_landed[s.slot], 16)

                def clear_sums(s):
                    rows, parts = (TROWS - 2 * P * EU, (TROWS - 2 * P * EU) // 2) if s.tail else (2 * P, P)
                    r0 = s.value(s.index * (2 * P))
                    for t in k["sums"]:
                        part = t[r0:r0 + rows, :] if s.tail else t[bass.ds(r0, rows), :]
                        sp.dma_start(part.rearrange("(p r) d -> p (r d)", r=2), zeros[0:parts, 0:2 * D])\
                            .then_inc(sums_cleared, 16)

                walk(sp, EU, 2, [(0, load_attr), (0, clear_sums)], EDGE_SIZES)
                sp.wait_ge(sums_cleared, 32 * (EU + 1))

            @block.gpsimd
            def _(pool):
                def hold(*waits):
                    for sem_, value in waits:
                        pool.wait_ge(sem_, value)
                    pool.sem_inc(held, 1)

                def gather(s, j):
                    for end in range(2):
                        pool.indirect_dma_start(
                            rows_in[0:s.rows, s.slot, j, end, :], None, x,
                            bass.IndirectOffsetOnAxis(index[0:s.rows, s.slot, j, end:end + 1], 0))\
                            .then_inc(landed[s.slot], 16)

                def add(s, j):
                    pool.indirect_dma_start(
                        table, bass.IndirectOffsetOnAxis(add_at[0:s.rows, s.slot, j:j + 1], 0),
                        group[0:s.rows, s.slot, j, :], None, compute_op=ALU.add).then_inc(rows_added, 16)

                def gather_first(s):
                    free = s.ago(2)
                    waits = [(index_ready, s.done)]
                    if s.had(2):
                        waits.append((h_ready, free))
                    hold(*waits)
                    gather(s, 0)

                def gather_second(s):
                    if s.tiles > 1:
                        gather(s, 1)

                def add_first(s):
                    last = s.value(s.index * 32)
                    waits = [(group_ready, s.done)]
                    if not s.first:
                        waits.append((rows_added, last))
                    hold(*waits)
                    add(s, 0)

                def add_second(s):
                    last = s.value(s.index * 32 + 16)
                    if s.tiles > 1:
                        hold((rows_added, last))
                        add(s, 1)

                walk(pool, EU, 2, [(0, gather_first), (4, add_first), (0, gather_second), (4, add_second)],
                     EDGE_SIZES)
                pool.wait_ge(rows_added, 32 * EU + 16)

            @block.vector
            def _(dve):
                def hold(*waits):
                    for sem_, value in waits:
                        dve.wait_ge(sem_, value)
                    dve.sem_inc(held, 1)

                def make_index(s):
                    landed_value = s.value(s.turn * 64)
                    if s.had(2):
                        hold((landed[s.slot], landed_value))
                    t0 = s.index * 2
                    part = (ends[0:s.rows, t0:t0 + s.tiles, :] if s.tail
                            else ends[:, bass.ds(t0, 2), :])
                    dve.tensor_copy(index[0:s.rows, s.slot, 0:s.tiles, :], part).then_inc(index_ready, 1)

                def stats(s):
                    full = s.value(s.turn * 64 + (32 if s.tail else 64))
                    dve.wait_ge(landed[s.slot], full)
                    for a in range(2 * s.tiles):
                        last = dve.bn_stats(stat[0:s.rows, s.slot, a, :],
                                            rows_in[0:s.rows, s.slot, a // 2, a % 2, :])
                    last.then_inc(stats_ready, 1)

                def mean_var(s):
                    n, r = 2 * s.tiles, s.rows
                    hold((stats_ready, s.done))
                    for a in range(n):
                        last = dve.bn_aggr(mv[0:r, s.slot, a, :], stat[0:r, s.slot, a, :])
                    last.then_inc(mv_ready, 1)
                    dve.tensor_copy(dst_now[0:r, s.slot, 0:s.tiles], cols(dst_f, s, 2))
                    dve.wait_ge(mv_ready, s.done)
                    dve.tensor_scalar(negmean[0:r, s.slot, 0:n], mv[0:r, s.slot, 0:n, 0], -1.0, None,
                                      ALU.mult).then_inc(negmean_ready, 1)

                def score_and_compare(s):
                    r, n = s.rows, s.tiles
                    free = s.ago(2)
                    dve.wait_ge(dst_turned, s.done)
                    if s.had(2):
                        dve.wait_ge(grouped, free)
                    dve.tensor_tensor(same[0:r, s.slot, 0:n, 0:r], dst_ps[0:r, 0:n, 0:r],
                                      spread(cols(dst_f, s, 2), r), ALU.is_equal).then_inc(same_ready, 1)
                    dve.wait_ge(q_ready, s.done)
                    dve.tensor_tensor(kq[0:r, 0:n, :], kv[s.slot][0:r, 0:n, 0, :], q[0:r, s.slot, 0:n, :],
                                      ALU.mult).then_inc(kq_ready, 1)
                    dve.wait_ge(same_ready, s.done)
                    for j in range(n):
                        last = dve.tensor_tensor_reduce(
                            out=earlier[0:r, j, 0:r], in0=same[0:r, s.slot, j, 0:r], in1=before[0:r, 0:r],
                            scale=1.0, scalar=0.0, op0=ALU.mult, op1=ALU.add, accum_out=rank[0:r, j:j + 1])
                    last.then_inc(rank_ready, 1)
                    dve.wait_ge(kq_ready, s.done)
                    dve.tensor_tensor(kqe[0:r, 0:n, :], kq[0:r, 0:n, :], qe[s.slot][0:r, 0:n, 1, :],
                                      ALU.mult).then_inc(kqe_ready, 1)
                    dve.wait_ge(rank_ready, s.done)
                    dve.scalar_tensor_tensor(move[0:r, 0:n], rank[0:r, 0:n], 0.0, cols(spare, s, 2),
                                             ALU.is_gt, ALU.mult).then_inc(move_ready, 1)
                    dve.wait_ge(rstd_ready, s.done)
                    rs = rstd[0:r, s.slot, 0:2 * n].rearrange("p (t a) -> p t a", a=2)
                    dve.tensor_tensor(rr[0:r, s.slot, 0:n], rs[:, :, 0], rs[:, :, 1], ALU.mult)\
                        .then_inc(rr_ready, 1)
                    dve.wait_ge(kqe_ready, s.done)
                    dve.tensor_reduce(raw[0:r, 0:n, :],
                                      kqe[0:r, 0:n, :].rearrange("p t (h d) -> p t h d", h=H), AX.X,
                                      ALU.add).then_inc(raw_ready, 1)
                    dve.wait_ge(move_ready, s.done)
                    dve.tensor_tensor(cols(target, s, 2), move[0:r, 0:n], cols(dst_f, s, 2), ALU.add)\
                        .then_inc(target_ready, 1)
                    dve.wait_ge(rr_ready, s.done)
                    dve.wait_ge(raw_ready, s.done)
                    dve.tensor_tensor(scaled[0:r, 0:n, :], raw[0:r, 0:n, :], spread(rr[0:r, s.slot, 0:n], H),
                                      ALU.mult).then_inc(scaled_ready, 1)
                    dve.wait_ge(scaled_ready, s.done)
                    dve.tensor_scalar(clipped[0:r, 0:n, :], scaled[0:r, 0:n, :], 5.0, -5.0, ALU.min, ALU.max)\
                        .then_inc(clipped_ready, 1)

                def messages(s):
                    r, n = s.rows, s.tiles
                    slot_added = s.value(s.index * 32 - 32)
                    t0 = s.index * 2
                    dve.wait_ge(weight_ready, s.done)
                    if s.had(2):
                        dve.wait_ge(rows_added, slot_added)
                    rs = rstd[0:r, s.slot, 0:2 * n].rearrange("p (t a) -> p t a", a=2)
                    dve.tensor_tensor(wr[0:r, 0:n, :], message[0:r, s.slot, 0:n, WCOL:WCOL + H],
                                      spread(rs[:, :, 0], H), ALU.mult).then_inc(wr_ready, 1)
                    hold((target_ready, s.done))
                    part = (target[0:r, t0:t0 + n] if s.tail else target[:, bass.ds(t0, 2)])
                    dve.tensor_copy(add_at[0:r, s.slot, 0:n], part)
                    dve.wait_ge(wr_ready, s.done)
                    for j in range(n):
                        last = dve.tensor_tensor(
                            message[0:r, s.slot, j, 0:D].rearrange("p (h d) -> p h d", h=H),
                            kv[s.slot][0:r, j, 1, :].rearrange("p (h d) -> p h d", h=H),
                            spread(wr[0:r, j, :], DH), ALU.mult)
                    last.then_inc(message_ready, 1)

                walk(dve, EU, 2, [(4, score_and_compare), (2, stats), (4, messages), (2, mean_var),
                               (0, make_index)], EDGE_SIZES)

            @block.scalar
            def _(act):
                act.preload_act_table_set("natural_log_exp_and_others")

                def queries(s):
                    r, n = s.rows, s.tiles
                    act.wait_ge(products_ready, s.done)
                    act.activation(q[0:r, s.slot, 0:n, :], qe[s.slot][0:r, 0:n, 0, :], ACT.Copy,
                                   scale=float(DH) ** -0.5).then_inc(q_ready, 1)

                def norm(s):
                    r, n = s.rows, 2 * s.tiles
                    act.wait_ge(negmean_ready, s.done)
                    for a in range(n):
                        last = act.activation(h[0:r, s.slot, a, :], rows_in[0:r, s.slot, a // 2, a % 2, :],
                                              ACT.Relu, bias=negmean[0:r, s.slot, a:a + 1])
                    last.then_inc(h_ready, 1)
                    act.activation(lnvar[0:r, s.slot, 0:n], mv[0:r, s.slot, 0:n, 1], ACT.Ln,
                                   bias=k["eps"][0:r, :]).then_inc(ln_ready, 1)
                    act.wait_ge(ln_ready, s.done)
                    act.activation(rstd[0:r, s.slot, 0:n], lnvar[0:r, s.slot, 0:n], ACT.Exp, scale=-0.5)\
                        .then_inc(rstd_ready, 1)

                def weights(s):
                    r, n = s.rows, s.tiles
                    act.wait_ge(clipped_ready, s.done)
                    act.activation(message[0:r, s.slot, 0:n, WCOL:WCOL + H], clipped[0:r, 0:n, :], ACT.Exp)\
                        .then_inc(weight_ready, 1)

                def evacuate(s):
                    r, n = s.rows, s.tiles
                    act.wait_ge(attr_turned, s.done)
                    act.activation(attrT[:, s.slot, 0:n, 0:r], attr_ps[:, 0:n, 0:r], ACT.Copy)\
                        .then_inc(attrT_ready, 1)
                    act.wait_ge(turned, s.done)
                    act.activation(hT[:, s.slot, 0:2 * n, 0:r], rowsT[:, 0:2 * n, 0:r], ACT.Copy)\
                        .then_inc(hT_ready, 1)

                def group_sums(s):
                    r, n = s.rows, s.tiles
                    act.wait_ge(grouped, s.done)
                    act.activation(group[0:r, s.slot, 0:n, :], grp[0:r, 0:n, :], ACT.Copy)\
                        .then_inc(group_ready, 1)

                walk(act, EU, 2, [(0, norm), (2, group_sums), (0, evacuate), (1, weights), (0, queries)],
                     EDGE_SIZES)

            @block.tensor
            def _(pe):
                def turn_dst(s):
                    r = s.rows
                    prev = s.ago(1)
                    pe.wait_ge(negmean_ready, s.done)
                    if not s.first:
                        pe.wait_ge(same_ready, prev)
                    for j in range(s.tiles):
                        last = pe.transpose(dst_ps[:, j, 0:r],
                                            dst_now[0:r, s.slot, j:j + 1].broadcast_to([r, P]),
                                            ident[0:r, 0:r])
                    last.then_inc(dst_turned, 1)

                def turn(s):
                    r, n = s.rows, s.tiles
                    full, prev = s.landed(), s.ago(1)
                    pe.wait_ge(attr_landed[s.slot], full)
                    if not s.first:
                        pe.wait_ge(attrT_ready, prev)
                    for j in range(n):
                        last = pe.transpose(attr_ps[:, j, 0:r], attr[0:r, s.slot, j, :], ident[0:r, 0:r])
                    last.then_inc(attr_turned, 1)
                    pe.wait_ge(h_ready, s.done)
                    if not s.first:
                        pe.wait_ge(hT_ready, prev)
                    for a in range(2 * n):
                        last = pe.transpose(rowsT[:, a, 0:r], h[0:r, s.slot, a, :], ident[0:r, 0:r])
                    last.then_inc(turned, 1)

                def product(s):
                    r = s.rows
                    free = s.ago(2)
                    pe.wait_ge(hT_ready, s.done)
                    pe.wait_ge(attrT_ready, s.done)
                    if s.had(2):
                        pe.wait_ge(message_ready, free)
                    for j in range(s.tiles):
                        pe.matmul(kv[s.slot][0:r, j, :, :].rearrange("p a f -> p (a f)"), hT[:, s.slot, 2 * j, 0:r],
                                  k["Wkv"][:, :], start=True, stop=True)
                        pe.matmul(qe[s.slot][0:r, j, 0, :], hT[:, s.slot, 2 * j + 1, 0:r], k["Wq"][:, :],
                                  start=True, stop=True)
                        last = pe.matmul(qe[s.slot][0:r, j, 1, :], attrT[:, s.slot, j, 0:r], k["We"][:, :],
                                         start=True, stop=True)
                    last.then_inc(products_ready, 1)

                def group_up(s):
                    r = s.rows
                    prev = s.ago(1)
                    pe.wait_ge(message_ready, s.done)
                    if not s.first:
                        pe.wait_ge(group_ready, prev)
                    for j in range(s.tiles):
                        last = pe.matmul(grp[0:r, j, :], same[0:r, s.slot, j, 0:r],
                                         message[0:r, s.slot, j, :], start=True, stop=True)
                    last.then_inc(grouped, 1)

                walk(pe, EU, 2, [(2, group_up), (1, turn_dst), (0, turn), (0, product)], EDGE_SIZES)


def norm_constants(k, act, dve, stats, gamma, beta, tiles, sems):
    mean_var, logvar, std_inv, scale, shift = tiles
    aggregated, logged, inverted, scaled, shift_ready = sems

    def on_act():
        act.wait_ge(aggregated, 1)
        act.activation(logvar[:, :], mean_var[:, 1:2], ACT.Ln, bias=k["eps"][:, :]).then_inc(logged, 1)
        act.wait_ge(logged, 1)
        act.activation(std_inv[:, :], logvar[:, :], ACT.Exp, scale=-0.5).then_inc(inverted, 1)

    def on_dve():
        dve.bn_aggr(mean_var[:, :], stats[:, :, :].rearrange("p a b -> p (a b)")).then_inc(aggregated, 1)
        dve.wait_ge(inverted, 1)
        dve.tensor_tensor(scale[:, :], std_inv[:, :], gamma[:, :], ALU.mult).then_inc(scaled, 1)
        dve.wait_ge(scaled, 1)
        dve.tensor_tensor(logvar[:, :], mean_var[:, 0:1], scale[:, :], ALU.mult).then_inc(scaled, 1)
        dve.wait_ge(scaled, 2)
        dve.tensor_tensor(shift[:, :], beta[:, :], logvar[:, :], ALU.subtract).then_inc(shift_ready, 1)

    return on_act, on_dve


def residual_stage(nc, k, x):
    ctx = Stage(nc)
    with ctx:
        def sb(name, shape, dt=FP32):
            return ctx.enter_context(nc.sbuf_tensor("b_" + name, shape, dt))

        def sem(name):
            return stage_semaphore(nc, ctx, "b_" + name)

        R = RING
        xg = sb("xg", [P, R, 4, D])
        acc = sb("acc", [P, R, 4, ROW])
        stat = sb("stat", [P, R, 4, 6])
        mv = sb("mv", [P, R, 4, 2])
        lnvar = sb("lnvar", [P, R, 4])
        rstd = sb("rstd", [P, R, 4])
        shift = sb("shift", [P, R, 4])
        h = sb("h", [P, R, 4, D])
        weight = sb("weight", [P, R, 4, H])
        weight_inv = sb("weight_inv", [P, R, 4, H])
        attn = sb("attn", [P, R, 4, D])
        h1 = sb("h1", [P, R, 4, D])
        h1T = sb("h1T", [P, R, 512])

        x_landed = [sem(f"x_landed{i}") for i in range(R)]
        acc_landed = [sem(f"acc_landed{i}") for i in range(R)]
        h1T_stored = [sem(f"h1T_stored{i}") for i in range(R)]
        stats_ready, mv_ready, ln_ready, rstd_ready = (
            sem("stats_ready"), sem("mv_ready"), sem("ln_ready"), sem("rstd_ready"))
        shift_ready, h_ready = sem("shift_ready"), sem("h_ready")
        weight_ready, inv_ready, attn_ready = sem("weight_ready"), sem("inv_ready"), sem("attn_ready")
        h1_ready, turned, h1T_ready, h1T_measured = (
            sem("h1_ready"), sem("turned"), sem("h1T_ready"), sem("h1T_measured"))
        held = sem("held")
        banks = k["bank"][0:2]

        with nc.Block() as block:
            @block.sync
            def _(sp):
                def load(s):
                    free = s.ago(R)
                    if s.had(R):
                        sp.wait_ge(h_ready, free)
                    sp.dma_start(xg[0:s.rows, s.slot, 0:s.tiles, :], node_rows(x, s))\
                        .then_inc(x_landed[s.slot], 16)
                    if s.had(R):
                        sp.wait_ge(attn_ready, free)
                    sp.dma_start(acc[0:s.rows, s.slot, 0:s.tiles, :], node_rows(k["table"], s))\
                        .then_inc(acc_landed[s.slot], 16)

                def store(s):
                    sp.wait_ge(h1T_ready, s.done)
                    sp.dma_start(group_rows(k["h1T"], s), h1T[:, s.slot, 0:s.width])\
                        .then_inc(h1T_stored[s.slot], 16)

                walk(sp, NG, R, [(0, load), (3, store)], NODE_SIZES)
                wait_stored(sp, h1T_stored)

            @block.gpsimd
            def _(pool):
                def residual(s):
                    r, n = s.rows, s.tiles
                    free = s.ago(R)
                    pool.wait_ge(inv_ready, s.done)
                    pool.tensor_tensor(
                        attn[0:r, s.slot, 0:n, :].rearrange("p t (h d) -> p t h d", h=H),
                        acc[0:r, s.slot, 0:n, 0:D].rearrange("p t (h d) -> p t h d", h=H),
                        weight_inv[0:r, s.slot, 0:n, :].unsqueeze(3).broadcast_to([r, n, H, DH]), ALU.mult)\
                        .then_inc(attn_ready, 1)
                    pool.wait_ge(h_ready, s.done)
                    pool.wait_ge(attn_ready, s.done)
                    if s.had(R):
                        pool.wait_ge(turned, free)
                    pool.tensor_tensor(h1[0:r, s.slot, 0:n, :], h[0:r, s.slot, 0:n, :],
                                       attn[0:r, s.slot, 0:n, :], ALU.add).then_inc(h1_ready, 1)

                walk(pool, NG, R, [(0, residual)], NODE_SIZES)

            @block.vector
            def _(dve):
                def stats(s):
                    r, n = s.rows, s.tiles
                    full, free = s.landed(), s.ago(R)
                    dve.wait_ge(acc_landed[s.slot], full)
                    if s.had(R):
                        dve.wait_ge(attn_ready, free)
                    dve.tensor_scalar(weight[0:r, s.slot, 0:n, :], acc[0:r, s.slot, 0:n, WCOL:WCOL + H],
                                      1e-6, None, ALU.add).then_inc(weight_ready, 1)
                    dve.wait_ge(x_landed[s.slot], full)
                    for j in range(n):
                        last = dve.bn_stats(stat[0:r, s.slot, j, :], xg[0:r, s.slot, j, :])
                    last.then_inc(stats_ready, 1)
                    dve.wait_ge(weight_ready, s.done)
                    dve.reciprocal(weight_inv[0:r, s.slot, 0:n, :], weight[0:r, s.slot, 0:n, :])\
                        .then_inc(inv_ready, 1)
                    dve.wait_ge(stats_ready, s.done)
                    dve.sem_inc(held, 1)
                    dve.tensor_copy(cols(k["in_deg"], s, 4), acc[0:r, s.slot, 0:n, CCOL])
                    for j in range(n):
                        last = dve.bn_aggr(mv[0:r, s.slot, j, :], stat[0:r, s.slot, j, :])
                    last.then_inc(mv_ready, 1)

                def norm_shift(s):
                    r, n = s.rows, s.tiles
                    dve.wait_ge(rstd_ready, s.done)
                    dve.scalar_tensor_tensor(shift[0:r, s.slot, 0:n], mv[0:r, s.slot, 0:n, 0], -1.0,
                                             rstd[0:r, s.slot, 0:n], ALU.mult, ALU.mult)\
                        .then_inc(shift_ready, 1)

                def measure(s):
                    dve.wait_ge(h1T_ready, s.done)
                    if not s.tail:
                        dve.sem_inc(held, 1)
                    dve.bn_stats(stat_cols(k["bn1"], s), h1T[:, s.slot, 0:s.width]).then_inc(h1T_measured, 1)

                walk(dve, NG, R, [(0, stats), (3, measure), (0, norm_shift)], NODE_SIZES)

            @block.scalar
            def _(act):
                def norm_scale(s):
                    r, n = s.rows, s.tiles
                    act.wait_ge(mv_ready, s.done)
                    act.activation(lnvar[0:r, s.slot, 0:n], mv[0:r, s.slot, 0:n, 1], ACT.Ln,
                                   bias=k["eps"][0:r, :]).then_inc(ln_ready, 1)
                    act.wait_ge(ln_ready, s.done)
                    act.activation(rstd[0:r, s.slot, 0:n], lnvar[0:r, s.slot, 0:n], ACT.Exp, scale=-0.5)\
                        .then_inc(rstd_ready, 1)

                def norm(s):
                    r, n = s.rows, s.tiles
                    free = s.ago(R)
                    act.wait_ge(shift_ready, s.done)
                    if s.had(R):
                        act.wait_ge(h1_ready, free)
                    for j in range(n):
                        last = act.activation(h[0:r, s.slot, j, :], xg[0:r, s.slot, j, :], ACT.Relu,
                                              bias=shift[0:r, s.slot, j:j + 1],
                                              scale=rstd[0:r, s.slot, j:j + 1])
                    last.then_inc(h_ready, 1)

                def evacuate(s):
                    stored, free = s.landed_before(), s.ago(R)
                    act.wait_ge(turned, s.done)
                    if s.had(R):
                        act.wait_ge(h1T_stored[s.slot], stored)
                        act.wait_ge(h1T_measured, free)
                    act.activation(h1T[:, s.slot, 0:s.width], banks[s.bank][:, 0:s.width], ACT.Copy)\
                        .then_inc(h1T_ready, 1)

                walk(act, NG, R, [(0, norm_scale), (2, evacuate), (0, norm)], NODE_SIZES)

            @block.tensor
            def _(pe):
                def turn(s):
                    r = s.rows
                    free = s.ago(2)
                    pe.wait_ge(h1_ready, s.done)
                    if s.had(2):
                        pe.wait_ge(h1T_ready, free)
                    for j in range(s.tiles):
                        last = pe.transpose(banks[s.bank][:, j * r:(j + 1) * r], h1[0:r, s.slot, j, :],
                                            k["ident"][0:r, 0:r])
                    last.then_inc(turned, 1)

                walk(pe, NG, R, [(0, turn)], NODE_SIZES)


def bn_tiles(sb, sem):
    return ([sb("mean_var", [P, 2])] + [sb(n, [P, 1]) for n in ("bn_log", "std_inv", "bn_scale", "bn_shift")],
            [sem(n) for n in ("aggregated", "logged", "inverted", "bn_scaled", "bn_ready")])


def mlp_stage(nc, k):
    ctx = Stage(nc)
    with ctx:
        def sb(name, shape, dt=FP32):
            return ctx.enter_context(nc.sbuf_tensor("c_" + name, shape, dt))

        def sem(name):
            return stage_semaphore(nc, ctx, "c_" + name)

        R = RING
        tiles, sems = bn_tiles(sb, sem)
        h1T = sb("h1T", [P, R, 512])
        y = sb("y", [P, R, 512])
        hidden = sb("hidden", [P, R, 2, 512])
        z = sb("z", [P, R, 512])
        landed = [sem(f"landed{i}") for i in range(R)]
        stored = [sem(f"stored{i}") for i in range(R)]
        y_ready, up_ready, hid0_ready, hid1_ready = (
            sem("y_ready"), sem("up_ready"), sem("hid0_ready"), sem("hid1_ready"))
        down_ready, z_ready, z_measured, held = (
            sem("down_ready"), sem("z_ready"), sem("z_measured"), sem("held"))
        up = [k["bank"][0:2], k["bank"][2:4]]
        down = k["bank"][4:6]

        with nc.Block() as block:
            @block.sync
            def _(sp):
                def load(s):
                    w = s.width
                    if s.had(R):
                        sp.wait_ge(y_ready, s.ago(R))
                    of = group_rows(k["h1T"], s)
                    sp.dma_start(h1T[:, s.slot, 0:w], of).then_inc(landed[s.slot], 16)

                def store(s):
                    w = s.width
                    sp.wait_ge(z_ready, s.done)
                    to = group_rows(k["zT"], s)
                    sp.dma_start(to, z[:, s.slot, 0:w]).then_inc(stored[s.slot], 16)

                walk(sp, NG, RING, [(0, load), (3, store)], NODE_SIZES)
                wait_stored(sp, stored)

            @block.scalar
            def _(act):
                norm_constants(k, act, None, k["bn1"], k["g1"], k["be1"], tiles, sems)[0]()
                act.wait_ge(sems[4], 1)

                def normed(s):
                    w = s.width
                    act.wait_ge(landed[s.slot], s.landed())
                    if s.had(R):
                        act.wait_ge(z_ready, s.ago(R))
                    act.activation(y[:, s.slot, 0:w], h1T[:, s.slot, 0:w], ACT.Identity,
                                   bias=tiles[4][:, :], scale=tiles[3][:, :]).then_inc(y_ready, 1)

                def hidden_first(s):
                    w = s.width
                    act.wait_ge(up_ready, s.done)
                    if s.had(R):
                        act.wait_ge(down_ready, s.ago(R))
                    act.activation(hidden[:, s.slot, 0, 0:w], up[s.bank][0][:, 0:w], ACT.Relu,
                                   bias=k["b1"][:, 0:1]).then_inc(hid0_ready, 1)

                walk(act, NG, RING, [(0, normed), (1, hidden_first)], NODE_SIZES)

            @block.vector
            def _(dve):
                norm_constants(k, None, dve, k["bn1"], k["g1"], k["be1"], tiles, sems)[1]()

                def hidden_second(s):
                    w = s.width
                    dve.wait_ge(up_ready, s.done)
                    if s.had(R):
                        dve.wait_ge(down_ready, s.ago(R))
                    dve.tensor_scalar(hidden[:, s.slot, 1, 0:w], up[s.bank][1][:, 0:w], k["b1"][:, 1:2],
                                      0.0, ALU.add, ALU.max).then_inc(hid1_ready, 1)

                def output(s):
                    w = s.width
                    kept = s.landed_before()
                    dve.wait_ge(down_ready, s.done)
                    if s.had(R):
                        dve.wait_ge(stored[s.slot], kept)
                    dve.scalar_tensor_tensor(z[:, s.slot, 0:w], down[s.bank][:, 0:w], k["b2"][:, :],
                                             y[:, s.slot, 0:w], ALU.add, ALU.add).then_inc(z_ready, 1)
                    dve.wait_ge(z_ready, s.done)
                    if not s.tail:
                        dve.sem_inc(held, 1)
                    dve.bn_stats(stat_cols(k["bn2"], s), z[:, s.slot, 0:w]).then_inc(z_measured, 1)

                walk(dve, NG, RING, [(1, hidden_second), (2, output)], NODE_SIZES)

            @block.tensor
            def _(pe):
                def expand(s):
                    w = s.width
                    free = s.ago(2)
                    pe.wait_ge(y_ready, s.done)
                    if s.had(2):
                        pe.wait_ge(hid0_ready, free)
                        pe.wait_ge(hid1_ready, free)
                    for c in range(2):
                        last = pe.matmul(up[s.bank][c][:, 0:w], k["W1"][:, c * D:(c + 1) * D],
                                         y[:, s.slot, 0:w], start=True, stop=True)
                    last.then_inc(up_ready, 1)

                def contract(s):
                    w = s.width
                    pe.wait_ge(hid0_ready, s.done)
                    pe.wait_ge(hid1_ready, s.done)
                    if s.had(2):
                        pe.wait_ge(z_ready, s.ago(2))
                    for c in range(2):
                        last = pe.matmul(down[s.bank][:, 0:w], k["W2"][:, c, :], hidden[:, s.slot, c, 0:w],
                                         start=c == 0, stop=c == 1)
                    last.then_inc(down_ready, 1)

                walk(pe, NG, RING, [(0, expand), (1, contract)], NODE_SIZES)


def normed_stage(nc, k, x):
    ctx = Stage(nc)
    with ctx:
        def sb(name, shape, dt=FP32):
            return ctx.enter_context(nc.sbuf_tensor("d_" + name, shape, dt))

        def sem(name):
            return stage_semaphore(nc, ctx, "d_" + name)

        R = RING
        tiles, sems = bn_tiles(sb, sem)
        xg = sb("xg", [P, R, 4, D])
        zT = sb("zT", [P, R, 512])
        zn = sb("zn", [P, R, 512])
        x2 = sb("x2", [P, R, 4, D])
        g = sb("g", [P, R, 4, D])
        stat = sb("stat", [P, R, 4, 6])
        mv = sb("mv", [P, R, 4, 2])
        lnvar = sb("lnvar", [P, R, 4])
        rstd = sb("rstd", [P, R, 4])
        gscale = sb("gscale", [P, R, 4])
        gshift = sb("gshift", [P, R, 4])
        x_landed = [sem(f"x_landed{i}") for i in range(R)]
        z_landed = [sem(f"z_landed{i}") for i in range(R)]
        x2_stored = [sem(f"x2_stored{i}") for i in range(R)]
        g_stored = [sem(f"g_stored{i}") for i in range(R)]
        deg_landed, deg_clipped, deg_logged, deg_ready = (
            sem("deg_landed"), sem("deg_clipped"), sem("deg_logged"), sem("deg_ready"))
        zn_ready, turned, x2_ready, stats_ready, mv_ready = (
            sem("zn_ready"), sem("turned"), sem("x2_ready"), sem("stats_ready"), sem("mv_ready"))
        ln_ready, rstd_ready, shift_ready, gshift_ready, g_ready, held = (
            sem("ln_ready"), sem("rstd_ready"), sem("shift_ready"), sem("gshift_ready"), sem("g_ready"),
            sem("held"))
        banks = k["bank"][0:2]
        out_deg, in_deg = k["out_deg"], k["in_deg"]
        deg_parts = [(t, slice(0, r), slice(c0, c1)) for t in (out_deg, in_deg)
                     for r, c0, c1 in ((P, 0, NT), (NR, NT, NC))]

        with nc.Block() as block:
            @block.sync
            def _(sp):
                flat = k["degree"].rearrange("a p -> (a p)")
                sp.dma_start(out_deg[:, 0:NT], flat[0:P * NT].rearrange("(p t) -> p t", p=P))\
                    .then_inc(deg_landed, 16)
                sp.dma_start(out_deg[0:NR, NT:NC], flat[P * NT:N].rearrange("(p t) -> p t", p=NR))\
                    .then_inc(deg_landed, 16)

                def load(s):
                    w = s.width
                    free = s.ago(R)
                    if s.had(R):
                        sp.wait_ge(zn_ready, free)
                    of = group_rows(k["zT"], s)
                    sp.dma_start(zT[:, s.slot, 0:w], of).then_inc(z_landed[s.slot], 16)
                    if s.had(R):
                        sp.wait_ge(x2_ready, free)
                    sp.dma_start(xg[0:s.rows, s.slot, 0:s.tiles, :], node_rows(x, s))\
                        .then_inc(x_landed[s.slot], 16)

                def store(s):
                    sp.wait_ge(x2_ready, s.done)
                    sp.dma_start(node_rows(k["x2"], s), x2[0:s.rows, s.slot, 0:s.tiles, :])\
                        .then_inc(x2_stored[s.slot], 16)
                    sp.wait_ge(g_ready, s.done)
                    sp.dma_start(node_rows(k["g"], s), g[0:s.rows, s.slot, 0:s.tiles, :])\
                        .then_inc(g_stored[s.slot], 16)

                walk(sp, NG, RING, [(0, load), (3, store)], NODE_SIZES)
                wait_stored(sp, x2_stored)
                wait_stored(sp, g_stored)

            @block.scalar
            def _(act):
                norm_constants(k, act, None, k["bn2"], k["g2"], k["be2"], tiles, sems)[0]()
                act.wait_ge(deg_clipped, 4)
                for t, rs, cs in deg_parts:
                    act.activation(t[rs, cs], t[rs, cs], ACT.Ln).then_inc(deg_logged, 1)
                act.wait_ge(deg_logged, 4)
                for t, rs, cs in deg_parts:
                    act.activation(t[rs, cs], t[rs, cs], ACT.Exp, scale=-0.5).then_inc(deg_ready, 1)
                act.wait_ge(sems[4], 1)

                def normed(s):
                    w = s.width
                    landed = s.landed()
                    act.wait_ge(z_landed[s.slot], landed)
                    if s.had(R):
                        act.wait_ge(turned, s.ago(R))
                    act.activation(zn[:, s.slot, 0:w], zT[:, s.slot, 0:w], ACT.Identity,
                                   bias=tiles[4][:, :], scale=tiles[3][:, :]).then_inc(zn_ready, 1)

                def norm_scale(s):
                    r, n = s.rows, s.tiles
                    act.wait_ge(mv_ready, s.done)
                    act.activation(lnvar[0:r, s.slot, 0:n], mv[0:r, s.slot, 0:n, 1], ACT.Ln,
                                   bias=k["eps"][0:r, :]).then_inc(ln_ready, 1)
                    act.wait_ge(ln_ready, s.done)
                    act.activation(rstd[0:r, s.slot, 0:n], lnvar[0:r, s.slot, 0:n], ACT.Exp, scale=-0.5)\
                        .then_inc(rstd_ready, 1)

                def scaled_rows(s):
                    r, n = s.rows, s.tiles
                    act.wait_ge(gshift_ready, s.done)
                    if s.had(R):
                        act.wait_ge(g_stored[s.slot], s.landed_before())
                    for j in range(n):
                        last = act.activation(g[0:r, s.slot, j, :], x2[0:r, s.slot, j, :], ACT.Relu,
                                              bias=gshift[0:r, s.slot, j:j + 1],
                                              scale=gscale[0:r, s.slot, j:j + 1])
                    last.then_inc(g_ready, 1)

                walk(act, NG, RING, [(0, normed), (2, scaled_rows), (1, norm_scale)], NODE_SIZES)

            @block.vector
            def _(dve):
                norm_constants(k, None, dve, k["bn2"], k["g2"], k["be2"], tiles, sems)[1]()
                dve.wait_ge(deg_landed, 32)
                for t, rs, cs in deg_parts:
                    dve.tensor_scalar(t[rs, cs], t[rs, cs], 1.0, None, ALU.max).then_inc(deg_clipped, 1)
                dve.wait_ge(deg_ready, 4)

                def residual(s):
                    r, n = s.rows, s.tiles
                    landed, kept = s.landed(), s.landed_before()
                    free = s.ago(R)
                    dve.wait_ge(x_landed[s.slot], landed)
                    dve.wait_ge(turned, s.done)
                    if s.had(R):
                        dve.wait_ge(x2_stored[s.slot], kept)
                        dve.wait_ge(g_ready, free)
                    dve.tensor_tensor(x2[0:r, s.slot, 0:n, :],
                                      banks[s.bank][0:r, 0:n * D].rearrange("p (t f) -> p t f", t=n),
                                      xg[0:r, s.slot, 0:n, :], ALU.add).then_inc(x2_ready, 1)
                    dve.wait_ge(x2_ready, s.done)
                    for j in range(n):
                        last = dve.bn_stats(stat[0:r, s.slot, j, :], x2[0:r, s.slot, j, :])
                    last.then_inc(stats_ready, 1)
                    dve.wait_ge(stats_ready, s.done)
                    dve.sem_inc(held, 1)
                    for j in range(n):
                        last = dve.bn_aggr(mv[0:r, s.slot, j, :], stat[0:r, s.slot, j, :])
                    last.then_inc(mv_ready, 1)

                def constants(s):
                    r, n = s.rows, s.tiles
                    dve.wait_ge(rstd_ready, s.done)
                    dve.scalar_tensor_tensor(cols(k["shift2"], s, 4), mv[0:r, s.slot, 0:n, 0], -1.0,
                                             rstd[0:r, s.slot, 0:n], ALU.mult, ALU.mult)\
                        .then_inc(shift_ready, 1)
                    dve.tensor_tensor(gscale[0:r, s.slot, 0:n], rstd[0:r, s.slot, 0:n], cols(out_deg, s, 4),
                                      ALU.mult)
                    dve.tensor_copy(cols(k["scale2"], s, 4), rstd[0:r, s.slot, 0:n])
                    dve.wait_ge(shift_ready, s.done)
                    dve.tensor_tensor(gshift[0:r, s.slot, 0:n], cols(k["shift2"], s, 4), cols(out_deg, s, 4),
                                      ALU.mult).then_inc(gshift_ready, 1)

                walk(dve, NG, RING, [(1, constants), (0, residual)], NODE_SIZES)

            @block.tensor
            def _(pe):
                def turn(s):
                    r = s.rows
                    pe.wait_ge(zn_ready, s.done)
                    if s.had(2):
                        pe.wait_ge(x2_ready, s.ago(2))
                    for j in range(s.tiles):
                        last = pe.transpose(banks[s.bank][0:r, j * D:(j + 1) * D],
                                            zn[:, s.slot, j * r:(j + 1) * r], k["ident"][:, :])
                    last.then_inc(turned, 1)

                walk(pe, NG, RING, [(0, turn)], NODE_SIZES)


def convolution_stage(nc, k):
    ctx = Stage(nc)
    with ctx:
        def sb(name, shape, dt=FP32):
            return ctx.enter_context(nc.sbuf_tensor("e_" + name, shape, dt))

        def sem(name):
            return stage_semaphore(nc, ctx, "e_" + name)

        index = sb("index", [P, 2, 2], I32)
        add_at = sb("add_at", [P, 2, 2], I32)
        dst_now = sb("dst_now", [P, 2, 2])
        g = sb("g", [P, 2, 2, D])
        same = sb("same", [P, 2, 2, P])
        group = sb("group", [P, 2, 2, D])
        landed = [sem(f"landed{i}") for i in range(2)]
        rows_added = [sem(f"rows_added{i}") for i in range(2)]
        index_ready, target_ready, dst_turned, same_ready, grouped, group_ready, held = (
            sem("index_ready"), sem("target_ready"), sem("dst_turned"), sem("same_ready"), sem("grouped"),
            sem("group_ready"), sem("held"))
        bank_dst, bank_grp = k["bank"][0:2], k["bank"][2:4]
        dst_f, ends, target, ident = k["dst_f"], k["ends"], k["target"], k["ident"]

        with nc.Block() as block:
            @block.gpsimd
            def _(pool):
                def hold(*waits):
                    for sem_, value in waits:
                        pool.wait_ge(sem_, value)
                    pool.sem_inc(held, 1)

                def gather(s):
                    free = s.ago(2)
                    waits = [(index_ready, s.done)]
                    if s.had(2):
                        waits.append((grouped, free))
                    hold(*waits)
                    for j in range(s.tiles):
                        pool.indirect_dma_start(
                            g[0:s.rows, s.slot, j, :], None, k["g"],
                            bass.IndirectOffsetOnAxis(index[0:s.rows, s.slot, j:j + 1], 0))\
                            .then_inc(landed[s.slot], 16)

                def add(s):
                    last = s.value(s.index * 16)
                    for j in range(s.tiles):
                        waits = [(group_ready, s.done), (target_ready, s.done)]
                        if not s.first:
                            waits.append((rows_added[j], last))
                        hold(*waits)
                        pool.indirect_dma_start(
                            k["sums"][j], bass.IndirectOffsetOnAxis(add_at[0:s.rows, s.slot, j:j + 1], 0),
                            group[0:s.rows, s.slot, j, :], None, compute_op=ALU.add)\
                            .then_inc(rows_added[j], 16)

                walk(pool, EU, 2, [(0, gather), (2, add)], EDGE_SIZES)
                pool.wait_ge(rows_added[0], 16 * (EU + 1))
                pool.wait_ge(rows_added[1], 16 * EU)

            @block.vector
            def _(dve):
                def make_index(s):
                    read, free = s.value(s.turn * 32), s.ago(2)
                    if s.had(2):
                        dve.wait_ge(dst_turned, free)
                        dve.wait_ge(landed[s.slot], read)
                        dve.sem_inc(held, 1)
                    dve.tensor_copy(dst_now[0:s.rows, s.slot, 0:s.tiles], cols(dst_f, s, 2))
                    t0, n = s.index * 2, s.tiles
                    part = ends[0:s.rows, t0:t0 + n, 0] if s.tail else ends[:, bass.ds(t0, 2), 0]
                    dve.tensor_copy(index[0:s.rows, s.slot, 0:n], part).then_inc(index_ready, 1)

                def compare(s):
                    r, n = s.rows, s.tiles
                    free = s.ago(2)
                    dve.wait_ge(dst_turned, s.done)
                    if s.had(2):
                        dve.wait_ge(grouped, free)
                    dve.tensor_tensor(same[0:r, s.slot, 0:n, 0:r],
                                      bank_dst[s.slot][0:r, 0:n * P].rearrange("p (t e) -> p t e", t=n)[:, :, 0:r],
                                      spread(cols(dst_f, s, 2), r), ALU.is_equal).then_inc(same_ready, 1)

                def targets(s):
                    n = s.tiles
                    added = s.value(s.index * 16 - 16)
                    if s.had(2):
                        dve.wait_ge(rows_added[0], added)
                        dve.wait_ge(rows_added[1], added)
                        dve.sem_inc(held, 1)
                    t0 = s.index * 2
                    part = target[0:s.rows, t0:t0 + n] if s.tail else target[:, bass.ds(t0, 2)]
                    dve.tensor_copy(add_at[0:s.rows, s.slot, 0:n], part).then_inc(target_ready, 1)

                walk(dve, EU, 2, [(0, make_index), (2, compare), (3, targets)], EDGE_SIZES)

            @block.scalar
            def _(act):
                def evacuate(s):
                    r, n = s.rows, s.tiles
                    added = s.value(s.index * 16 - 16)
                    act.wait_ge(grouped, s.done)
                    if s.had(2):
                        act.wait_ge(rows_added[0], added)
                        act.wait_ge(rows_added[1], added)
                    act.activation(group[0:r, s.slot, 0:n, :],
                                   bank_grp[s.slot][0:r, 0:n * D].rearrange("p (t f) -> p t f", t=n),
                                   ACT.Copy).then_inc(group_ready, 1)

                walk(act, EU, 2, [(0, evacuate)], EDGE_SIZES)

            @block.tensor
            def _(pe):
                def turn(s):
                    r = s.rows
                    free = s.ago(2)
                    pe.wait_ge(index_ready, s.done)
                    if s.had(2):
                        pe.wait_ge(same_ready, free)
                    for j in range(s.tiles):
                        last = pe.transpose(bank_dst[s.slot][0:P, j * P:j * P + r],
                                            dst_now[0:r, s.slot, j:j + 1].broadcast_to([r, P]),
                                            ident[0:r, 0:r])
                    last.then_inc(dst_turned, 1)

                def group_up(s):
                    r = s.rows
                    full = s.value(s.turn * 32 + (16 if s.tail else 32))
                    free = s.ago(2)
                    pe.wait_ge(landed[s.slot], full)
                    pe.wait_ge(same_ready, s.done)
                    if s.had(2):
                        pe.wait_ge(group_ready, free)
                    for j in range(s.tiles):
                        last = pe.matmul(bank_grp[s.slot][0:r, j * D:(j + 1) * D],
                                         same[0:r, s.slot, j, 0:r], g[0:r, s.slot, j, :],
                                         start=True, stop=True)
                    last.then_inc(grouped, 1)

                walk(pe, EU, 2, [(0, turn), (1, group_up)], EDGE_SIZES)


def output_stage(nc, k, out):
    ctx = Stage(nc)
    with ctx:
        def sb(name, shape, dt=FP32):
            return ctx.enter_context(nc.sbuf_tensor("f_" + name, shape, dt))

        def sem(name):
            return stage_semaphore(nc, ctx, "f_" + name)

        R = OUT_RING
        x2 = sb("x2", [P, R, 4, D])
        sums = [sb(f"sums{i}", [P, R, 4, D]) for i in range(2)]
        h = sb("h", [P, R, 4, D])
        total = sb("total", [P, R, 4, D])
        hs = sb("hs", [P, R, 4, D])
        both = sb("both", [P, R, 2, 4, D])
        bothT = sb("bothT", [P, R, 2, 512])
        res = sb("res", [P, R, 4, D])
        x_landed = [sem(f"x_landed{i}") for i in range(R)]
        sums_landed = [sem(f"sums_landed{i}") for i in range(R)]
        stored = [sem(f"stored{i}") for i in range(R)]
        h_ready, total_ready, hs_ready, plus_ready, times_ready = (
            sem("h_ready"), sem("total_ready"), sem("hs_ready"), sem("plus_ready"), sem("times_ready"))
        plus_turned, times_turned, plusT_ready, timesT_ready, product_ready, res_ready, held = (
            sem("plus_turned"), sem("times_turned"), sem("plusT_ready"), sem("timesT_ready"),
            sem("product_ready"), sem("res_ready"), sem("held"))
        bank_plus, bank_times, bank_out = k["bank"][0:2], k["bank"][2:4], k["bank"][4:6]

        with nc.Block() as block:
            @block.sync
            def _(sp):
                def load(s):
                    free = s.ago(R)
                    if s.had(R):
                        sp.wait_ge(total_ready, free)
                    for i in range(2):
                        sp.dma_start(sums[i][0:s.rows, s.slot, 0:s.tiles, :], node_rows(k["sums"][i], s))\
                            .then_inc(sums_landed[s.slot], 16)
                    if s.had(R):
                        sp.wait_ge(res_ready, free)
                    sp.dma_start(x2[0:s.rows, s.slot, 0:s.tiles, :], node_rows(k["x2"], s))\
                        .then_inc(x_landed[s.slot], 16)

                def store(s):
                    sp.wait_ge(res_ready, s.done)
                    sp.dma_start(node_rows(out, s), res[0:s.rows, s.slot, 0:s.tiles, :])\
                        .then_inc(stored[s.slot], 16)

                walk(sp, NG, OUT_RING, [(0, load), (4, store)], NODE_SIZES)
                wait_stored(sp, stored)

            @block.gpsimd
            def _(pool):
                def add_tables(s):
                    r, n = s.rows, s.tiles
                    full = s.landed(2)
                    free = s.ago(R)
                    pool.wait_ge(sums_landed[s.slot], full)
                    if s.had(R):
                        pool.wait_ge(hs_ready, free)
                    pool.tensor_tensor(total[0:r, s.slot, 0:n, :], sums[0][0:r, s.slot, 0:n, :],
                                       sums[1][0:r, s.slot, 0:n, :], ALU.add).then_inc(total_ready, 1)

                def plus(s):
                    r, n = s.rows, s.tiles
                    free = s.ago(R)
                    pool.wait_ge(hs_ready, s.done)
                    pool.wait_ge(h_ready, s.done)
                    if s.had(R):
                        pool.wait_ge(plus_turned, free)
                    pool.tensor_tensor(both[0:r, s.slot, 0, 0:n, :], hs[0:r, s.slot, 0:n, :],
                                       h[0:r, s.slot, 0:n, :], ALU.add).then_inc(plus_ready, 1)

                walk(pool, NG, OUT_RING, [(0, add_tables), (1, plus)], NODE_SIZES)

            @block.scalar
            def _(act):
                def norm(s):
                    r, n = s.rows, s.tiles
                    landed = s.landed()
                    free = s.ago(R)
                    act.wait_ge(x_landed[s.slot], landed)
                    if s.had(R):
                        act.wait_ge(plus_ready, free)
                        act.wait_ge(times_ready, free)
                    act.sem_inc(held, 1)
                    for j in range(n):
                        t = s.index * 4 + j
                        sc, sh = (v[0:r, t:t + 1] if s.tail else v[0:r, bass.ds(t, 1)]
                                  for v in (k["scale2"], k["shift2"]))
                        last = act.activation(h[0:r, s.slot, j, :], x2[0:r, s.slot, j, :], ACT.Relu,
                                              bias=sh, scale=sc)
                    last.then_inc(h_ready, 1)

                def evacuate(s):
                    w = s.width
                    free = s.ago(R)
                    for c, (bank, turned, ready) in enumerate(((bank_plus, plus_turned, plusT_ready),
                                                               (bank_times, times_turned, timesT_ready))):
                        act.wait_ge(turned, s.done)
                        if s.had(R) and c == 0:
                            act.wait_ge(product_ready, free)
                        act.activation(bothT[:, s.slot, c, 0:w], bank[s.bank][:, 0:w], ACT.Copy)\
                            .then_inc(ready, 1)

                walk(act, NG, OUT_RING, [(0, norm), (2, evacuate)], NODE_SIZES)

            @block.vector
            def _(dve):
                def scale_sums(s):
                    r, n = s.rows, s.tiles
                    free = s.ago(R)
                    dve.wait_ge(total_ready, s.done)
                    if s.had(R):
                        dve.wait_ge(plus_ready, free)
                    dve.tensor_tensor(hs[0:r, s.slot, 0:n, :], total[0:r, s.slot, 0:n, :],
                                      spread(cols(k["in_deg"], s, 4), D), ALU.mult).then_inc(hs_ready, 1)
                    dve.wait_ge(h_ready, s.done)
                    dve.wait_ge(hs_ready, s.done)
                    if s.had(R):
                        dve.wait_ge(times_turned, free)
                    dve.tensor_tensor(both[0:r, s.slot, 1, 0:n, :], hs[0:r, s.slot, 0:n, :],
                                      h[0:r, s.slot, 0:n, :], ALU.mult).then_inc(times_ready, 1)

                def result(s):
                    r, n = s.rows, s.tiles
                    kept = s.landed_before()
                    dve.wait_ge(product_ready, s.done)
                    if s.had(R):
                        dve.wait_ge(stored[s.slot], kept)
                    dve.tensor_tensor(res[0:r, s.slot, 0:n, :],
                                      bank_out[s.bank][0:r, 0:n * D].rearrange("p (t f) -> p t f", t=n),
                                      x2[0:r, s.slot, 0:n, :], ALU.add).then_inc(res_ready, 1)

                walk(dve, NG, OUT_RING, [(3, result), (0, scale_sums)], NODE_SIZES)

            @block.tensor
            def _(pe):
                def turn(s):
                    r = s.rows
                    free = s.ago(2)
                    for c, (bank, ready, turned, read) in enumerate((
                            (bank_times, times_ready, times_turned, timesT_ready),
                            (bank_plus, plus_ready, plus_turned, plusT_ready))):
                        pe.wait_ge(ready, s.done)
                        if s.had(2):
                            pe.wait_ge(read, free)
                        for j in range(s.tiles):
                            last = pe.transpose(bank[s.bank][:, j * r:(j + 1) * r],
                                                both[0:r, s.slot, 1 - c, j, :], k["ident"][0:r, 0:r])
                        last.then_inc(turned, 1)

                def product(s):
                    r = s.rows
                    free = s.ago(2)
                    pe.wait_ge(plusT_ready, s.done)
                    pe.wait_ge(timesT_ready, s.done)
                    if s.had(2):
                        pe.wait_ge(res_ready, free)
                    for j in range(s.tiles):
                        o = bank_out[s.bank][0:r, j * D:(j + 1) * D]
                        pe.matmul(o, bothT[:, s.slot, 0, j * r:(j + 1) * r], k["Ws"][:, :], start=True,
                                  stop=False)
                        last = pe.matmul(o, bothT[:, s.slot, 1, j * r:(j + 1) * r], k["Wi"][:, :],
                                         start=False, stop=True)
                    last.then_inc(product_ready, 1)

                walk(pe, NG, OUT_RING, [(0, turn), (1, product)], NODE_SIZES)


_INS = ["x", "src", "dst", "edge_attr_128", "L0_gnn_Wq", "L0_gnn_Wk", "L0_gnn_We", "L0_gnn_Wv",
        "L0_gnn_bn1_g", "L0_gnn_bn1_b", "L0_gnn_W1", "L0_gnn_b1", "L0_gnn_W2", "L0_gnn_b2",
        "L0_gnn_bn2_g", "L0_gnn_bn2_b", "L1_gnn_W_self", "L1_gnn_W_inter"]


def kernel(**inputs):
    import numpy as _np
    import concourse.bacc as _bacc
    from concourse import mybir as _mybir
    from concourse.bass_utils import run_bass_kernel_spmd as _run

    nc = _bacc.Bacc("TRN2", target_bir_lowering=False, num_devices=1)
    arrays, args = {}, []
    for name in _INS:
        a = _np.ascontiguousarray(inputs[name])
        arrays[f"in_{name}_dram"] = a
        args.append(nc.dram_tensor(f"in_{name}_dram", a.shape, _mybir.dt.from_np(a.dtype), kind="ExternalInput").ap())
    args.append(nc.dram_tensor("out_0_dram", (N, D), FP32, kind="ExternalOutput").ap())
    build(nc, *args)
    r = _run(nc, [arrays], core_ids=[0])
    return r.results[0]["out_0_dram"]
```

```python
import concourse.bass as bass
from concourse import mybir
from contextlib import ExitStack

FP32 = mybir.dt.float32
FP16 = mybir.dt.float16
I32 = mybir.dt.int32
ALU = mybir.AluOpType
ACT = mybir.ActivationFunctionType
AX = mybir.AxisListType

P = 128
N = 50000
D = 128
H, DH = 8, 16
EPS = 1e-5

ET = N // P
ER = N - ET * P
EU = ET // 2
NG = 97
NT = 4 * NG
NR, NRC = 112, 3
assert P * NT + NR * NRC == N and EU * 2 == ET
NC = NT + NRC
RING = 6
KEPT = 7 * RING

CLEARING = 3
HI = ET + 2

ROW = 144
WCOL, CCOL = D, D + H
USED = D + H + 1
TROWS = N + P


class Step:

    def __init__(self, eng, index, turn, slot, bank, tail, sizes, ring=1, kept=False):
        self.eng, self.index, self.turn, self.slot, self.tail = eng, index, turn, slot, tail
        self.rows, self.tiles = sizes[1] if tail else sizes[0]
        self.width = self.rows * self.tiles
        self.bank = bank
        self.first = isinstance(index, int) and index == 0
        self.done = self.value(index + 1)
        self.kept = kept
        self.had_moved = not kept and (not isinstance(index, int) or index >= KEPT + ring)
        self.moved_turn = turn - KEPT // ring

    def value(self, x):
        return x if isinstance(x, int) else self.eng.snap(x)

    def had(self, n):
        return not isinstance(self.index, int) or self.index >= n

    def ago(self, n):
        return self.value(self.index + (1 - n)) if self.had(n) else None

    def landed(self, n=1):
        return self.value(self.turn * (16 * n) + 16 * n)

    def landed_before(self, n=1):
        return self.value(self.turn * (16 * n))


    def moved(self, n=1):
        return self.value(self.moved_turn * (16 * n) + 16 * n)

    def moved_before(self, n=1):
        return self.value(self.moved_turn * (16 * n))


def walk(eng, units, ring, stages, sizes, keep=0):
    most = max(lag for lag, _ in stages)
    lap = ring if ring % 2 == 0 else 2 * ring

    def full(u):
        for lag, fn in stages:
            at = u - lag
            if 0 <= at <= units:
                fn(Step(eng, at, at // ring, at % ring, at % 2, at == units, sizes, ring, at < keep))

    def loop(first, turns, kept):
        with eng.Fori(0, turns) as i:
            for part in range(lap):
                for lag, fn in stages:
                    at = first + part - lag
                    fn(Step(eng, i * lap + at, i * (lap // ring) + at // ring, at % ring, at % 2, False,
                            sizes, ring, kept))

    start = 0
    if keep:
        start = most + ring
        for u in range(start):
            full(u)
        turns = (keep - start) // lap
        loop(start, turns, True)
        start += turns * lap
    first = keep + most + ring
    first += (units - first) % lap
    for u in range(start, first):
        full(u)
    loop(first, (units - first) // lap, False)
    for u in range(units, units + most + 1):
        full(u)


EDGE_SIZES = ((P, 2), (ER, 1))
NODE_SIZES = ((P, 4), (NR, NRC))


def edge_rows(t, s):
    if s.tail:
        return t[P * ET:N, :].rearrange("(p t) d -> p t d", t=1)
    return t[0:P * ET, :].rearrange("(p t) d -> p t d", p=P)[:, bass.ds(s.index * 2, 2), :]


def node_rows(t, s):
    if s.tail:
        return t[P * NT:N, :].rearrange("(p t) d -> p t d", p=NR)
    return t[0:P * NT, :].rearrange("(p t) d -> p t d", p=P)[:, bass.ds(s.index * 4, 4), :]


def cols(t, s, width):
    if s.tail:
        return t[0:s.rows, width * s.index:width * s.index + s.tiles]
    return t[:, bass.ds(s.index * width, width)]


def group_rows(t, s):
    return t[s.index, :, 0:s.width] if s.tail else t[bass.ds(s.index, 1), :, :].rearrange("a p n -> p (a n)")


def stat_cols(t, s):
    return t[:, s.index, :] if s.tail else t[:, bass.ds(s.index, 1), :].rearrange("p a b -> p (a b)")


def wait_stored(eng, sems, first=0):
    for i, s in enumerate(sems):
        eng.wait_ge(s, 16 * len(range(first + i, NG + 1, len(sems))))


def resident_cols(k, s):
    if isinstance(s.index, int):
        return k["resident"][:, s.index, :]
    return k["resident"][:, bass.ds(s.index, 1), :].rearrange("p a n -> p (a n)")


def resident_rows(k, s):
    return resident_cols(k, s).rearrange("p (t f) -> p t f", t=4)


def stage_semaphore(nc, ctx, name):
    sem = nc.alloc_semaphore(name)
    ctx.sems.append(sem)
    return sem


class Stage(ExitStack):

    def __init__(self, nc):
        super().__init__()
        self.nc, self.sems = nc, []

    def __exit__(self, *e):
        self.nc.clear_and_free_semaphores(self.sems)
        self.nc.all_engine_barrier()
        return super().__exit__(*e)


def spread(ap, n):
    a, b = ap.shape
    return ap.unsqueeze(2).broadcast_to([a, b, n])


def build(nc, x, src, dst, edge_attr, Wq, Wk, We, Wv, bn1_g, bn1_b, W1, b1, W2, b2, bn2_g, bn2_b,
          W_self, W_inter, out):
    ctx = ExitStack()
    with ctx:
        def sb(name, shape, dt=FP32):
            return ctx.enter_context(nc.sbuf_tensor(name, shape, dt))

        def dram(name, shape):
            return nc.dram_tensor(name, shape, FP32, kind="Internal").ap()

        k = {}
        k["bank"] = [ctx.enter_context(nc.psum_tensor(f"bank{i}", [P, 512], FP32)) for i in range(8)]
        k["table"] = dram("table", (TROWS, ROW))
        k["sums"] = [dram(f"sums{i}", (TROWS, D)) for i in range(2)]
        k["h1T"] = dram("h1T", (NG + 1, P, 512))
        k["zT"] = dram("zT", (NG + 1, P, 512))
        k["x2"] = dram("x2", (N, D))
        k["g"] = dram("g", (N, D))
        k["degree"] = dram("degree", (ET + 1, P))

        k["ident"] = sb("ident", [P, P])
        k["Wkv"] = sb("Wkv", [P, 2 * D])
        k["Wq"] = sb("Wq", [P, D])
        k["We"] = sb("We", [P, D])
        k["W1"] = sb("W1", [P, 2 * D])
        k["W2"] = sb("W2", [P, 2, D])
        k["Ws"] = sb("Ws", [P, D])
        k["Wi"] = sb("Wi", [P, D])
        k["b1"] = sb("b1", [P, 2])
        for name in ("b2", "g1", "be1", "g2", "be2", "eps"):
            k[name] = sb(name, [P, 1])
        k["dst_f"] = sb("dst_f", [P, ET + 1])
        k["ends"] = sb("ends", [P, ET + 1, 2], I32)
        k["target"] = sb("target", [P, ET + 1], I32)
        k["in_deg"] = sb("in_deg", [P, NC])
        k["out_deg"] = sb("out_deg", [P, NC])
        k["scale2"] = sb("scale2", [P, NC])
        k["shift2"] = sb("shift2", [P, NC])
        k["resident"] = sb("resident", [P, KEPT, 512])
        k["bn1"] = sb("bn1", [P, NG + 1, 6])
        k["bn2"] = sb("bn2", [P, NG + 1, 6])

        edge_stages(nc, k, x, src, dst, edge_attr, Wq, Wk, We, Wv, bn1_g, bn1_b, W1, b1, W2, b2, bn2_g,
                    bn2_b, W_self, W_inter)
        residual_stage(nc, k, x)
        mlp_stage(nc, k)
        normed_stage(nc, k, x)
        convolution_stage(nc, k)
        output_stage(nc, k, out)


def edge_stages(nc, k, x, src, dst, edge_attr, Wq, Wk, We, Wv, bn1_g, bn1_b, W1, b1, W2, b2, bn2_g,
                bn2_b, W_self, W_inter):
    ctx = Stage(nc)
    with ctx:
        def sb(name, shape, dt=FP32):
            return ctx.enter_context(nc.sbuf_tensor(name, shape, dt))

        def sem(name):
            return stage_semaphore(nc, ctx, name)

        table, ident, dst_f, ends, target = k["table"], k["ident"], k["dst_f"], k["ends"], k["target"]
        src_i = sb("src_i", [P, ET + 1], I32)
        dst_i = sb("dst_i", [P, ET + 1], I32)
        bits = sb("bits", [P, ET + 1], I32)
        src_lo = sb("src_lo", [P, ET + 1])
        src_hi = sb("src_hi", [P, ET + 1])
        spare = sb("spare", [P, ET + 1])
        spare_row = sb("spare_row", [P, 1])
        count_i = sb("count_i", [P, HI], I32)
        count_h = sb("count_h", [P, HI], FP16)
        prow_i = sb("prow_i", [P, 1], I32)
        before = sb("before", [P, P])
        ones = sb("ones", [P, P])
        zero_cols = 2169
        pieces = TROWS * ROW // P // zero_cols
        assert pieces % 2 == 0 and pieces * zero_cols * P == TROWS * ROW
        zeros = sb("zeros", [P, zero_cols])

        index = sb("index", [P, 2, 2, 2], I32)
        rows_in = sb("rows_in", [P, 2, 2, 2, D])
        attr = sb("attr", [P, 2, 2, D])
        stat = sb("stat", [P, 2, 4, 6])
        mv = sb("mv", [P, 2, 4, 2])
        negmean = sb("negmean", [P, 2, 4])
        lnvar = sb("lnvar", [P, 2, 4])
        rstd = sb("rstd", [P, 2, 4])
        rr = sb("rr", [P, 2, 2])
        dst_now = sb("dst_now", [P, 2, 2])
        h = sb("h", [P, 2, 4, D])
        hT = sb("hT", [P, 2, 4, P])
        attrT = sb("attrT", [P, 2, 2, P])
        q = sb("q", [P, 2, 2, D])
        kq = sb("kq", [P, 2, D])
        kqe = sb("kqe", [P, 2, D])
        raw = sb("raw", [P, 2, H])
        scaled = sb("scaled", [P, 2, H])
        clipped = sb("clipped", [P, 2, H])
        wr = sb("wr", [P, 2, H])
        message = sb("message", [P, 2, 2, ROW])
        same = sb("same", [P, 2, 2, P])
        earlier = sb("earlier", [P, 2, P])
        rank = sb("rank", [P, 2])
        move = sb("move", [P, 2])
        hot_lo = sb("hot_lo", [P, 2, 2, P], FP16)
        hot_hi = sb("hot_hi", [P, 2, 2, HI], FP16)
        group = sb("group", [P, 2, 2, ROW])
        add_at = sb("add_at", [P, 2, 2], I32)
        hist = sb("hist", [P, HI])
        histT = sb("histT", [P, 4, P])

        loaded, const_ready = sem("loaded"), sem("const_ready")
        cleared = [sem(f"cleared{i}") for i in range(2)]
        prep, zeros_ready = sem("prep"), sem("zeros_ready")
        index_ready = sem("index_ready")
        landed = [sem(f"landed{i}") for i in range(2)]
        attr_landed = [sem(f"attr_landed{i}") for i in range(2)]
        stats_ready, mv_ready, negmean_ready = sem("stats_ready"), sem("mv_ready"), sem("negmean_ready")
        ln_ready, rstd_ready, h_ready = sem("ln_ready"), sem("rstd_ready"), sem("h_ready")
        turned, attr_turned, dst_turned = sem("turned"), sem("attr_turned"), sem("dst_turned")
        hT_ready, attrT_ready = sem("hT_ready"), sem("attrT_ready")
        same_ready, rank_ready = sem("same_ready"), sem("rank_ready")
        move_ready, target_ready = sem("move_ready"), sem("target_ready")
        hot_ready, counted = sem("hot_ready"), sem("counted")
        products_ready, q_ready = sem("products_ready"), sem("q_ready")
        kq_ready, kqe_ready, raw_ready = sem("kq_ready"), sem("kqe_ready"), sem("raw_ready")
        rr_ready, scaled_ready, clipped_ready = sem("rr_ready"), sem("scaled_ready"), sem("clipped_ready")
        weight_ready, wr_ready, message_ready = sem("weight_ready"), sem("wr_ready"), sem("message_ready")
        grouped, group_ready = sem("grouped"), sem("group_ready")
        rows_added, held = sem("rows_added"), sem("held")
        sums_cleared, weights_loaded = sem("sums_cleared"), sem("weights_loaded")
        hist_ready, hist_turned, histT_ready, degree_stored = (
            sem("hist_ready"), sem("hist_turned"), sem("histT_ready"), sem("degree_stored"))

        bank = k["bank"]
        bank_rows, bank_turned, bank_hist, bank_group = bank[0:4]
        rowsT = bank_rows[:, :].rearrange("p (a e) -> p a e", a=4)
        attr_ps = bank_turned[:, 0:2 * P].rearrange("p (a e) -> p a e", a=2)
        dst_ps = bank_turned[:, 2 * P:4 * P].rearrange("p (a e) -> p a e", a=2)
        kv = [b[:, :].rearrange("p (t a f) -> p t a f", t=2, a=2) for b in bank[4:6]]
        qe = [b[:, :].rearrange("p (t a f) -> p t a f", t=2, a=2) for b in bank[6:8]]
        grp = bank_group[:, 0:2 * ROW].rearrange("p (t f) -> p t f", t=2)
        hist_ps = bank_hist[:, 0:HI]
        histT_ps = bank_rows[:, :].rearrange("p (a e) -> p a e", a=4)

        weight_loads = [
            (k["Wkv"][:, 0:D], Wk), (k["Wkv"][:, D:2 * D], Wv), (k["Wq"][:, :], Wq), (k["We"][:, :], We),
            (k["W1"][:, :], W1), (k["W2"][:, :, :], W2.rearrange("(c p) n -> p c n", p=P)),
            (k["Ws"][:, :], W_self), (k["Wi"][:, :], W_inter),
        ] + [(k["b1"][:, c:c + 1], b1[c * D:(c + 1) * D].rearrange("(p o) -> p o", o=1)) for c in range(2)
        ] + [(k[name][:, :], v.rearrange("(p o) -> p o", o=1)) for name, v in
             (("b2", b2), ("g1", bn1_g), ("be1", bn1_b), ("g2", bn2_g), ("be2", bn2_b))]
        index_loads = [
            (t[:, 0:ET], v[0:P * ET].rearrange("(p t) -> p t", p=P)) for t, v in ((src_i, src), (dst_i, dst))
        ] + [(t[0:ER, ET:ET + 1], v[P * ET:N].rearrange("(p t) -> p t", t=1))
             for t, v in ((src_i, src), (dst_i, dst))]

        def clear_piece(sp, c):
            flat = table.rearrange("r f -> (r f)").rearrange("(p c n) -> p c n", p=P, n=zero_cols)
            sp.dma_start(flat[:, c, :], zeros[:, :]).then_inc(cleared[c % 2], 16)

        with nc.Block() as block:
            @block.sync
            def _(sp):
                for to, of in index_loads:
                    sp.dma_start(to, of).then_inc(loaded, 16)
                sp.wait_ge(zeros_ready, 1)
                for c in range(2):
                    clear_piece(sp, c)

            @block.gpsimd
            def _(pool):
                nc.gpsimd.iota(count_i[:, :], pattern=[[1, HI]], base=0, channel_multiplier=0)\
                    .then_inc(const_ready, 1)
                nc.gpsimd.iota(prow_i[:, :], pattern=[[1, 1]], base=N, channel_multiplier=1)\
                    .then_inc(const_ready, 1)
                pool.wait_ge(prep, 1)
                nc.gpsimd.affine_select(out=ident[:, :], in_=ones[:, :], compare_op=ALU.is_equal, fill=0.0,
                                        base=0, pattern=[[-1, P]], channel_multiplier=1)\
                    .then_inc(const_ready, 1)
                nc.gpsimd.affine_select(out=before[:, :], in_=ones[:, :], compare_op=ALU.is_gt, fill=0.0,
                                        base=0, pattern=[[-1, P]], channel_multiplier=1)\
                    .then_inc(const_ready, 1)

            @block.scalar
            def _(act):
                for to, of in weight_loads:
                    act.dma_start(to, of).then_inc(weights_loaded, 16)
                act.wait_ge(weights_loaded, 16 * len(weight_loads))

            @block.vector
            def _(dve):
                dve.memset(zeros[:, :], 0.0).then_inc(zeros_ready, 1)
                dve.memset(ones[:, :], 1.0).then_inc(prep, 1)
                dve.memset(message[:, :, :, USED:ROW], 0.0).then_inc(prep, 1)
                dve.memset(message[:, :, :, CCOL:CCOL + 1], 1.0).then_inc(prep, 1)
                dve.memset(k["eps"][:, :], EPS).then_inc(prep, 1)
                dve.wait_ge(const_ready, 2)
                dve.tensor_copy(count_h[:, :], count_i[:, :])
                dve.tensor_copy(spare_row[:, :], prow_i[:, :]).then_inc(prep, 1)
                dve.wait_ge(loaded, 16 * len(index_loads))
                for rows, c0, c1 in ((P, 0, ET), (ER, ET, ET + 1)):
                    a = slice(0, rows), slice(c0, c1)
                    dve.tensor_copy(ends[a[0], a[1], 0], src_i[a])
                    dve.tensor_copy(ends[a[0], a[1], 1], dst_i[a])
                    dve.tensor_copy(dst_f[a], dst_i[a])
                    dve.tensor_scalar(bits[a], src_i[a], P - 1, None, ALU.bitwise_and).then_inc(prep, 1)
                dve.wait_ge(prep, 7)
                for rows, c0, c1 in ((P, 0, ET), (ER, ET, ET + 1)):
                    a = slice(0, rows), slice(c0, c1)
                    dve.tensor_copy(src_lo[a], bits[a])
                    dve.tensor_scalar(spare[a], dst_f[a], -1.0, spare_row[0:rows, :], ALU.mult, ALU.add)\
                        .then_inc(prep, 1)
                dve.wait_ge(prep, 9)
                for rows, c0, c1 in ((P, 0, ET), (ER, ET, ET + 1)):
                    a = slice(0, rows), slice(c0, c1)
                    dve.tensor_scalar(bits[a], src_i[a], 7, None, ALU.logical_shift_right).then_inc(prep, 1)
                dve.wait_ge(prep, 11)
                for rows, c0, c1 in ((P, 0, ET), (ER, ET, ET + 1)):
                    a = slice(0, rows), slice(c0, c1)
                    dve.tensor_copy(src_hi[a], bits[a]).then_inc(prep, 1)

        with nc.Block() as block:
            @block.sync
            def _(sp):
                def load_attr(s):
                    free = s.ago(2)
                    if s.had(2):
                        sp.wait_ge(attr_turned, free)
                    sp.dma_start(attr[0:s.rows, s.slot, 0:s.tiles, :], edge_rows(edge_attr, s))\
                        .then_inc(attr_landed[s.slot], 16)

                def clear_table(s):
                    if not isinstance(s.index, int) or s.index >= CLEARING:
                        return
                    for c in range(max(2, s.index * pieces // CLEARING), (s.index + 1) * pieces // CLEARING):
                        sp.wait_ge(cleared[c % 2], 16 * (c // 2))
                        clear_piece(sp, c)

                def clear_sums(s):
                    rows, parts = (TROWS - 2 * P * EU, (TROWS - 2 * P * EU) // 2) if s.tail else (2 * P, P)
                    r0 = s.value(s.index * (2 * P))
                    for t in k["sums"]:
                        part = t[r0:r0 + rows, :] if s.tail else t[bass.ds(r0, rows), :]
                        sp.dma_start(part.rearrange("(p r) d -> p (r d)", r=2), zeros[0:parts, 0:2 * D])\
                            .then_inc(sums_cleared, 16)

                walk(sp, EU, 2, [(0, load_attr), (0, clear_table), (0, clear_sums)], EDGE_SIZES)
                sp.wait_ge(sums_cleared, 32 * (EU + 1))

            @block.gpsimd
            def _(pool):
                def hold(*waits):
                    for sem_, value in waits:
                        pool.wait_ge(sem_, value)
                    pool.sem_inc(held, 1)

                def gather(s, j):
                    for end in range(2):
                        pool.indirect_dma_start(
                            rows_in[0:s.rows, s.slot, j, end, :], None, x,
                            bass.IndirectOffsetOnAxis(index[0:s.rows, s.slot, j, end:end + 1], 0))\
                            .then_inc(landed[s.slot], 16)

                def add(s, j):
                    pool.indirect_dma_start(
                        table, bass.IndirectOffsetOnAxis(add_at[0:s.rows, s.slot, j:j + 1], 0),
                        group[0:s.rows, s.slot, j, :], None, compute_op=ALU.add).then_inc(rows_added, 16)

                def gather_first(s):
                    free = s.ago(2)
                    waits = [(index_ready, s.done)]
                    if s.had(2):
                        waits.append((h_ready, free))
                    hold(*waits)
                    gather(s, 0)

                def gather_second(s):
                    if s.tiles > 1:
                        gather(s, 1)

                def add_first(s):
                    last = s.value(s.index * 32)
                    waits = [(group_ready, s.done)]
                    if s.first:
                        waits += [(sem_, 16 * (pieces // 2)) for sem_ in cleared]
                    else:
                        waits.append((rows_added, last))
                    hold(*waits)
                    add(s, 0)

                def add_second(s):
                    last = s.value(s.index * 32 + 16)
                    if s.tiles > 1:
                        hold((rows_added, last))
                        add(s, 1)

                walk(pool, EU, 2, [(0, gather_first), (4, add_first), (0, gather_second), (4, add_second)],
                     EDGE_SIZES)
                pool.wait_ge(rows_added, 32 * EU + 16)

            @block.vector
            def _(dve):
                def hold(*waits):
                    for sem_, value in waits:
                        dve.wait_ge(sem_, value)
                    dve.sem_inc(held, 1)

                def make_index(s):
                    landed_value = s.value(s.turn * 64)
                    if s.had(2):
                        hold((landed[s.slot], landed_value))
                    t0 = s.index * 2
                    part = (ends[0:s.rows, t0:t0 + s.tiles, :] if s.tail
                            else ends[:, bass.ds(t0, 2), :])
                    dve.tensor_copy(index[0:s.rows, s.slot, 0:s.tiles, :], part).then_inc(index_ready, 1)

                def stats(s):
                    full = s.value(s.turn * 64 + (32 if s.tail else 64))
                    dve.wait_ge(landed[s.slot], full)
                    for a in range(2 * s.tiles):
                        last = dve.bn_stats(stat[0:s.rows, s.slot, a, :],
                                            rows_in[0:s.rows, s.slot, a // 2, a % 2, :])
                    last.then_inc(stats_ready, 1)

                def mean_var(s):
                    n, r = 2 * s.tiles, s.rows
                    hold((stats_ready, s.done))
                    for a in range(n):
                        last = dve.bn_aggr(mv[0:r, s.slot, a, :], stat[0:r, s.slot, a, :])
                    last.then_inc(mv_ready, 1)
                    dve.tensor_copy(dst_now[0:r, s.slot, 0:s.tiles], cols(dst_f, s, 2))
                    dve.wait_ge(mv_ready, s.done)
                    dve.tensor_scalar(negmean[0:r, s.slot, 0:n], mv[0:r, s.slot, 0:n, 0], -1.0, None,
                                      ALU.mult).then_inc(negmean_ready, 1)

                def score_and_compare(s):
                    r, n = s.rows, s.tiles
                    free, next_turned = s.ago(2), s.value(s.index + 2)
                    dve.wait_ge(dst_turned, s.done)
                    if not s.tail:
                        dve.wait_ge(attr_turned, next_turned)
                    if s.had(2):
                        dve.wait_ge(grouped, free)
                    dve.tensor_tensor(same[0:r, s.slot, 0:n, 0:r], dst_ps[0:r, 0:n, 0:r],
                                      spread(cols(dst_f, s, 2), r), ALU.is_equal).then_inc(same_ready, 1)
                    dve.wait_ge(q_ready, s.done)
                    dve.tensor_tensor(kq[0:r, 0:n, :], kv[s.slot][0:r, 0:n, 0, :], q[0:r, s.slot, 0:n, :],
                                      ALU.mult).then_inc(kq_ready, 1)
                    dve.wait_ge(same_ready, s.done)
                    for j in range(n):
                        last = dve.tensor_tensor_reduce(
                            out=earlier[0:r, j, 0:r], in0=same[0:r, s.slot, j, 0:r], in1=before[0:r, 0:r],
                            scale=1.0, scalar=0.0, op0=ALU.mult, op1=ALU.add, accum_out=rank[0:r, j:j + 1])
                    last.then_inc(rank_ready, 1)
                    dve.wait_ge(kq_ready, s.done)
                    dve.tensor_tensor(kqe[0:r, 0:n, :], kq[0:r, 0:n, :], qe[s.slot][0:r, 0:n, 1, :],
                                      ALU.mult).then_inc(kqe_ready, 1)
                    dve.wait_ge(rank_ready, s.done)
                    dve.scalar_tensor_tensor(move[0:r, 0:n], rank[0:r, 0:n], 0.0, cols(spare, s, 2),
                                             ALU.is_gt, ALU.mult).then_inc(move_ready, 1)
                    dve.wait_ge(rstd_ready, s.done)
                    rs = rstd[0:r, s.slot, 0:2 * n].rearrange("p (t a) -> p t a", a=2)
                    dve.tensor_tensor(rr[0:r, s.slot, 0:n], rs[:, :, 0], rs[:, :, 1], ALU.mult)\
                        .then_inc(rr_ready, 1)
                    dve.wait_ge(kqe_ready, s.done)
                    dve.tensor_reduce(raw[0:r, 0:n, :],
                                      kqe[0:r, 0:n, :].rearrange("p t (h d) -> p t h d", h=H), AX.X,
                                      ALU.add).then_inc(raw_ready, 1)
                    dve.wait_ge(move_ready, s.done)
                    dve.tensor_tensor(cols(target, s, 2), move[0:r, 0:n], cols(dst_f, s, 2), ALU.add)\
                        .then_inc(target_ready, 1)
                    dve.wait_ge(rr_ready, s.done)
                    dve.wait_ge(raw_ready, s.done)
                    dve.tensor_tensor(scaled[0:r, 0:n, :], raw[0:r, 0:n, :], spread(rr[0:r, s.slot, 0:n], H),
                                      ALU.mult).then_inc(scaled_ready, 1)
                    dve.wait_ge(scaled_ready, s.done)
                    dve.tensor_scalar(clipped[0:r, 0:n, :], scaled[0:r, 0:n, :], 5.0, -5.0, ALU.min, ALU.max)\
                        .then_inc(clipped_ready, 1)

                def messages(s):
                    r, n = s.rows, s.tiles
                    slot_added = s.value(s.index * 32 - 32)
                    t0 = s.index * 2
                    dve.wait_ge(weight_ready, s.done)
                    if s.had(2):
                        dve.wait_ge(rows_added, slot_added)
                    rs = rstd[0:r, s.slot, 0:2 * n].rearrange("p (t a) -> p t a", a=2)
                    dve.tensor_tensor(wr[0:r, 0:n, :], message[0:r, s.slot, 0:n, WCOL:WCOL + H],
                                      spread(rs[:, :, 0], H), ALU.mult).then_inc(wr_ready, 1)
                    hold((target_ready, s.done))
                    part = (target[0:r, t0:t0 + n] if s.tail else target[:, bass.ds(t0, 2)])
                    dve.tensor_copy(add_at[0:r, s.slot, 0:n], part)
                    dve.wait_ge(wr_ready, s.done)
                    for j in range(n):
                        last = dve.tensor_tensor(
                            message[0:r, s.slot, j, 0:D].rearrange("p (h d) -> p h d", h=H),
                            kv[s.slot][0:r, j, 1, :].rearrange("p (h d) -> p h d", h=H),
                            spread(wr[0:r, j, :], DH), ALU.mult)
                    last.then_inc(message_ready, 1)

                def one_hots(s):
                    r = s.rows
                    free = s.ago(2)
                    if s.had(2):
                        dve.wait_ge(counted, free)
                        dve.sem_inc(held, 1)
                    for j in range(s.tiles):
                        t = s.index * 2 + j
                        lo = src_lo[0:r, t:t + 1] if s.tail else src_lo[0:r, bass.ds(t, 1)]
                        hi = src_hi[0:r, t:t + 1] if s.tail else src_hi[0:r, bass.ds(t, 1)]
                        dve.tensor_scalar(hot_lo[0:r, s.slot, j, :], count_h[0:r, 0:P], lo, None,
                                          ALU.is_equal)
                        last = dve.tensor_scalar(hot_hi[0:r, s.slot, j, :], count_h[0:r, :], hi, None,
                                                 ALU.is_equal)
                    last.then_inc(hot_ready, 1)

                walk(dve, EU, 2, [(4, score_and_compare), (2, stats), (2, one_hots), (4, messages),
                                  (2, mean_var), (0, make_index)], EDGE_SIZES)
                dve.wait_ge(counted, EU + 1)
                dve.tensor_copy(hist[:, :], hist_ps).then_inc(hist_ready, 1)
                dve.wait_ge(hist_turned, 1)
                for c in range(4):
                    w = min(P, ET + 1 - c * P)
                    last = dve.tensor_copy(histT[0:w, c, :], histT_ps[0:w, c, :])
                last.then_inc(histT_ready, 1)

            @block.scalar
            def _(act):
                act.preload_act_table_set("natural_log_exp_and_others")

                def queries(s):
                    r, n = s.rows, s.tiles
                    act.wait_ge(products_ready, s.done)
                    act.activation(q[0:r, s.slot, 0:n, :], qe[s.slot][0:r, 0:n, 0, :], ACT.Copy,
                                   scale=float(DH) ** -0.5).then_inc(q_ready, 1)

                def norm(s):
                    r, n = s.rows, 2 * s.tiles
                    act.wait_ge(negmean_ready, s.done)
                    for a in range(n):
                        last = act.activation(h[0:r, s.slot, a, :], rows_in[0:r, s.slot, a // 2, a % 2, :],
                                              ACT.Relu, bias=negmean[0:r, s.slot, a:a + 1])
                    last.then_inc(h_ready, 1)
                    act.activation(lnvar[0:r, s.slot, 0:n], mv[0:r, s.slot, 0:n, 1], ACT.Ln,
                                   bias=k["eps"][0:r, :]).then_inc(ln_ready, 1)
                    act.wait_ge(ln_ready, s.done)
                    act.activation(rstd[0:r, s.slot, 0:n], lnvar[0:r, s.slot, 0:n], ACT.Exp, scale=-0.5)\
                        .then_inc(rstd_ready, 1)

                def weights(s):
                    r, n = s.rows, s.tiles
                    act.wait_ge(clipped_ready, s.done)
                    act.activation(message[0:r, s.slot, 0:n, WCOL:WCOL + H], clipped[0:r, 0:n, :], ACT.Exp)\
                        .then_inc(weight_ready, 1)

                def evacuate(s):
                    r, n = s.rows, s.tiles
                    prev = s.ago(1)
                    act.wait_ge(attr_turned, s.done)
                    if not s.first:
                        act.wait_ge(same_ready, prev)
                    act.activation(attrT[:, s.slot, 0:n, 0:r], attr_ps[:, 0:n, 0:r], ACT.Copy)\
                        .then_inc(attrT_ready, 1)
                    act.wait_ge(turned, s.done)
                    act.activation(hT[:, s.slot, 0:2 * n, 0:r], rowsT[:, 0:2 * n, 0:r], ACT.Copy)\
                        .then_inc(hT_ready, 1)

                def group_sums(s):
                    r, n = s.rows, s.tiles
                    act.wait_ge(grouped, s.done)
                    act.activation(group[0:r, s.slot, 0:n, :], grp[0:r, 0:n, :], ACT.Copy)\
                        .then_inc(group_ready, 1)

                walk(act, EU, 2, [(0, norm), (2, group_sums), (0, evacuate), (1, weights), (0, queries)],
                     EDGE_SIZES)
                act.wait_ge(histT_ready, 1)
                for c in range(4):
                    w = min(P, ET + 1 - c * P)
                    act.dma_start(k["degree"][c * P:c * P + w, :], histT[0:w, c, :])\
                        .then_inc(degree_stored, 16)
                act.wait_ge(degree_stored, 64)

            @block.tensor
            def _(pe):
                def turn_dst(s):
                    r = s.rows
                    prev = s.ago(1)
                    pe.wait_ge(negmean_ready, s.done)
                    pe.wait_ge(attrT_ready, s.done)
                    if not s.first:
                        pe.wait_ge(same_ready, prev)
                    for j in range(s.tiles):
                        last = pe.transpose(dst_ps[:, j, 0:r],
                                            dst_now[0:r, s.slot, j:j + 1].broadcast_to([r, P]),
                                            ident[0:r, 0:r])
                    last.then_inc(dst_turned, 1)

                def turn(s):
                    r, n = s.rows, s.tiles
                    full, prev = s.landed(), s.ago(1)
                    pe.wait_ge(attr_landed[s.slot], full)
                    for j in range(n):
                        last = pe.transpose(attr_ps[:, j, 0:r], attr[0:r, s.slot, j, :], ident[0:r, 0:r])
                    last.then_inc(attr_turned, 1)
                    pe.wait_ge(h_ready, s.done)
                    if not s.first:
                        pe.wait_ge(hT_ready, prev)
                    for a in range(2 * n):
                        last = pe.transpose(rowsT[:, a, 0:r], h[0:r, s.slot, a, :], ident[0:r, 0:r])
                    last.then_inc(turned, 1)

                def product(s):
                    r = s.rows
                    free = s.ago(2)
                    pe.wait_ge(hT_ready, s.done)
                    pe.wait_ge(attrT_ready, s.done)
                    if s.had(2):
                        pe.wait_ge(message_ready, free)
                    for j in range(s.tiles):
                        pe.matmul(kv[s.slot][0:r, j, :, :].rearrange("p a f -> p (a f)"), hT[:, s.slot, 2 * j, 0:r],
                                  k["Wkv"][:, :], start=True, stop=True)
                        pe.matmul(qe[s.slot][0:r, j, 0, :], hT[:, s.slot, 2 * j + 1, 0:r], k["Wq"][:, :],
                                  start=True, stop=True)
                        last = pe.matmul(qe[s.slot][0:r, j, 1, :], attrT[:, s.slot, j, 0:r], k["We"][:, :],
                                         start=True, stop=True)
                    last.then_inc(products_ready, 1)

                def group_up(s):
                    r = s.rows
                    prev = s.ago(1)
                    pe.wait_ge(message_ready, s.done)
                    if not s.first:
                        pe.wait_ge(group_ready, prev)
                    for j in range(s.tiles):
                        last = pe.matmul(grp[0:r, j, :], same[0:r, s.slot, j, 0:r],
                                         message[0:r, s.slot, j, :], start=True, stop=True)
                    last.then_inc(grouped, 1)

                def count(s):
                    r = s.rows
                    pe.wait_ge(hot_ready, s.done)
                    for j in range(s.tiles):
                        last = pe.matmul(hist_ps, hot_lo[0:r, s.slot, j, :], hot_hi[0:r, s.slot, j, :],
                                         start=s.first and j == 0, stop=s.tail)
                    last.then_inc(counted, 1)

                walk(pe, EU, 2, [(2, group_up), (1, turn_dst), (0, turn), (0, product), (0, count)],
                     EDGE_SIZES)
                pe.wait_ge(hist_ready, 1)
                pe.wait_ge(hT_ready, EU + 1)
                for c in range(4):
                    w = min(P, ET + 1 - c * P)
                    last = pe.transpose(histT_ps[0:w, c, :], hist[:, c * P:c * P + w], ident[:, :])
                last.then_inc(hist_turned, 1)


def norm_constants(k, act, dve, stats, gamma, beta, tiles, sems):
    mean_var, logvar, std_inv, scale, shift = tiles
    aggregated, logged, inverted, scaled, shift_ready = sems

    def on_act():
        act.wait_ge(aggregated, 1)
        act.activation(logvar[:, :], mean_var[:, 1:2], ACT.Ln, bias=k["eps"][:, :]).then_inc(logged, 1)
        act.wait_ge(logged, 1)
        act.activation(std_inv[:, :], logvar[:, :], ACT.Exp, scale=-0.5).then_inc(inverted, 1)

    def on_dve():
        dve.bn_aggr(mean_var[:, :], stats[:, :, :].rearrange("p a b -> p (a b)")).then_inc(aggregated, 1)
        dve.wait_ge(inverted, 1)
        dve.tensor_tensor(scale[:, :], std_inv[:, :], gamma[:, :], ALU.mult).then_inc(scaled, 1)
        dve.wait_ge(scaled, 1)
        dve.tensor_tensor(logvar[:, :], mean_var[:, 0:1], scale[:, :], ALU.mult).then_inc(scaled, 1)
        dve.wait_ge(scaled, 2)
        dve.tensor_tensor(shift[:, :], beta[:, :], logvar[:, :], ALU.subtract).then_inc(shift_ready, 1)

    return on_act, on_dve


def residual_stage(nc, k, x):
    ctx = Stage(nc)
    with ctx:
        def sb(name, shape, dt=FP32):
            return ctx.enter_context(nc.sbuf_tensor("b_" + name, shape, dt))

        def sem(name):
            return stage_semaphore(nc, ctx, "b_" + name)

        R = RING
        xg = sb("xg", [P, R, 4, D])
        acc = sb("acc", [P, R, 4, ROW])
        stat = sb("stat", [P, R, 4, 6])
        mv = sb("mv", [P, R, 4, 2])
        lnvar = sb("lnvar", [P, R, 4])
        rstd = sb("rstd", [P, R, 4])
        shift = sb("shift", [P, R, 4])
        h = sb("h", [P, R, 4, D])
        weight = sb("weight", [P, R, 4, H])
        weight_inv = sb("weight_inv", [P, R, 4, H])
        attn = sb("attn", [P, R, 4, D])
        h1 = sb("h1", [P, R, 4, D])
        h1T = sb("h1T", [P, R, 512])

        x_landed = [sem(f"x_landed{i}") for i in range(R)]
        acc_landed = [sem(f"acc_landed{i}") for i in range(R)]
        h1T_stored = [sem(f"h1T_stored{i}") for i in range(R)]
        stats_ready, mv_ready, ln_ready, rstd_ready = (
            sem("stats_ready"), sem("mv_ready"), sem("ln_ready"), sem("rstd_ready"))
        shift_ready, h_ready = sem("shift_ready"), sem("h_ready")
        weight_ready, inv_ready, attn_ready = sem("weight_ready"), sem("inv_ready"), sem("attn_ready")
        h1_ready, turned, h1T_ready, h1T_measured = (
            sem("h1_ready"), sem("turned"), sem("h1T_ready"), sem("h1T_measured"))
        held, act_held = sem("held"), sem("act_held")
        banks = k["bank"][0:2]

        with nc.Block() as block:
            @block.sync
            def _(sp):
                def load(s):
                    free = s.ago(R)
                    if s.had(R):
                        sp.wait_ge(h_ready, free)
                    sp.dma_start(xg[0:s.rows, s.slot, 0:s.tiles, :], node_rows(x, s))\
                        .then_inc(x_landed[s.slot], 16)
                    if s.had(R):
                        sp.wait_ge(attn_ready, free)
                    sp.dma_start(acc[0:s.rows, s.slot, 0:s.tiles, :], node_rows(k["table"], s))\
                        .then_inc(acc_landed[s.slot], 16)

                def store(s):
                    if s.kept:
                        return
                    sp.wait_ge(h1T_ready, s.done)
                    sp.dma_start(group_rows(k["h1T"], s), h1T[:, s.slot, 0:s.width])\
                        .then_inc(h1T_stored[s.slot], 16)

                walk(sp, NG, R, [(0, load), (5, store)], NODE_SIZES, KEPT)
                wait_stored(sp, h1T_stored, KEPT)

            @block.gpsimd
            def _(pool):
                def residual(s):
                    r, n = s.rows, s.tiles
                    free = s.ago(R)
                    pool.wait_ge(inv_ready, s.done)
                    pool.tensor_tensor(
                        attn[0:r, s.slot, 0:n, :].rearrange("p t (h d) -> p t h d", h=H),
                        acc[0:r, s.slot, 0:n, 0:D].rearrange("p t (h d) -> p t h d", h=H),
                        weight_inv[0:r, s.slot, 0:n, :].unsqueeze(3).broadcast_to([r, n, H, DH]), ALU.mult)\
                        .then_inc(attn_ready, 1)
                    pool.wait_ge(h_ready, s.done)
                    pool.wait_ge(attn_ready, s.done)
                    if s.had(R):
                        pool.wait_ge(turned, free)
                    pool.tensor_tensor(h1[0:r, s.slot, 0:n, :], h[0:r, s.slot, 0:n, :],
                                       attn[0:r, s.slot, 0:n, :], ALU.add).then_inc(h1_ready, 1)

                walk(pool, NG, R, [(0, residual)], NODE_SIZES)

            @block.vector
            def _(dve):
                def stats(s):
                    r, n = s.rows, s.tiles
                    full, free = s.landed(), s.ago(R)
                    dve.wait_ge(acc_landed[s.slot], full)
                    if s.had(R):
                        dve.wait_ge(attn_ready, free)
                    dve.tensor_scalar(weight[0:r, s.slot, 0:n, :], acc[0:r, s.slot, 0:n, WCOL:WCOL + H],
                                      1e-6, None, ALU.add).then_inc(weight_ready, 1)
                    dve.wait_ge(x_landed[s.slot], full)
                    for j in range(n):
                        last = dve.bn_stats(stat[0:r, s.slot, j, :], xg[0:r, s.slot, j, :])
                    last.then_inc(stats_ready, 1)
                    dve.wait_ge(weight_ready, s.done)
                    dve.reciprocal(weight_inv[0:r, s.slot, 0:n, :], weight[0:r, s.slot, 0:n, :])\
                        .then_inc(inv_ready, 1)
                    dve.wait_ge(stats_ready, s.done)
                    dve.sem_inc(held, 1)
                    dve.tensor_copy(cols(k["in_deg"], s, 4), acc[0:r, s.slot, 0:n, CCOL])
                    for j in range(n):
                        last = dve.bn_aggr(mv[0:r, s.slot, j, :], stat[0:r, s.slot, j, :])
                    last.then_inc(mv_ready, 1)

                def norm_shift(s):
                    r, n = s.rows, s.tiles
                    dve.wait_ge(rstd_ready, s.done)
                    dve.scalar_tensor_tensor(shift[0:r, s.slot, 0:n], mv[0:r, s.slot, 0:n, 0], -1.0,
                                             rstd[0:r, s.slot, 0:n], ALU.mult, ALU.mult)\
                        .then_inc(shift_ready, 1)

                def measure(s):
                    dve.wait_ge(h1T_ready, s.done)
                    if not s.tail:
                        dve.sem_inc(held, 1)
                    of = resident_cols(k, s) if s.kept else h1T[:, s.slot, 0:s.width]
                    dve.bn_stats(stat_cols(k["bn1"], s), of).then_inc(h1T_measured, 1)

                walk(dve, NG, R, [(1, norm_shift), (0, stats), (4, measure)], NODE_SIZES, KEPT)

            @block.scalar
            def _(act):
                def norm_scale(s):
                    r, n = s.rows, s.tiles
                    act.wait_ge(mv_ready, s.done)
                    act.activation(lnvar[0:r, s.slot, 0:n], mv[0:r, s.slot, 0:n, 1], ACT.Ln,
                                   bias=k["eps"][0:r, :]).then_inc(ln_ready, 1)
                    act.wait_ge(ln_ready, s.done)
                    act.activation(rstd[0:r, s.slot, 0:n], lnvar[0:r, s.slot, 0:n], ACT.Exp, scale=-0.5)\
                        .then_inc(rstd_ready, 1)

                def norm(s):
                    r, n = s.rows, s.tiles
                    free = s.ago(R)
                    act.wait_ge(shift_ready, s.done)
                    if s.had(R):
                        act.wait_ge(h1_ready, free)
                    for j in range(n):
                        last = act.activation(h[0:r, s.slot, j, :], xg[0:r, s.slot, j, :], ACT.Relu,
                                              bias=shift[0:r, s.slot, j:j + 1],
                                              scale=rstd[0:r, s.slot, j:j + 1])
                    last.then_inc(h_ready, 1)

                def evacuate(s):
                    act.wait_ge(turned, s.done)
                    if s.kept:
                        act.sem_inc(act_held, 1)
                        to = resident_cols(k, s)
                    else:
                        to = h1T[:, s.slot, 0:s.width]
                    if s.had_moved:
                        stored, free = s.moved_before(), s.ago(R)
                        act.wait_ge(h1T_stored[s.slot], stored)
                        act.wait_ge(h1T_measured, free)
                    act.activation(to, banks[s.bank][:, 0:s.width], ACT.Copy).then_inc(h1T_ready, 1)

                walk(act, NG, R, [(1, norm), (0, norm_scale), (3, evacuate)], NODE_SIZES, KEPT)

            @block.tensor
            def _(pe):
                def turn(s):
                    r = s.rows
                    free = s.ago(2)
                    pe.wait_ge(h1_ready, s.done)
                    if s.had(2):
                        pe.wait_ge(h1T_ready, free)
                    for j in range(s.tiles):
                        last = pe.transpose(banks[s.bank][:, j * r:(j + 1) * r], h1[0:r, s.slot, j, :],
                                            k["ident"][0:r, 0:r])
                    last.then_inc(turned, 1)

                walk(pe, NG, R, [(0, turn)], NODE_SIZES)


def bn_tiles(sb, sem):
    return ([sb("mean_var", [P, 2])] + [sb(n, [P, 1]) for n in ("bn_log", "std_inv", "bn_scale", "bn_shift")],
            [sem(n) for n in ("aggregated", "logged", "inverted", "bn_scaled", "bn_ready")])


def mlp_stage(nc, k):
    ctx = Stage(nc)
    with ctx:
        def sb(name, shape, dt=FP32):
            return ctx.enter_context(nc.sbuf_tensor("c_" + name, shape, dt))

        def sem(name):
            return stage_semaphore(nc, ctx, "c_" + name)

        R = RING
        tiles, sems = bn_tiles(sb, sem)
        h1T = sb("h1T", [P, R, 512])
        y = sb("y", [P, R, 512])
        hidden = sb("hidden", [P, R, 2, 512])
        z = sb("z", [P, R, 512])
        landed = [sem(f"landed{i}") for i in range(R)]
        stored = [sem(f"stored{i}") for i in range(R)]
        y_ready, up_ready, hid0_ready, hid1_ready = (
            sem("y_ready"), sem("up_ready"), sem("hid0_ready"), sem("hid1_ready"))
        down_ready, z_ready, z_measured, held, act_held = (
            sem("down_ready"), sem("z_ready"), sem("z_measured"), sem("held"), sem("act_held"))
        up = [k["bank"][0:2], k["bank"][2:4]]
        down = k["bank"][4:6]

        with nc.Block() as block:
            @block.sync
            def _(sp):
                def load(s):
                    if s.kept:
                        return
                    w = s.width
                    if s.had(R):
                        sp.wait_ge(y_ready, s.ago(R))
                    of = group_rows(k["h1T"], s)
                    sp.dma_start(h1T[:, s.slot, 0:w], of).then_inc(landed[s.slot], 16)

                def store(s):
                    if s.kept:
                        return
                    w = s.width
                    sp.wait_ge(z_ready, s.done)
                    to = group_rows(k["zT"], s)
                    sp.dma_start(to, z[:, s.slot, 0:w]).then_inc(stored[s.slot], 16)

                walk(sp, NG, RING, [(0, load), (3, store)], NODE_SIZES, KEPT)
                wait_stored(sp, stored, KEPT)

            @block.scalar
            def _(act):
                norm_constants(k, act, None, k["bn1"], k["g1"], k["be1"], tiles, sems)[0]()
                act.wait_ge(sems[4], 1)

                def normed(s):
                    w = s.width
                    if not s.kept:
                        act.wait_ge(landed[s.slot], s.moved())
                    if s.had(R):
                        act.wait_ge(z_ready, s.ago(R))
                    if s.kept:
                        act.sem_inc(act_held, 1)
                    of = resident_cols(k, s) if s.kept else h1T[:, s.slot, 0:w]
                    act.activation(y[:, s.slot, 0:w], of, ACT.Identity,
                                   bias=tiles[4][:, :], scale=tiles[3][:, :]).then_inc(y_ready, 1)

                def hidden_first(s):
                    w = s.width
                    act.wait_ge(up_ready, s.done)
                    if s.had(R):
                        act.wait_ge(down_ready, s.ago(R))
                    act.activation(hidden[:, s.slot, 0, 0:w], up[s.bank][0][:, 0:w], ACT.Relu,
                                   bias=k["b1"][:, 0:1]).then_inc(hid0_ready, 1)

                walk(act, NG, RING, [(0, normed), (1, hidden_first)], NODE_SIZES, KEPT)

            @block.vector
            def _(dve):
                norm_constants(k, None, dve, k["bn1"], k["g1"], k["be1"], tiles, sems)[1]()

                def hidden_second(s):
                    w = s.width
                    dve.wait_ge(up_ready, s.done)
                    if s.had(R):
                        dve.wait_ge(down_ready, s.ago(R))
                    dve.tensor_scalar(hidden[:, s.slot, 1, 0:w], up[s.bank][1][:, 0:w], k["b1"][:, 1:2],
                                      0.0, ALU.add, ALU.max).then_inc(hid1_ready, 1)

                def output(s):
                    w = s.width
                    dve.wait_ge(down_ready, s.done)
                    if s.had_moved:
                        dve.wait_ge(stored[s.slot], s.moved_before())
                    if s.kept:
                        dve.sem_inc(held, 1)
                    to = resident_cols(k, s) if s.kept else z[:, s.slot, 0:w]
                    dve.scalar_tensor_tensor(to, down[s.bank][:, 0:w], k["b2"][:, :],
                                             y[:, s.slot, 0:w], ALU.add, ALU.add).then_inc(z_ready, 1)
                    dve.wait_ge(z_ready, s.done)
                    if not s.tail:
                        dve.sem_inc(held, 1)
                    dve.bn_stats(stat_cols(k["bn2"], s), to).then_inc(z_measured, 1)

                walk(dve, NG, RING, [(1, hidden_second), (2, output)], NODE_SIZES, KEPT)

            @block.tensor
            def _(pe):
                def expand(s):
                    w = s.width
                    free = s.ago(2)
                    pe.wait_ge(y_ready, s.done)
                    if s.had(2):
                        pe.wait_ge(hid0_ready, free)
                        pe.wait_ge(hid1_ready, free)
                    for c in range(2):
                        last = pe.matmul(up[s.bank][c][:, 0:w], k["W1"][:, c * D:(c + 1) * D],
                                         y[:, s.slot, 0:w], start=True, stop=True)
                    last.then_inc(up_ready, 1)

                def contract(s):
                    w = s.width
                    pe.wait_ge(hid0_ready, s.done)
                    pe.wait_ge(hid1_ready, s.done)
                    if s.had(2):
                        pe.wait_ge(z_ready, s.ago(2))
                    for c in range(2):
                        last = pe.matmul(down[s.bank][:, 0:w], k["W2"][:, c, :], hidden[:, s.slot, c, 0:w],
                                         start=c == 0, stop=c == 1)
                    last.then_inc(down_ready, 1)

                walk(pe, NG, RING, [(0, expand), (1, contract)], NODE_SIZES)


def normed_stage(nc, k, x):
    ctx = Stage(nc)
    with ctx:
        def sb(name, shape, dt=FP32):
            return ctx.enter_context(nc.sbuf_tensor("d_" + name, shape, dt))

        def sem(name):
            return stage_semaphore(nc, ctx, "d_" + name)

        R = RING
        tiles, sems = bn_tiles(sb, sem)
        xg = sb("xg", [P, R, 4, D])
        zT = sb("zT", [P, R, 512])
        zn = sb("zn", [P, R, 512])
        x2 = sb("x2", [P, R, 4, D])
        g = sb("g", [P, R, 4, D])
        stat = sb("stat", [P, R, 4, 6])
        mv = sb("mv", [P, R, 4, 2])
        lnvar = sb("lnvar", [P, R, 4])
        rstd = sb("rstd", [P, R, 4])
        gscale = sb("gscale", [P, R, 4])
        gshift = sb("gshift", [P, R, 4])
        x_landed = [sem(f"x_landed{i}") for i in range(R)]
        z_landed = [sem(f"z_landed{i}") for i in range(R)]
        x2_stored = [sem(f"x2_stored{i}") for i in range(R)]
        g_stored = [sem(f"g_stored{i}") for i in range(R)]
        deg_landed, deg_clipped, deg_logged, deg_ready = (
            sem("deg_landed"), sem("deg_clipped"), sem("deg_logged"), sem("deg_ready"))
        zn_ready, turned, x2_ready, stats_ready, mv_ready = (
            sem("zn_ready"), sem("turned"), sem("x2_ready"), sem("stats_ready"), sem("mv_ready"))
        act_held = sem("act_held")
        ln_ready, rstd_ready, shift_ready, gshift_ready, g_ready, held = (
            sem("ln_ready"), sem("rstd_ready"), sem("shift_ready"), sem("gshift_ready"), sem("g_ready"),
            sem("held"))
        banks = k["bank"][0:2]
        out_deg, in_deg = k["out_deg"], k["in_deg"]
        deg_parts = [(t, slice(0, r), slice(c0, c1)) for t in (out_deg, in_deg)
                     for r, c0, c1 in ((P, 0, NT), (NR, NT, NC))]

        with nc.Block() as block:
            @block.sync
            def _(sp):
                flat = k["degree"].rearrange("a p -> (a p)")
                sp.dma_start(out_deg[:, 0:NT], flat[0:P * NT].rearrange("(p t) -> p t", p=P))\
                    .then_inc(deg_landed, 16)
                sp.dma_start(out_deg[0:NR, NT:NC], flat[P * NT:N].rearrange("(p t) -> p t", p=NR))\
                    .then_inc(deg_landed, 16)

                def load(s):
                    w = s.width
                    free = s.ago(R)
                    if not s.kept:
                        if s.had(R):
                            sp.wait_ge(zn_ready, free)
                        of = group_rows(k["zT"], s)
                        sp.dma_start(zT[:, s.slot, 0:w], of).then_inc(z_landed[s.slot], 16)
                    if s.had(R):
                        sp.wait_ge(x2_ready, free)
                    sp.dma_start(xg[0:s.rows, s.slot, 0:s.tiles, :], node_rows(x, s))\
                        .then_inc(x_landed[s.slot], 16)

                def store(s):
                    if not s.kept:
                        sp.wait_ge(x2_ready, s.done)
                        sp.dma_start(node_rows(k["x2"], s), x2[0:s.rows, s.slot, 0:s.tiles, :])\
                            .then_inc(x2_stored[s.slot], 16)
                    sp.wait_ge(g_ready, s.done)
                    sp.dma_start(node_rows(k["g"], s), g[0:s.rows, s.slot, 0:s.tiles, :])\
                        .then_inc(g_stored[s.slot], 16)

                walk(sp, NG, RING, [(0, load), (5, store)], NODE_SIZES, KEPT)
                wait_stored(sp, x2_stored, KEPT)
                wait_stored(sp, g_stored)

            @block.scalar
            def _(act):
                norm_constants(k, act, None, k["bn2"], k["g2"], k["be2"], tiles, sems)[0]()
                act.wait_ge(deg_clipped, 4)
                for t, rs, cs in deg_parts:
                    act.activation(t[rs, cs], t[rs, cs], ACT.Ln).then_inc(deg_logged, 1)
                act.wait_ge(deg_logged, 4)
                for t, rs, cs in deg_parts:
                    act.activation(t[rs, cs], t[rs, cs], ACT.Exp, scale=-0.5).then_inc(deg_ready, 1)
                act.wait_ge(sems[4], 1)

                def normed(s):
                    w = s.width
                    if not s.kept:
                        act.wait_ge(z_landed[s.slot], s.moved())
                    if s.had(R):
                        act.wait_ge(turned, s.ago(R))
                    if s.kept:
                        act.sem_inc(act_held, 1)
                    of = resident_cols(k, s) if s.kept else zT[:, s.slot, 0:w]
                    act.activation(zn[:, s.slot, 0:w], of, ACT.Identity,
                                   bias=tiles[4][:, :], scale=tiles[3][:, :]).then_inc(zn_ready, 1)

                def norm_scale(s):
                    r, n = s.rows, s.tiles
                    act.wait_ge(mv_ready, s.done)
                    act.activation(lnvar[0:r, s.slot, 0:n], mv[0:r, s.slot, 0:n, 1], ACT.Ln,
                                   bias=k["eps"][0:r, :]).then_inc(ln_ready, 1)
                    act.wait_ge(ln_ready, s.done)
                    act.activation(rstd[0:r, s.slot, 0:n], lnvar[0:r, s.slot, 0:n], ACT.Exp, scale=-0.5)\
                        .then_inc(rstd_ready, 1)

                def scaled_rows(s):
                    r, n = s.rows, s.tiles
                    act.wait_ge(gshift_ready, s.done)
                    if s.had(R):
                        act.wait_ge(g_stored[s.slot], s.landed_before())
                    if s.kept:
                        act.sem_inc(act_held, 1)
                    of = resident_rows(k, s) if s.kept else x2[0:r, s.slot, 0:n, :]
                    for j in range(n):
                        last = act.activation(g[0:r, s.slot, j, :], of[:, j, :], ACT.Relu,
                                              bias=gshift[0:r, s.slot, j:j + 1],
                                              scale=gscale[0:r, s.slot, j:j + 1])
                    last.then_inc(g_ready, 1)

                walk(act, NG, RING, [(0, normed), (3, scaled_rows), (2, norm_scale)], NODE_SIZES, KEPT)

            @block.vector
            def _(dve):
                norm_constants(k, None, dve, k["bn2"], k["g2"], k["be2"], tiles, sems)[1]()
                dve.wait_ge(deg_landed, 32)
                for t, rs, cs in deg_parts:
                    dve.tensor_scalar(t[rs, cs], t[rs, cs], 1.0, None, ALU.max).then_inc(deg_clipped, 1)
                dve.wait_ge(deg_ready, 4)

                def residual(s):
                    r, n = s.rows, s.tiles
                    landed, free = s.landed(), s.ago(R)
                    dve.wait_ge(x_landed[s.slot], landed)
                    dve.wait_ge(turned, s.done)
                    if s.had_moved:
                        dve.wait_ge(x2_stored[s.slot], s.moved_before())
                        dve.wait_ge(g_ready, free)
                    if s.kept:
                        dve.sem_inc(held, 1)
                    to = resident_rows(k, s) if s.kept else x2[0:r, s.slot, 0:n, :]
                    dve.tensor_tensor(to,
                                      banks[s.bank][0:r, 0:n * D].rearrange("p (t f) -> p t f", t=n),
                                      xg[0:r, s.slot, 0:n, :], ALU.add).then_inc(x2_ready, 1)
                    dve.wait_ge(x2_ready, s.done)
                    if s.kept:
                        dve.sem_inc(held, 1)
                    for j in range(n):
                        last = dve.bn_stats(stat[0:r, s.slot, j, :], to[:, j, :])
                    last.then_inc(stats_ready, 1)
                    dve.wait_ge(stats_ready, s.done)
                    dve.sem_inc(held, 1)
                    for j in range(n):
                        last = dve.bn_aggr(mv[0:r, s.slot, j, :], stat[0:r, s.slot, j, :])
                    last.then_inc(mv_ready, 1)

                def constants(s):
                    r, n = s.rows, s.tiles
                    dve.wait_ge(rstd_ready, s.done)
                    dve.scalar_tensor_tensor(cols(k["shift2"], s, 4), mv[0:r, s.slot, 0:n, 0], -1.0,
                                             rstd[0:r, s.slot, 0:n], ALU.mult, ALU.mult)\
                        .then_inc(shift_ready, 1)
                    dve.tensor_tensor(gscale[0:r, s.slot, 0:n], rstd[0:r, s.slot, 0:n], cols(out_deg, s, 4),
                                      ALU.mult)
                    dve.tensor_copy(cols(k["scale2"], s, 4), rstd[0:r, s.slot, 0:n])
                    dve.wait_ge(shift_ready, s.done)
                    dve.tensor_tensor(gshift[0:r, s.slot, 0:n], cols(k["shift2"], s, 4), cols(out_deg, s, 4),
                                      ALU.mult).then_inc(gshift_ready, 1)

                walk(dve, NG, RING, [(2, constants), (0, residual)], NODE_SIZES, KEPT)

            @block.tensor
            def _(pe):
                def turn(s):
                    r = s.rows
                    pe.wait_ge(zn_ready, s.done)
                    if s.had(2):
                        pe.wait_ge(x2_ready, s.ago(2))
                    for j in range(s.tiles):
                        last = pe.transpose(banks[s.bank][0:r, j * D:(j + 1) * D],
                                            zn[:, s.slot, j * r:(j + 1) * r], k["ident"][:, :])
                    last.then_inc(turned, 1)

                walk(pe, NG, RING, [(0, turn)], NODE_SIZES)


def convolution_stage(nc, k):
    ctx = Stage(nc)
    with ctx:
        def sb(name, shape, dt=FP32):
            return ctx.enter_context(nc.sbuf_tensor("e_" + name, shape, dt))

        def sem(name):
            return stage_semaphore(nc, ctx, "e_" + name)

        index = sb("index", [P, 2, 2], I32)
        add_at = sb("add_at", [P, 2, 2], I32)
        dst_now = sb("dst_now", [P, 2, 2])
        g = sb("g", [P, 2, 2, D])
        same = sb("same", [P, 2, 2, P])
        group = sb("group", [P, 2, 2, D])
        landed = [sem(f"landed{i}") for i in range(2)]
        rows_added = [sem(f"rows_added{i}") for i in range(2)]
        index_ready, target_ready, dst_turned, same_ready, grouped, group_ready, held = (
            sem("index_ready"), sem("target_ready"), sem("dst_turned"), sem("same_ready"), sem("grouped"),
            sem("group_ready"), sem("held"))
        bank_dst, bank_grp = k["bank"][0:2], k["bank"][2:4]
        dst_f, ends, target, ident = k["dst_f"], k["ends"], k["target"], k["ident"]

        with nc.Block() as block:
            @block.gpsimd
            def _(pool):
                def hold(*waits):
                    for sem_, value in waits:
                        pool.wait_ge(sem_, value)
                    pool.sem_inc(held, 1)

                def gather(s):
                    free = s.ago(2)
                    waits = [(index_ready, s.done)]
                    if s.had(2):
                        waits.append((grouped, free))
                    hold(*waits)
                    for j in range(s.tiles):
                        pool.indirect_dma_start(
                            g[0:s.rows, s.slot, j, :], None, k["g"],
                            bass.IndirectOffsetOnAxis(index[0:s.rows, s.slot, j:j + 1], 0))\
                            .then_inc(landed[s.slot], 16)

                def add(s):
                    last = s.value(s.index * 16)
                    for j in range(s.tiles):
                        waits = [(group_ready, s.done), (target_ready, s.done)]
                        if not s.first:
                            waits.append((rows_added[j], last))
                        hold(*waits)
                        pool.indirect_dma_start(
                            k["sums"][j], bass.IndirectOffsetOnAxis(add_at[0:s.rows, s.slot, j:j + 1], 0),
                            group[0:s.rows, s.slot, j, :], None, compute_op=ALU.add)\
                            .then_inc(rows_added[j], 16)

                walk(pool, EU, 2, [(0, gather), (2, add)], EDGE_SIZES)
                pool.wait_ge(rows_added[0], 16 * (EU + 1))
                pool.wait_ge(rows_added[1], 16 * EU)

            @block.vector
            def _(dve):
                def make_index(s):
                    read, free = s.value(s.turn * 32), s.ago(2)
                    if s.had(2):
                        dve.wait_ge(dst_turned, free)
                        dve.wait_ge(landed[s.slot], read)
                        dve.sem_inc(held, 1)
                    dve.tensor_copy(dst_now[0:s.rows, s.slot, 0:s.tiles], cols(dst_f, s, 2))
                    t0, n = s.index * 2, s.tiles
                    part = ends[0:s.rows, t0:t0 + n, 0] if s.tail else ends[:, bass.ds(t0, 2), 0]
                    dve.tensor_copy(index[0:s.rows, s.slot, 0:n], part).then_inc(index_ready, 1)

                def compare(s):
                    r, n = s.rows, s.tiles
                    free = s.ago(2)
                    dve.wait_ge(dst_turned, s.done)
                    if s.had(2):
                        dve.wait_ge(grouped, free)
                    dve.tensor_tensor(same[0:r, s.slot, 0:n, 0:r],
                                      bank_dst[s.slot][0:r, 0:n * P].rearrange("p (t e) -> p t e", t=n)[:, :, 0:r],
                                      spread(cols(dst_f, s, 2), r), ALU.is_equal).then_inc(same_ready, 1)

                def targets(s):
                    n = s.tiles
                    added = s.value(s.index * 16 - 16)
                    if s.had(2):
                        dve.wait_ge(rows_added[0], added)
                        dve.wait_ge(rows_added[1], added)
                        dve.sem_inc(held, 1)
                    t0 = s.index * 2
                    part = target[0:s.rows, t0:t0 + n] if s.tail else target[:, bass.ds(t0, 2)]
                    dve.tensor_copy(add_at[0:s.rows, s.slot, 0:n], part).then_inc(target_ready, 1)

                walk(dve, EU, 2, [(0, make_index), (2, compare), (3, targets)], EDGE_SIZES)

            @block.scalar
            def _(act):
                def evacuate(s):
                    r, n = s.rows, s.tiles
                    added = s.value(s.index * 16 - 16)
                    act.wait_ge(grouped, s.done)
                    if s.had(2):
                        act.wait_ge(rows_added[0], added)
                        act.wait_ge(rows_added[1], added)
                    act.activation(group[0:r, s.slot, 0:n, :],
                                   bank_grp[s.slot][0:r, 0:n * D].rearrange("p (t f) -> p t f", t=n),
                                   ACT.Copy).then_inc(group_ready, 1)

                walk(act, EU, 2, [(0, evacuate)], EDGE_SIZES)

            @block.tensor
            def _(pe):
                def turn(s):
                    r = s.rows
                    free = s.ago(2)
                    pe.wait_ge(index_ready, s.done)
                    if s.had(2):
                        pe.wait_ge(same_ready, free)
                    for j in range(s.tiles):
                        last = pe.transpose(bank_dst[s.slot][0:P, j * P:j * P + r],
                                            dst_now[0:r, s.slot, j:j + 1].broadcast_to([r, P]),
                                            ident[0:r, 0:r])
                    last.then_inc(dst_turned, 1)

                def group_up(s):
                    r = s.rows
                    full = s.value(s.turn * 32 + (16 if s.tail else 32))
                    free = s.ago(2)
                    pe.wait_ge(landed[s.slot], full)
                    pe.wait_ge(same_ready, s.done)
                    if s.had(2):
                        pe.wait_ge(group_ready, free)
                    for j in range(s.tiles):
                        last = pe.matmul(bank_grp[s.slot][0:r, j * D:(j + 1) * D],
                                         same[0:r, s.slot, j, 0:r], g[0:r, s.slot, j, :],
                                         start=True, stop=True)
                    last.then_inc(grouped, 1)

                walk(pe, EU, 2, [(0, turn), (1, group_up)], EDGE_SIZES)


def output_stage(nc, k, out):
    ctx = Stage(nc)
    with ctx:
        def sb(name, shape, dt=FP32):
            return ctx.enter_context(nc.sbuf_tensor("f_" + name, shape, dt))

        def sem(name):
            return stage_semaphore(nc, ctx, "f_" + name)

        R = RING
        x2 = sb("x2", [P, R, 4, D])
        sums = [sb(f"sums{i}", [P, R, 4, D]) for i in range(2)]
        h = sb("h", [P, R, 4, D])
        total, hs = sums
        plus = total
        times = sb("times", [P, R, 4, D])
        bothT = sb("bothT", [P, R, 2, 512])
        res = sb("res", [P, R, 4, D])
        x_landed = [sem(f"x_landed{i}") for i in range(R)]
        sums_landed = [sem(f"sums_landed{i}") for i in range(R)]
        stored = [sem(f"stored{i}") for i in range(R)]
        h_ready, total_ready, hs_ready, plus_ready, times_ready = (
            sem("h_ready"), sem("total_ready"), sem("hs_ready"), sem("plus_ready"), sem("times_ready"))
        plus_turned, times_turned, plusT_ready, timesT_ready, product_ready, res_ready, held = (
            sem("plus_turned"), sem("times_turned"), sem("plusT_ready"), sem("timesT_ready"),
            sem("product_ready"), sem("res_ready"), sem("held"))
        dve_held = sem("dve_held")
        bank_plus, bank_times, bank_out = k["bank"][0:2], k["bank"][2:4], k["bank"][4:6]

        with nc.Block() as block:
            @block.sync
            def _(sp):
                def load(s):
                    free = s.ago(R)
                    if s.had(R):
                        sp.wait_ge(plus_turned, free)
                        sp.wait_ge(times_ready, free)
                    for i in range(2):
                        sp.dma_start(sums[i][0:s.rows, s.slot, 0:s.tiles, :], node_rows(k["sums"][i], s))\
                            .then_inc(sums_landed[s.slot], 16)
                    if s.kept:
                        return
                    if s.had(R):
                        sp.wait_ge(res_ready, free)
                    sp.dma_start(x2[0:s.rows, s.slot, 0:s.tiles, :], node_rows(k["x2"], s))\
                        .then_inc(x_landed[s.slot], 16)

                def store(s):
                    sp.wait_ge(res_ready, s.done)
                    sp.dma_start(node_rows(out, s), res[0:s.rows, s.slot, 0:s.tiles, :])\
                        .then_inc(stored[s.slot], 16)

                walk(sp, NG, RING, [(0, load), (5, store)], NODE_SIZES, KEPT)
                wait_stored(sp, stored)

            @block.gpsimd
            def _(pool):
                def add_tables(s):
                    r, n = s.rows, s.tiles
                    full = s.landed(2)
                    pool.wait_ge(sums_landed[s.slot], full)
                    pool.tensor_tensor(total[0:r, s.slot, 0:n, :], sums[0][0:r, s.slot, 0:n, :],
                                       sums[1][0:r, s.slot, 0:n, :], ALU.add).then_inc(total_ready, 1)

                def add_rows(s):
                    r, n = s.rows, s.tiles
                    pool.wait_ge(hs_ready, s.done)
                    pool.wait_ge(h_ready, s.done)
                    pool.tensor_tensor(plus[0:r, s.slot, 0:n, :], hs[0:r, s.slot, 0:n, :],
                                       h[0:r, s.slot, 0:n, :], ALU.add).then_inc(plus_ready, 1)

                walk(pool, NG, RING, [(0, add_tables), (1, add_rows)], NODE_SIZES)

            @block.scalar
            def _(act):
                def norm(s):
                    r, n = s.rows, s.tiles
                    free = s.ago(R)
                    if not s.kept:
                        act.wait_ge(x_landed[s.slot], s.moved())
                    if s.had(R):
                        act.wait_ge(plus_ready, free)
                        act.wait_ge(times_ready, free)
                    act.sem_inc(held, 1)
                    of = resident_rows(k, s) if s.kept else x2[0:r, s.slot, 0:n, :]
                    for j in range(n):
                        t = s.index * 4 + j
                        sc, sh = (v[0:r, t:t + 1] if s.tail else v[0:r, bass.ds(t, 1)]
                                  for v in (k["scale2"], k["shift2"]))
                        last = act.activation(h[0:r, s.slot, j, :], of[:, j, :], ACT.Relu,
                                              bias=sh, scale=sc)
                    last.then_inc(h_ready, 1)

                def evacuate(s):
                    w = s.width
                    free = s.ago(R)
                    for c, (bank, turned, ready) in enumerate(((bank_plus, plus_turned, plusT_ready),
                                                               (bank_times, times_turned, timesT_ready))):
                        act.wait_ge(turned, s.done)
                        if s.had(R) and c == 0:
                            act.wait_ge(product_ready, free)
                        act.activation(bothT[:, s.slot, c, 0:w], bank[s.bank][:, 0:w], ACT.Copy)\
                            .then_inc(ready, 1)

                walk(act, NG, RING, [(0, norm), (2, evacuate)], NODE_SIZES, KEPT)

            @block.vector
            def _(dve):
                def scale_sums(s):
                    r, n = s.rows, s.tiles
                    free = s.ago(R)
                    dve.wait_ge(total_ready, s.done)
                    dve.tensor_tensor(hs[0:r, s.slot, 0:n, :], total[0:r, s.slot, 0:n, :],
                                      spread(cols(k["in_deg"], s, 4), D), ALU.mult).then_inc(hs_ready, 1)
                    dve.wait_ge(h_ready, s.done)
                    dve.wait_ge(hs_ready, s.done)
                    if s.had(R):
                        dve.wait_ge(times_turned, free)
                    dve.tensor_tensor(times[0:r, s.slot, 0:n, :], hs[0:r, s.slot, 0:n, :],
                                      h[0:r, s.slot, 0:n, :], ALU.mult).then_inc(times_ready, 1)

                def result(s):
                    r, n = s.rows, s.tiles
                    kept = s.landed_before()
                    dve.wait_ge(product_ready, s.done)
                    if s.had(R):
                        dve.wait_ge(stored[s.slot], kept)
                    if s.kept:
                        dve.sem_inc(dve_held, 1)
                    of = resident_rows(k, s) if s.kept else x2[0:r, s.slot, 0:n, :]
                    dve.tensor_tensor(res[0:r, s.slot, 0:n, :],
                                      bank_out[s.bank][0:r, 0:n * D].rearrange("p (t f) -> p t f", t=n),
                                      of, ALU.add).then_inc(res_ready, 1)

                walk(dve, NG, RING, [(3, result), (0, scale_sums)], NODE_SIZES, KEPT)

            @block.tensor
            def _(pe):
                def turn(s):
                    r = s.rows
                    free = s.ago(2)
                    for rows, bank, ready, turned, read in (
                            (times, bank_times, times_ready, times_turned, timesT_ready),
                            (plus, bank_plus, plus_ready, plus_turned, plusT_ready)):
                        pe.wait_ge(ready, s.done)
                        if s.had(2):
                            pe.wait_ge(read, free)
                        for j in range(s.tiles):
                            last = pe.transpose(bank[s.bank][:, j * r:(j + 1) * r],
                                                rows[0:r, s.slot, j, :], k["ident"][0:r, 0:r])
                        last.then_inc(turned, 1)

                def product(s):
                    r = s.rows
                    free = s.ago(2)
                    pe.wait_ge(plusT_ready, s.done)
                    pe.wait_ge(timesT_ready, s.done)
                    if s.had(2):
                        pe.wait_ge(res_ready, free)
                    for j in range(s.tiles):
                        o = bank_out[s.bank][0:r, j * D:(j + 1) * D]
                        pe.matmul(o, bothT[:, s.slot, 0, j * r:(j + 1) * r], k["Ws"][:, :], start=True,
                                  stop=False)
                        last = pe.matmul(o, bothT[:, s.slot, 1, j * r:(j + 1) * r], k["Wi"][:, :],
                                         start=False, stop=True)
                    last.then_inc(product_ready, 1)

                walk(pe, NG, RING, [(0, turn), (1, product)], NODE_SIZES)


_INS = ["x", "src", "dst", "edge_attr_128", "L0_gnn_Wq", "L0_gnn_Wk", "L0_gnn_We", "L0_gnn_Wv",
        "L0_gnn_bn1_g", "L0_gnn_bn1_b", "L0_gnn_W1", "L0_gnn_b1", "L0_gnn_W2", "L0_gnn_b2",
        "L0_gnn_bn2_g", "L0_gnn_bn2_b", "L1_gnn_W_self", "L1_gnn_W_inter"]


def kernel(**inputs):
    import numpy as _np
    import concourse.bacc as _bacc
    from concourse import mybir as _mybir
    from concourse.bass_utils import run_bass_kernel_spmd as _run

    nc = _bacc.Bacc("TRN2", target_bir_lowering=False, num_devices=1)
    arrays, args = {}, []
    for name in _INS:
        a = _np.ascontiguousarray(inputs[name])
        arrays[f"in_{name}_dram"] = a
        args.append(nc.dram_tensor(f"in_{name}_dram", a.shape, _mybir.dt.from_np(a.dtype), kind="ExternalInput").ap())
    args.append(nc.dram_tensor("out_0_dram", (N, D), FP32, kind="ExternalOutput").ap())
    build(nc, *args)
    r = _run(nc, [arrays], core_ids=[0])
    return r.results[0]["out_0_dram"]
```
